# Optimizing a Trainium2 kernel written in Bass

```python
import numpy as np
import jax
import jax.numpy as jnp

def _softmax(x, axis=-1):
    return jax.nn.softmax(x, axis=axis)

def _gelu(x):
    return jax.nn.gelu(x, approximate=True)

def _silu(x):
    return jax.nn.silu(x)

def _sigmoid(x):
    return jax.nn.sigmoid(x)

def _layernorm(x, axis=-1, eps=1e-05):
    m = jnp.mean(x, axis=axis, keepdims=True)
    v = jnp.var(x, axis=axis, keepdims=True)
    return (x - m) / jnp.sqrt(v + eps)

def _scatter_add(tgt, idx, src, axis=0):
    return tgt.at[idx].add(src)

def _segment_sum(src, seg, n):
    return jax.ops.segment_sum(src, seg, n)
kernel_name = 'mk_cond_seq_d2_seqx_r4_23852b'

def setup_inputs(seed: int=0):
    np.random.seed(seed)
    _w = jnp.asarray

    def _rec_inputs():
        import jax
        import jax.numpy as jnp
        _rk = jax.random.key(seed)
        x = 7.22e-05 + 1 * jax.random.normal(jax.random.fold_in(_rk, 1), (16, 256, 512), jnp.float32)
        _lenS = 256 - jax.random.randint(jax.random.fold_in(_rk, 7), (16,), 0, max(1, 256 // 4) + 1, jnp.int32)
        _lenS2 = 256 - jax.random.randint(jax.random.fold_in(_rk, 8), (16,), 0, max(1, 256 // 4) + 1, jnp.int32)
        cond_2048 = 0.0061147 + 1.02565 * jax.random.normal(jax.random.fold_in(_rk, 11), (16, 512), jnp.float32)
        pos_BxS = jnp.broadcast_to(jnp.arange(256, dtype=jnp.int32), (16, 256))
        _validS = jnp.arange(256)[None, :] < _lenS[:, None]
        _validS2 = jnp.arange(256)[None, :] < _lenS2[:, None]
        _causal = jnp.tril(jnp.ones((256, 256), dtype=bool))
        mask_1x1xSxS_ff0 = jnp.where(jnp.ones((1, 1, 256, 256), dtype=bool), 0.0, -1000000000.0).astype(jnp.float32)
        return (x, cond_2048, pos_BxS, mask_1x1xSxS_ff0)
    x, cond_2048, pos_BxS, mask_1x1xSxS_ff0 = _rec_inputs()

    def _L0_cond_setup():
        import jax, jax.numpy as jnp
        import numpy as np
        B, L, C, H = (2, 512, 512, 16)
        COND = 512
        HID = 4 * C
        LN_EPS = 1e-06

        def _ln(x):
            m = jnp.mean(x, axis=-1, keepdims=True)
            v = jnp.mean((x - m) ** 2, axis=-1, keepdims=True)
            return (x - m) / jnp.sqrt(v + LN_EPS)

        def _gelu_tanh(u):
            c = np.sqrt(2.0 / np.pi).astype(np.float32)
            return 0.5 * u * (1.0 + jnp.tanh(c * (u + 0.044715 * u ** 3)))
        key = jax.random.key(seed)
        ks = jax.random.split(key, 8)
        s = 0.02
        return {'x': jax.random.normal(ks[0], (B, L, C), jnp.float32), 'cond_BD': jax.random.normal(ks[1], (B, COND), jnp.float32), 'attn_bias': jnp.zeros((1, 1, L, L), jnp.float32), 'Wqkv': jax.random.normal(ks[2], (3 * C, C), jnp.float32) * s, 'q_bias': jnp.zeros((C,), jnp.float32), 'v_bias': jnp.zeros((C,), jnp.float32), 'scale_mul_log': jnp.full((1, H, 1, 1), np.log(4.0), jnp.float32), 'Wproj': jax.random.normal(ks[3], (C, C), jnp.float32) * s, 'bproj': jnp.zeros((C,), jnp.float32), 'Wada': jax.random.normal(ks[4], (6 * C, COND), jnp.float32) * s, 'bada': jnp.zeros((6 * C,), jnp.float32), 'Wfc1': jax.random.normal(ks[5], (HID, C), jnp.float32) * s, 'bfc1': jnp.zeros((HID,), jnp.float32), 'Wfc2': jax.random.normal(ks[6], (C, HID), jnp.float32) * s, 'bfc2': jnp.zeros((C,), jnp.float32)}
    _L0_cond_all = _L0_cond_setup()
    _L0_cond_in = {k: v for k, v in _L0_cond_all.items() if k in ('Wqkv', 'q_bias', 'v_bias', 'scale_mul_log', 'Wproj', 'bproj', 'Wada', 'bada', 'Wfc1', 'bfc1', 'Wfc2', 'bfc2')}
    del _L0_cond_all

    def _L1_cond_setup():
        import jax, jax.numpy as jnp
        import numpy as np
        HIDDEN, NQ, NKV, HD, INTER = (512, 8, 1, 64, 2048)
        B, S = (4, 512)
        EPS = 1e-06
        ROPE_BASE = 10000.0

        def ada_rms(x, t, w, tw):
            n = x * jax.lax.rsqrt(jnp.mean(jnp.square(x), axis=-1, keepdims=True) + EPS)
            scale = t @ tw.T
            return n * (w * (1.0 + scale))[:, None, :]

        def apply_rope(x, pos_ids):
            half = HD // 2
            inv_freq = 1.0 / ROPE_BASE ** (jnp.arange(0, HD, 2, dtype=jnp.float32) / HD)
            ang = pos_ids.astype(jnp.float32)[:, :, None] * inv_freq
            cos = jnp.concatenate([jnp.cos(ang), jnp.cos(ang)], axis=-1)[:, None]
            sin = jnp.concatenate([jnp.sin(ang), jnp.sin(ang)], axis=-1)[:, None]
            x1, x2 = (x[..., :half], x[..., half:])
            rot = jnp.concatenate([-x2, x1], axis=-1)
            return x * cos + rot * sin
        key = jax.random.key(seed)
        ks = jax.random.split(key, 12)
        f32 = jnp.float32
        inp = {'x': jax.random.normal(ks[0], (B, S, HIDDEN), f32), 'pos_ids': jnp.broadcast_to(jnp.arange(S, dtype=jnp.int32), (B, S)), 'time_emb': jax.random.normal(ks[1], (B, HIDDEN), f32), 'ln1_w': jnp.ones((HIDDEN,), f32), 'ln1_tw': jax.random.normal(ks[2], (HIDDEN, HIDDEN), f32) * 0.02, 'ln2_w': jnp.ones((HIDDEN,), f32), 'ln2_tw': jax.random.normal(ks[3], (HIDDEN, HIDDEN), f32) * 0.02, 'Wq': jax.random.normal(ks[4], (NQ * HD, HIDDEN), f32) * 0.02, 'Wk': jax.random.normal(ks[5], (NKV * HD, HIDDEN), f32) * 0.02, 'Wv': jax.random.normal(ks[6], (NKV * HD, HIDDEN), f32) * 0.02, 'Wo': jax.random.normal(ks[7], (HIDDEN, NQ * HD), f32) * 0.02, 'Wg': jax.random.normal(ks[8], (INTER, HIDDEN), f32) * 0.02, 'Wu': jax.random.normal(ks[9], (INTER, HIDDEN), f32) * 0.02, 'Wd': jax.random.normal(ks[10], (HIDDEN, INTER), f32) * 0.02}
        return inp
    _L1_cond_all = _L1_cond_setup()
    _L1_cond_in = {k: v for k, v in _L1_cond_all.items() if k in ('ln1_w', 'ln1_tw', 'ln2_w', 'ln2_tw', 'Wq', 'Wk', 'Wv', 'Wo', 'Wg', 'Wu', 'Wd')}
    del _L1_cond_all
    return {'x': x, 'cond_2048': cond_2048, 'pos_BxS': pos_BxS, 'mask_1x1xSxS_ff0': mask_1x1xSxS_ff0, 'L0_cond_Wqkv': _L0_cond_in['Wqkv'], 'L0_cond_q_bias': _L0_cond_in['q_bias'], 'L0_cond_v_bias': _L0_cond_in['v_bias'], 'L0_cond_scale_mul_log': _L0_cond_in['scale_mul_log'], 'L0_cond_Wproj': _L0_cond_in['Wproj'], 'L0_cond_bproj': _L0_cond_in['bproj'], 'L0_cond_Wada': _L0_cond_in['Wada'], 'L0_cond_bada': _L0_cond_in['bada'], 'L0_cond_Wfc1': _L0_cond_in['Wfc1'], 'L0_cond_bfc1': _L0_cond_in['bfc1'], 'L0_cond_Wfc2': _L0_cond_in['Wfc2'], 'L0_cond_bfc2': _L0_cond_in['bfc2'], 'L1_cond_ln1_w': _L1_cond_in['ln1_w'], 'L1_cond_ln1_tw': _L1_cond_in['ln1_tw'], 'L1_cond_ln2_w': _L1_cond_in['ln2_w'], 'L1_cond_ln2_tw': _L1_cond_in['ln2_tw'], 'L1_cond_Wq': _L1_cond_in['Wq'], 'L1_cond_Wk': _L1_cond_in['Wk'], 'L1_cond_Wv': _L1_cond_in['Wv'], 'L1_cond_Wo': _L1_cond_in['Wo'], 'L1_cond_Wg': _L1_cond_in['Wg'], 'L1_cond_Wu': _L1_cond_in['Wu'], 'L1_cond_Wd': _L1_cond_in['Wd']}

def reference(x, cond_2048, pos_BxS, mask_1x1xSxS_ff0, L0_cond_Wqkv, L0_cond_q_bias, L0_cond_v_bias, L0_cond_scale_mul_log, L0_cond_Wproj, L0_cond_bproj, L0_cond_Wada, L0_cond_bada, L0_cond_Wfc1, L0_cond_bfc1, L0_cond_Wfc2, L0_cond_bfc2, L1_cond_ln1_w, L1_cond_ln1_tw, L1_cond_ln2_w, L1_cond_ln2_tw, L1_cond_Wq, L1_cond_Wk, L1_cond_Wv, L1_cond_Wo, L1_cond_Wg, L1_cond_Wu, L1_cond_Wd):
    import jax
    import jax.numpy as jnp

    def _L0_cond_ref(x, cond_BD, attn_bias, Wqkv, q_bias, v_bias, scale_mul_log, Wproj, bproj, Wada, bada, Wfc1, bfc1, Wfc2, bfc2):
        import jax, jax.numpy as jnp
        import numpy as np
        B, L, C, H = (2, 512, 512, 16)
        COND = 512
        HID = 4 * C
        LN_EPS = 1e-06

        def _ln(x):
            m = jnp.mean(x, axis=-1, keepdims=True)
            v = jnp.mean((x - m) ** 2, axis=-1, keepdims=True)
            return (x - m) / jnp.sqrt(v + LN_EPS)

        def _gelu_tanh(u):
            c = np.sqrt(2.0 / np.pi).astype(np.float32)
            return 0.5 * u * (1.0 + jnp.tanh(c * (u + 0.044715 * u ** 3)))
        Bs, Lx, Cx = x.shape
        D = Cx // H
        ada = (jax.nn.silu(cond_BD) @ Wada.T + bada).reshape(Bs, 1, 6, Cx)
        gamma1, gamma2, scale1, scale2, shift1, shift2 = [ada[:, :, i, :] for i in range(6)]

        def attn(xin):
            qkv_bias = jnp.concatenate([q_bias, jnp.zeros_like(q_bias), v_bias])
            qkv = (xin @ Wqkv.T + qkv_bias).reshape(Bs, Lx, 3, H, D)
            qkv = jnp.transpose(qkv, (2, 0, 3, 1, 4))
            q, k, v = (qkv[0], qkv[1], qkv[2])
            sm = jnp.exp(jnp.minimum(scale_mul_log, jnp.log(jnp.float32(100.0))))
            qn = q / jnp.maximum(jnp.linalg.norm(q, axis=-1, keepdims=True), 1e-12) * sm
            kn = k / jnp.maximum(jnp.linalg.norm(k, axis=-1, keepdims=True), 1e-12)
            scores = jnp.einsum('bhqd,bhkd->bhqk', qn, kn) + attn_bias
            p = jax.nn.softmax(scores, axis=-1)
            o = jnp.einsum('bhqk,bhkd->bhqd', p, v)
            o = jnp.transpose(o, (0, 2, 1, 3)).reshape(Bs, Lx, Cx)
            return o @ Wproj.T + bproj
        x = x + attn(_ln(x) * (scale1 + 1.0) + shift1) * gamma1
        h = _gelu_tanh((_ln(x) * (scale2 + 1.0) + shift2) @ Wfc1.T + bfc1)
        x = x + (h @ Wfc2.T + bfc2) * gamma2
        return x

    def _L1_cond_ref(x, pos_ids, time_emb, ln1_w, ln1_tw, ln2_w, ln2_tw, Wq, Wk, Wv, Wo, Wg, Wu, Wd):
        import jax, jax.numpy as jnp
        import numpy as np
        HIDDEN, NQ, NKV, HD, INTER = (512, 8, 1, 64, 2048)
        B, S = (4, 512)
        EPS = 1e-06
        ROPE_BASE = 10000.0

        def ada_rms(x, t, w, tw):
            n = x * jax.lax.rsqrt(jnp.mean(jnp.square(x), axis=-1, keepdims=True) + EPS)
            scale = t @ tw.T
            return n * (w * (1.0 + scale))[:, None, :]

        def apply_rope(x, pos_ids):
            half = HD // 2
            inv_freq = 1.0 / ROPE_BASE ** (jnp.arange(0, HD, 2, dtype=jnp.float32) / HD)
            ang = pos_ids.astype(jnp.float32)[:, :, None] * inv_freq
            cos = jnp.concatenate([jnp.cos(ang), jnp.cos(ang)], axis=-1)[:, None]
            sin = jnp.concatenate([jnp.sin(ang), jnp.sin(ang)], axis=-1)[:, None]
            x1, x2 = (x[..., :half], x[..., half:])
            rot = jnp.concatenate([-x2, x1], axis=-1)
            return x * cos + rot * sin
        b, s, _ = x.shape
        g = NQ // NKV
        res = x
        h = ada_rms(x, time_emb, ln1_w, ln1_tw)
        q = (h @ Wq.T).reshape(b, s, NQ, HD).transpose(0, 2, 1, 3)
        k = (h @ Wk.T).reshape(b, s, NKV, HD).transpose(0, 2, 1, 3)
        v = (h @ Wv.T).reshape(b, s, NKV, HD).transpose(0, 2, 1, 3)
        q = apply_rope(q, pos_ids)
        k = apply_rope(k, pos_ids)
        qg = q.reshape(b, NKV, g, s, HD)
        scores = jnp.einsum('bkgsd,bktd->bkgst', qg, k) / jnp.sqrt(jnp.float32(HD))
        attn = jax.nn.softmax(scores, axis=-1)
        ctx = jnp.einsum('bkgst,bktd->bkgsd', attn, v)
        ctx = ctx.reshape(b, NQ, s, HD).transpose(0, 2, 1, 3).reshape(b, s, NQ * HD)
        x = res + ctx @ Wo.T
        res = x
        h = ada_rms(x, time_emb, ln2_w, ln2_tw)
        mlp = jax.nn.silu(h @ Wg.T) * (h @ Wu.T) @ Wd.T
        return res + mlp
    x = _L0_cond_ref(x, cond_2048, mask_1x1xSxS_ff0, L0_cond_Wqkv, L0_cond_q_bias, L0_cond_v_bias, L0_cond_scale_mul_log, L0_cond_Wproj, L0_cond_bproj, L0_cond_Wada, L0_cond_bada, L0_cond_Wfc1, L0_cond_bfc1, L0_cond_Wfc2, L0_cond_bfc2)
    x = _L1_cond_ref(x, pos_BxS, cond_2048, L1_cond_ln1_w, L1_cond_ln1_tw, L1_cond_ln2_w, L1_cond_ln2_tw, L1_cond_Wq, L1_cond_Wk, L1_cond_Wv, L1_cond_Wo, L1_cond_Wg, L1_cond_Wu, L1_cond_Wd)
    return x

_drawn_inputs = setup_inputs


def setup_inputs(seed=0):
    import zlib

    import numpy as np

    out = dict(_drawn_inputs(seed))
    spreads = {'L0_cond_q_bias': (0.0, 0.8),
     'L0_cond_v_bias': (0.0, 0.547),
     'L0_cond_scale_mul_log': (1.3862943649291992, 0.6),
     'L0_cond_bproj': (0.0, 0.1),
     'L0_cond_bada': (0.0, 0.1),
     'L0_cond_bfc1': (0.0, 0.523),
     'L0_cond_bfc2': (0.0, 0.1),
     'L1_cond_ln1_w': (1.0, 0.6),
     'L1_cond_ln2_w': (1.0, 0.6)}
    factors = {'L0_cond_Wqkv': 2.846,
     'L1_cond_ln1_tw': 6.478,
     'L1_cond_Wq': 8.0,
     'L1_cond_Wk': 8.0,
     'L1_cond_Wv': 2.898,
     'L1_cond_Wo': 2.914,
     'L1_cond_ln2_tw': 6.182,
     'L1_cond_Wg': 3.588,
     'L1_cond_Wu': 3.503,
     'L1_cond_Wd': 3.502}
    for name, (base, spread) in spreads.items():
        noise = np.random.default_rng([zlib.crc32(name.encode()), seed]).standard_normal(out[name].shape)
        drawn = base * np.exp(spread * noise) if base else spread * noise
        out[name] = jnp.asarray(drawn.astype(out[name].dtype))
    for name, factor in factors.items():
        out[name] = (out[name] * factor).astype(out[name].dtype)
    return out
```

```python
from contextlib import ExitStack, contextmanager

import numpy as np

import concourse.bass as bass
from concourse import mybir

F32 = mybir.dt.float32
F32R = mybir.dt.float32r
I32 = mybir.dt.int32
ACT = mybir.ActivationFunctionType
ALU = mybir.AluOpType
AX = mybir.AxisListType.X

P = 128
B, L, C = 16, 256, 512
CC = C // P
TB = L // P
H0, D0 = 16, C // 16
H1, D1 = 8, 64
HID = 4 * C
LN_EPS = 1e-6
RMS_EPS = 1e-6
GAMMA1, GAMMA2, SCALE1, SCALE2, SHIFT1, SHIFT2 = range(6)
TWO_PI_HI = 6.28125
TWO_PI_MID = 0.0019350051879882812
TWO_PI_LO = float(2 * np.pi - TWO_PI_HI - TWO_PI_MID)
ROUND = 12582912.0


@contextmanager
def semaphores(nc, prefix):
    made = []

    def sem(name):
        made.append(nc.alloc_semaphore(name=f"{prefix}_{name}"))
        return made[-1]

    yield sem
    nc.clear_and_free_semaphores(made)
    nc.all_engine_barrier()


class At:

    def __init__(self, half, par):
        self.half, self.par = half + par // 2 if par // 2 else half, par % 2

    def __add__(self, k):
        return At(self.half, self.par + k)

    def __sub__(self, k):
        return At(self.half - 4, self.par + 8 - k)

    def count(self, per, k):
        return self.half * (2 * per) + (self.par * per + k)

    def value(self):
        return self.half * 2 + self.par

    def live(self, n=B):
        return not isinstance(self.half, int) or 0 <= self.value() < n


def wait(eng, sem, value):
    if not isinstance(value, int) or value > 0:
        eng.wait_ge(sem, value)


def over_batches(eng, body, n=B):
    for b in range(-2, 2):
        body(At(b // 2, b % 2))
    with eng.Fori(1, n // 2 - 1) as half:
        for par in range(2):
            body(At(half, par))
    for b in range(n - 2, n + 1):
        body(At(b // 2, b % 2))


def split_products(eng, out, stat, mov, first, last):
    eng.matmul(out, stat[0], mov[0], start=first, stop=False)
    eng.matmul(out, stat[0], mov[1], start=False, stop=False)
    return eng.matmul(out, stat[1], mov[0], start=False, stop=last)


def load_split_weights(nc, sem, parts):
    W = 2048
    pieces = [(d, h, lo, c) for d, h, lo in parts for c in range(0, d.shape[1], W)]
    with ExitStack() as ctx:
        stage = ctx.enter_context(nc.sbuf_tensor([P, 2, W], F32))
        loaded = [sem(f"w_loaded{i}") for i in range(2)]
        high, low = sem("w_high"), sem("w_low")
        with nc.Block() as block:
            @block.sync
            def _(sp):
                for n, (d, h, lo, c) in enumerate(pieces):
                    w = min(W, d.shape[1] - c)
                    wait(sp, low, n - 1)
                    sp.dma_start(stage[:, n % 2, 0:w], d[:, c:c + w]).then_inc(loaded[n % 2], 16)

            @block.scalar
            def _(act):
                for n, (d, h, lo, c) in enumerate(pieces):
                    w = min(W, d.shape[1] - c)
                    act.wait_ge(loaded[n % 2], 16 * (n // 2 + 1))
                    act.activation(h[:, c:c + w], stage[:, n % 2, 0:w], ACT.Copy).then_inc(high, 1)

            @block.vector
            def _(dve):
                for n, (d, h, lo, c) in enumerate(pieces):
                    w = min(W, d.shape[1] - c)
                    dve.wait_ge(high, n + 1)
                    dve.tensor_tensor(lo[:, c:c + w], stage[:, n % 2, 0:w], h[:, c:c + w].bitcast(F32),
                                      ALU.subtract).then_inc(low, 1)


def modulation(nc, io, scratch):
    NT = B * TB
    with ExitStack() as ctx:
        def sb(name, shape, dt=F32):
            return ctx.enter_context(nc.sbuf_tensor("mod_" + name, shape, dt))

        sem = ctx.enter_context(semaphores(nc, "mod"))

        cond = sb("cond", [P, CC * B])
        silu = sb("silu", [P, CC * B])
        wada = [sb(f"wada{s}", [P, CC, C]) for s in range(6)]
        tw = [sb(f"tw{s}", [P, CC, C]) for s in range(2)]
        bada = sb("bada", [P, 6 * CC])
        lnw = sb("lnw", [P, 2, CC])
        bgam = sb("bgam", [B, 2 * C])
        gam = sb("gam", [B, 2 * C])
        tmp = sb("tmp", [P, 2, B, CC])
        mod0 = [sb(f"mod0_{s}", [P, B, 2, CC]) for s in range(2)]
        mod1 = [sb(f"mod1_{s}", [P, B, CC]) for s in range(2)]
        pos = sb("pos", [P, NT], I32)
        posf = sb("posf", [P, NT])
        freq = sb("freq", [P, D1 // 2])
        ang = sb("ang", [P, NT, D1 // 2])
        turns = sb("turns", [P, NT, D1 // 2])
        half = sb("half", [P, NT, D1 // 2])
        rope = sb("rope", [P, NT, 2, D1 // 2])
        ps_f = ctx.enter_context(nc.psum_tensor("mod_ps_f", [P, 6 * CC, B], F32))
        ps_g = [ctx.enter_context(nc.psum_tensor(f"mod_ps_g{i}", [B, C], F32)) for i in range(2)]
        loaded, silu_ready, feat_ready, gam_ready = sem("loaded"), sem("silu"), sem("feat"), sem("gam")
        step, sines, stored = sem("dve_step"), sem("sines"), sem("stored")
        SECTION = [SCALE1, SHIFT1, SCALE2, SHIFT2]
        LOADS = 16 * 14
        ANGLES, STEPS = 8, 22

        with nc.Block() as block:
            @block.sync
            def _(sp):
                for dst, src in [(cond[:, :], io["condT"]), (bada[:, :], io["badaF"]),
                                 (lnw[:, :, :], io["lnwF"]), (pos[:, :], io["posT"]),
                                 (freq[:, :], io["freq"].partition_broadcast(P)),
                                 (bgam[:, :], io["bada_gamma"].partition_broadcast(B))]:
                    sp.dma_start(dst, src).then_inc(loaded, 16)
                for s in range(2):
                    sp.dma_start(tw[s][:, :, :], io[f"tw{s + 1}T"]).then_inc(loaded, 16)
                for s in range(6):
                    sp.dma_start(wada[s][:, :, :], io["WadaT"][:, :, s * C:(s + 1) * C]).then_inc(loaded, 16)
                sp.wait_ge(step, STEPS)
                for s in range(2):
                    sp.dma_start(scratch["mod0"][s], mod0[s][:, :, :, :].rearrange("p b s c -> p b (s c)")).then_inc(stored, 16)
                    sp.dma_start(scratch["mod1"][s], mod1[s][:, :, :]).then_inc(stored, 16)
                sp.dma_start(scratch["gamma"], gam[:, :]).then_inc(stored, 16)
                sp.dma_start(scratch["rope"], rope[:, :, :, :].rearrange("p t s f -> p t (s f)")).then_inc(stored, 16)
                sp.wait_ge(stored, 16 * 6)


            @block.scalar
            def _(act):
                act.wait_ge(loaded, LOADS)
                act.activation(silu[:, :], cond[:, :], ACT.Silu).then_inc(silu_ready, 1)
                act.wait_ge(step, ANGLES)
                act.activation(rope[:, :, 1, :], ang[:, :, :], ACT.Sin).then_inc(sines, 1)
                act.activation(half[:, :, :], ang[:, :, :], ACT.Sin, scale=0.5).then_inc(sines, 1)

            @block.tensor
            def _(pe):
                pe.wait_ge(loaded, LOADS)
                pe.wait_ge(silu_ready, 1)
                for v in range(6):
                    w = wada[SECTION[v]] if v < 4 else tw[v - 4]
                    x = silu if v < 4 else cond
                    for c in range(CC):
                        for k in range(CC):
                            last = pe.matmul(ps_f[:, v * CC + c, :], w[:, k, c * P:(c + 1) * P],
                                             x[:, k * B:(k + 1) * B], start=(k == 0), stop=(k == CC - 1))
                last.then_inc(feat_ready, 1)
                for s in range(2):
                    for k in range(CC):
                        last = pe.matmul(ps_g[s][:, :], silu[:, k * B:(k + 1) * B], wada[s][:, k, :],
                                         start=(k == 0), stop=(k == CC - 1))
                last.then_inc(gam_ready, 1)

            @block.vector
            def _(dve):
                done = 0

                def chain(ins):
                    nonlocal done
                    done += 1
                    ins.then_inc(step, 1)
                    dve.wait_ge(step, done)

                dve.wait_ge(loaded, LOADS)
                chain(dve.tensor_copy(posf[:, :], pos[:, :]))
                chain(dve.tensor_tensor(ang[:, :, :], posf[:, :].unsqueeze(2).to_broadcast([P, NT, D1 // 2]),
                                        freq[:, :].unsqueeze(1).to_broadcast([P, NT, D1 // 2]), ALU.mult))
                chain(dve.tensor_scalar(turns[:, :, :], ang[:, :, :], float(1 / (2 * np.pi)), ROUND, ALU.mult, ALU.add))
                chain(dve.tensor_scalar(turns[:, :, :], turns[:, :, :], -ROUND, None, ALU.add))
                for part in (TWO_PI_HI, TWO_PI_MID, TWO_PI_LO):
                    chain(dve.scalar_tensor_tensor(out=ang[:, :, :], in0=turns[:, :, :], scalar=-part,
                                                   in1=ang[:, :, :], op0=ALU.mult, op1=ALU.add))
                chain(dve.tensor_scalar(ang[:, :, :], ang[:, :, :], 3.1415925, -3.1415925, ALU.min, ALU.max))
                dve.wait_ge(feat_ready, 1)
                for v in range(4):
                    s, which = v // 2, v % 2
                    src = ps_f[:, v * CC:(v + 1) * CC, :].rearrange("p c b -> p b c")
                    bias = bada[:, SECTION[v] * CC:(SECTION[v] + 1) * CC].unsqueeze(1).to_broadcast([P, B, CC])
                    dst = mod0[s][:, :, which, :]
                    chain(dve.tensor_tensor(dst, src, bias, ALU.add))
                    if which == 0:
                        chain(dve.tensor_scalar(dst, dst, 1.0, None, ALU.add))
                for s in range(2):
                    src = ps_f[:, (4 + s) * CC:(5 + s) * CC, :].rearrange("p c b -> p b c")
                    chain(dve.tensor_scalar(tmp[:, s, :, :], src, 1.0, None, ALU.add))
                    chain(dve.tensor_tensor(mod1[s][:, :, :], tmp[:, s, :, :],
                                            lnw[:, s, :].unsqueeze(1).to_broadcast([P, B, CC]), ALU.mult))
                dve.wait_ge(gam_ready, 1)
                for s in range(2):
                    chain(dve.tensor_tensor(gam[:, s * C:(s + 1) * C], ps_g[s][:, :], bgam[:, s * C:(s + 1) * C], ALU.add))
                dve.wait_ge(sines, 2)
                chain(dve.tensor_tensor(half[:, :, :], half[:, :, :], half[:, :, :], ALU.mult))
                chain(dve.tensor_scalar(rope[:, :, 0, :], half[:, :, :], -2.0, 1.0, ALU.mult, ALU.add))
                assert done == STEPS, done


def attention_l0(nc, io, scratch):
    with ExitStack() as ctx:
        def sb(name, shape, dt=F32):
            return ctx.enter_context(nc.sbuf_tensor("a0_" + name, shape, dt))

        def pb(name, shape):
            return ctx.enter_context(nc.psum_tensor("a0_" + name, shape, F32))

        sem = ctx.enter_context(semaphores(nc, "a0"))

        G = 4
        NG = H0 // G
        NQ = 3 * C
        wqkv = [sb(f"wqkv{i}", [P, CC * NQ], F32R) for i in range(2)]
        wproj = [sb(f"wproj{i}", [P, CC * C], F32R) for i in range(2)]
        load_split_weights(nc, sem, [(io["WqkvT"], wqkv[0], wqkv[1]), (io["WprojT"], wproj[0], wproj[1])])
        W = [w[:, :].rearrange("p (k n) -> p k n", k=CC) for w in wqkv]
        WP = [w[:, :].rearrange("p (k n) -> p k n", k=CC) for w in wproj]

        xin = sb("xin", [P, 2, TB, C])
        xres = sb("xres", [P, TB, C])
        mod = sb("mod", [P, 2, 2, CC])
        gamma = sb("gamma", [P, 2, C])
        xn = sb("xn", [P, TB, C])
        h32 = sb("h32", [P, 2, L])
        hh = sb("hh", [P, CC, L], F32R)
        hl = sb("hl", [P, CC, L], F32R)
        qk = sb("qk", [P, 2 * C])
        square = sb("square", [P, 2 * C])
        unit = sb("unit", [P, 2, NG, 2, TB * G, D0])
        stack = sb("stack", [P, 2, 2, TB * G, P], F32R)
        v32 = sb("v32", [P, 2, TB, C])
        vh = sb("vh", [P, 2, TB, G, P], F32R)
        vl = sb("vl", [P, 2, TB, G, P], F32R)
        qkT = sb("qkT", [P, 2, 2, L], F32R)
        prob = sb("prob", [P, 4, TB, L])
        pTh = sb("pTh", [P, 2, TB, L], F32R)
        pTl = sb("pTl", [P, 2, TB, L], F32R)
        rdT = sb("rdT", [P, L])
        o32 = sb("o32", [P, L])
        oTh = sb("oTh", [P, NG, L], F32R)
        oTl = sb("oTl", [P, NG, L], F32R)
        y = sb("y", [P, TB, C])
        mask = sb("mask", [P, TB, L])
        qbias, vbias, pbias = sb("qbias", [P, C]), sb("vbias", [P, C]), sb("pbias", [P, C])
        ident = sb("ident", [P, P])
        sm = sb("sm", [P, 2 * H0])
        minus_half = sb("minus_half", [P, 2 * H0])
        spacer = sb("spacer", [P, 5])
        stats = sb("stats", [P, 6])
        mv = sb("mv", [P, 2])
        var = sb("var", [P, 1])
        rstd = sb("rstd", [P, 1])
        ss = sb("ss", [P, 2 * H0])
        norm = sb("norm", [P, 2 * H0])
        inv = sb("inv", [P, 2 * H0])
        nmax = sb("nmax", [P, 4, TB])
        den = sb("den", [P, 2, TB, G])
        rd = sb("rd", [P, TB, G])
        rden = sb("rden", [P, 2, TB, G * D0])

        psT = pb("psT", [P, 2, L])
        psF = pb("psF", [P, C])
        psS = [pb(f"psS{i}", [P, TB, L]) for i in range(2)]
        psP = [pb(f"psP{i}", [P, TB, L]) for i in range(2)]
        psO = [pb(f"psO{i}", [P, 2, L]) for i in range(2)]

        consts_loaded, const_ready = sem("consts_loaded"), sem("const_ready")
        x_loaded = [sem(f"x_loaded{i}") for i in range(2)]
        mod_loaded = [sem(f"mod_loaded{i}") for i in range(2)]
        gamma_loaded = [sem(f"gamma_loaded{i}") for i in range(2)]
        res_loaded = [sem(f"res_loaded{i}") for i in range(TB)]
        stored = [sem(f"stored{i}") for i in range(TB)]
        mean_ready, var_ready, rstd_ready, xn_ready = sem("mean"), sem("var"), sem("rstd"), sem("xn")
        stats_ready = sem("stats")
        hT_ready, h32_ready, hh_ready, hl_ready = sem("hT"), sem("h32"), sem("hh"), sem("hl")
        q_ready, k_ready, v_ready = sem("q_ready"), sem("k_ready"), sem("v_ready")
        q_taken, k_taken, v_taken = sem("q_taken"), sem("k_taken"), sem("v_taken")
        sq_ready, ss_ready, norm_ready = sem("sq"), sem("ss"), sem("norm")
        pow_ready, inv_ready, unit_ready = sem("pow"), sem("inv"), sem("unit")
        stack_high_ready, stack_ready = sem("stack_high"), sem("stack")
        t_ready, t_taken = sem("t_ready"), [sem("t_taken_act"), sem("t_taken_dve")]
        s_ready, max_ready, exp_ready = sem("s_ready"), sem("max_ready"), sem("exp_ready")
        p_ready, pTh_ready, pTl_ready = sem("p_ready"), sem("pTh"), sem("pTl")
        vh_ready, vl_ready, pv_ready = sem("vh"), sem("vl"), sem("pv")
        rden_ready, rdp_ready, rdT_ready = sem("rden"), sem("rdp"), sem("rdT")
        rd_ready = sem("rd")
        o32_ready, oTh_ready, oTl_ready = sem("o32"), sem("oTh"), sem("oTl")
        proj_ready, y_bias, y_gamma, y_ready = sem("proj"), sem("y_bias"), sem("y_gamma"), sem("y_ready")
        CONSTS = 16 * 6

        LN_AT = {0: 0, 1: 1}
        HT_AT = {2: 0, 3: 1}
        Q_AT, K_AT, V_AT = {4: 0, 9: 1}, {5: 0, 10: 1}, {6: 0, 12: 1}
        PROJ_AT = {7: 0, 8: 1}
        NORM_AT = {6: 0, 11: 1}
        UNIT_AT = {8: 0, 13: 1}
        SCORES, EXP, PT, SPLIT, VALUES, OUT, OUT_SPLIT = 1, 2, 3, 4, 5, 6, 7

        def head(b, s, lag):
            return (b, s - lag) if s >= lag else (b - 1, H0 + s - lag)

        def stack_parts(g, i):
            if i == 0:
                rows = stack[:, g % 2, i, :, :].rearrange("p n (r s d) -> p n r s d", r=2, s=2)
                return rows[:, :, :, 0, :], rows[:, :, :, 1, :]
            rows = stack[:, g % 2, i, :, :].rearrange("p n (s r d) -> p n s r d", r=2, s=2)
            return rows[:, :, 0, :, :], rows[:, :, 1, :, :]

        def next_group(b, s):
            return (b, s // G + 1) if s < H0 - G else (b + 1, 0)

        def pieces(b, s, fn, table):
            if s in table and b.live():
                fn(b, table[s])

        with nc.Block() as block:
            @block.sync
            def _(sp):
                for dst, src in [(mask[:, :, :], io["mask"]), (qbias[:, :], io["q_bias"].partition_broadcast(P)),
                                 (vbias[:, :], io["v_bias"].partition_broadcast(P)),
                                 (pbias[:, :], io["bproj"].partition_broadcast(P)),
                                 (sm[:, 0:H0], io["scale_mul_log"].partition_broadcast(P)),
                                 (ident[:, :], io["ident"])]:
                    sp.dma_start(dst, src).then_inc(consts_loaded, 16)

                def load_front(b):
                    wait(sp, xn_ready, (b - 2).count(TB, TB))
                    sp.dma_start(xin[:, b.par, :, :], io["x"][bass.ds(b.value() * L, L), :].rearrange("(t p) c -> p t c", p=P))\
                      .then_inc(x_loaded[b.par], 16)
                    wait(sp, h32_ready, (b - 2).count(CC, CC))
                    sp.dma_start(mod[:, b.par, :, :].rearrange("p s c -> p (s c)"),
                                 scratch["mod0"][0, :, bass.ds(b.value(), 1), :].rearrange("p b s -> p (b s)"))\
                      .then_inc(mod_loaded[b.par], 16)

                def load_back(b):
                    wait(sp, y_gamma, (b - 1).count(TB, TB))
                    sp.dma_start(gamma[:, b.par, :],
                                 scratch["gamma"][bass.ds(b.value(), 1), GAMMA1 * C:(GAMMA1 + 1) * C].partition_broadcast(P)
                                 .rearrange("p a c -> p (a c)"))\
                      .then_inc(gamma_loaded[b.par], 16)
                    for t in range(TB):
                        wait(sp, y_ready, (b - 1).count(TB, t + 1))
                        sp.dma_start(xres[:, t, :], io["x"][bass.ds(b.value() * L + t * P, P), :]).then_inc(res_loaded[t], 16)

                def store(b):
                    for t in range(TB):
                        wait(sp, y_ready, b.count(TB, t + 1))
                        sp.dma_start(scratch["x1"][bass.ds(b.value() * L + t * P, P), :], y[:, t, :]).then_inc(stored[t], 16)

                def body(b):
                    if (b + 1).live():
                        load_front(b + 1)
                    if (b - 1).live():
                        load_back(b - 1)
                        store(b - 1)

                over_batches(sp, body)
                for t in range(TB):
                    sp.wait_ge(stored[t], 16 * B)

            @block.gpsimd
            def _(pool):
                pool.memset(minus_half[:, :], -0.5).then_inc(const_ready, 1)
                pool.memset(vh[:, :, :, :, :].bitcast(F32), 0.0).then_inc(const_ready, 1)
                pool.memset(vl[:, :, :, :, :].bitcast(F32), 0.0).then_inc(const_ready, 1)
                pool.wait_ge(const_ready, 3)

                def layer_norm(b, t):
                    wait(pool, var_ready, b.count(TB, t + 1))
                    pool.tensor_tensor(rstd[:, :], var[:, :], minus_half[:, 0:1], ALU.pow).then_inc(rstd_ready, 1)

                def unit_heads(b, t):
                    wait(pool, norm_ready, b.count(TB, t + 1))
                    pool.tensor_tensor(norm[:, :], norm[:, :], minus_half[:, :], ALU.pow).then_inc(pow_ready, 1)

                def stack_low(b, g):
                    wait(pool, stack_high_ready, b.count(NG, g + 1))
                    for i in range(2):
                        src = unit[:, b.par, g, i, :, :].unsqueeze(2).to_broadcast([P, TB * G, 2, D0])
                        high, low = stack_parts(g, i)
                        ins = pool.tensor_tensor(low, src, high.bitcast(F32), ALU.subtract)
                    ins.then_inc(stack_ready, 1)

                def values_low(b, g):
                    wait(pool, vh_ready, b.count(NG, g + 1))
                    for j in range(G):
                        src = (slice(None), g % 2, slice(None), j, slice(D0 * j, D0 * j + D0))
                        ins = pool.tensor_tensor(vl[src], v32[:, b.par, :, (g * G + j) * D0:(g * G + j + 1) * D0],
                                                 vh[src].bitcast(F32), ALU.subtract)
                    ins.then_inc(vl_ready, 1)

                def residual(b, t):
                    wait(pool, y_bias, b.count(TB, t + 1))
                    pool.wait_ge(gamma_loaded[b.par], b.half * 16 + 16)
                    pool.tensor_tensor(y[:, t, :], y[:, t, :], gamma[:, b.par, :], ALU.mult).then_inc(y_gamma, 1)
                    pool.wait_ge(res_loaded[t], b.count(16, 16))
                    wait(pool, y_gamma, b.count(TB, t + 1))
                    pool.tensor_tensor(y[:, t, :], y[:, t, :], xres[:, t, :], ALU.add).then_inc(y_ready, 1)

                def body(b):
                    for s in range(H0):
                        if b.live() and s % G == 1:
                            values_low(b, s // G)
                        if s % G == 2:
                            bb, g = next_group(b, s)
                            if bb.live():
                                stack_low(bb, g)
                        pieces(b + 1, s, layer_norm, LN_AT)
                        pieces(b + 1, s, unit_heads, NORM_AT)
                        pieces(b - 1, s, residual, PROJ_AT)

                over_batches(pool, body)

            @block.scalar
            def _(act):
                act.wait_ge(const_ready, 5)
                act.activation(sm[:, 0:H0], sm[:, 0:H0], ACT.Exp).then_inc(const_ready, 1)

                def modulate(b, pair):
                    act.wait_ge(mod_loaded[b.par], b.half * 16 + 16)
                    wait(act, hT_ready, b.count(2, pair + 1))
                    for i in range(2):
                        c = 2 * pair + i
                        wait(act, hl_ready, b.count(CC, c - 1))
                        act.activation(h32[:, i, :], psF[:, i * L:(i + 1) * L], ACT.Identity,
                                       bias=mod[:, b.par, 1, c:c + 1], scale=mod[:, b.par, 0, c:c + 1]).then_inc(h32_ready, 1)
                    if pair == 0:
                        wait(act, v_ready, (b - 1).count(TB, TB))
                    for i in range(2):
                        c = 2 * pair + i
                        act.wait_ge(h32_ready, b.count(CC, c + 1))
                        act.activation(hh[:, c, :], h32[:, i, :], ACT.Copy).then_inc(hh_ready, 1)

                def take_k(b, t):
                    wait(act, k_ready, b.count(TB, t + 1))
                    wait(act, unit_ready, b.count(TB, t))
                    act.activation(qk[:, C:2 * C], psF[:, :], ACT.Copy).then_inc(k_taken, 1)

                def unit_heads(b, t):
                    wait(act, q_taken, b.count(TB, t + 1))
                    wait(act, k_taken, b.count(TB, t + 1))
                    wait(act, ss_ready, b.count(TB, t))
                    act.activation(square[:, :], qk[:, :], ACT.Square).then_inc(sq_ready, 1)

                def stack_high(b, g):
                    if g == 0:
                        wait(act, unit_ready, b.count(TB, TB))
                    wait(act, t_ready, b.count(H0, (g - 1) * G))
                    for i in range(2):
                        src = unit[:, b.par, g, i, :, :].unsqueeze(2).to_broadcast([P, TB * G, 2, D0])
                        ins = act.activation(stack_parts(g, i)[0], src, ACT.Copy)
                    ins.then_inc(stack_high_ready, 1)

                def values_high(b, g):
                    if g == 0:
                        wait(act, v_taken, b.count(TB, TB))
                    wait(act, pv_ready, b.count(H0, (g - 1) * G))
                    for j in range(G):
                        ins = act.activation(vh[:, g % 2, :, j, D0 * j:D0 * j + D0],
                                             v32[:, b.par, :, (g * G + j) * D0:(g * G + j + 1) * D0], ACT.Copy)
                    ins.then_inc(vh_ready, 1)

                def take_heads(b, h):
                    wait(act, t_ready, b.count(H0, h + 1))
                    wait(act, s_ready, b.count(H0, h - 1))
                    act.activation(qkT[:, h % 2, :, :], psT[:, :, :], ACT.Copy).then_inc(t_taken[0], 1)

                def softmax(b, h):
                    g, j = h // G, h % G
                    wait(act, max_ready, b.count(H0, h + 1))
                    if j == 0:
                        wait(act, rden_ready, b.count(NG, g - 1))
                    for qc in range(TB):
                        ins = act.activation(prob[:, h % 4, qc, :], prob[:, h % 4, qc, :], ACT.Exp, scale=-1.0,
                                             bias=nmax[:, h % 4, qc:qc + 1], accum_out=den[:, g % 2, qc, j:j + 1])
                    ins.then_inc(exp_ready, 1)

                def probs_high(b, h):
                    wait(act, p_ready, b.count(H0, h + 1))
                    wait(act, pv_ready, b.count(H0, h - 1))
                    act.activation(pTh[:, h % 2, :, :], psP[h % 2][:, :, :], ACT.Copy).then_inc(pTh_ready, 1)

                def take_denominators(b, g):
                    wait(act, rdp_ready, b.count(NG, g + 1))
                    wait(act, o32_ready, b.count(NG, g))
                    act.activation(rdT[:, :], psO[g % 2][:, 1, :], ACT.Copy).then_inc(rdT_ready, 1)

                def output_high(b, g):
                    act.wait_ge(o32_ready, b.count(NG, g + 1))
                    if g == 0:
                        wait(act, proj_ready, (b - 1).count(TB, TB))
                    act.activation(oTh[:, g, :], o32[:, :], ACT.Copy).then_inc(oTh_ready, 1)

                def body(b):
                    for s in range(H0):
                        for lag, stage in ((OUT_SPLIT, output_high), (OUT, take_denominators)):
                            bb, h = head(b, s, lag)
                            if bb.live() and h % G == G - 1:
                                stage(bb, h // G)
                        for lag, stage in ((SPLIT, probs_high), (EXP, softmax)):
                            bb, h = head(b, s, lag)
                            if bb.live():
                                stage(bb, h)
                        if b.live():
                            if s % 2 == 0:
                                take_heads(b, s)
                            if s % G == 1:
                                values_high(b, s // G)
                        if s % G == 2:
                            bb, g = next_group(b, s)
                            if bb.live():
                                stack_high(bb, g)
                        pieces(b + 1, s, modulate, HT_AT)
                        pieces(b + 1, s, take_k, K_AT)
                        pieces(b + 1, s, unit_heads, NORM_AT)

                over_batches(act, body)

            @block.tensor
            def _(pe):
                pe.wait_ge(consts_loaded, CONSTS)
                pe.wait_ge(const_ready, 5)

                def transposes_h(b, pair):
                    if pair == 0:
                        wait(pe, xn_ready, b.count(TB, TB))
                        wait(pe, v_taken, (b - 1).count(TB, TB))
                    else:
                        wait(pe, h32_ready, b.count(CC, 2))
                    for i in range(2):
                        for t in range(TB):
                            c = 2 * pair + i
                            last = pe.transpose(psF[:, i * L + t * P:i * L + (t + 1) * P], xn[:, t, c * P:(c + 1) * P], ident[:, :])
                    last.then_inc(hT_ready, 1)

                def project(b, t, section, ready):
                    for k in range(CC):
                        last = split_products(pe, psF[:, :], (hh[:, k, t * P:(t + 1) * P], hl[:, k, t * P:(t + 1) * P]),
                                              [w[:, k, section * C:(section + 1) * C] for w in W], k == 0, k == CC - 1)
                    last.then_inc(ready, 1)

                def project_q(b, t):
                    if t == 0:
                        wait(pe, hl_ready, b.count(CC, CC))
                    elif (b - 2).live():
                        wait(pe, y_bias, (b - 2).count(TB, TB))
                    else:
                        wait(pe, v_taken, b.count(TB, t))
                    project(b, t, 0, q_ready)

                def project_k(b, t):
                    wait(pe, q_taken, b.count(TB, t + 1))
                    project(b, t, 1, k_ready)

                def project_v(b, t):
                    wait(pe, k_taken, b.count(TB, t + 1))
                    project(b, t, 2, v_ready)

                def transposes_qk(b, h):
                    g, j = h // G, h % G
                    if j == 0:
                        wait(pe, stack_ready, b.count(NG, g + 1))
                    wait(pe, t_taken[(h - 1) % 2], b.count(H0 // 2, (h + 1) // 2))
                    for i in range(2):
                        for t in range(TB):
                            last = pe.transpose(psT[:, i, t * P:(t + 1) * P], stack[:, g % 2, i, t * G + j, :].bitcast(F32),
                                                ident[:, :])
                    last.then_inc(t_ready, 1)

                def scores(b, h):
                    wait(pe, t_taken[h % 2], b.count(H0 // 2, h // 2 + 1))
                    wait(pe, max_ready, b.count(H0, h - 1))
                    for qc in range(TB):
                        last = pe.matmul(psS[h % 2][:, qc, :], qkT[:, h % 2, 0, qc * P:(qc + 1) * P], qkT[:, h % 2, 1, :],
                                         start=True, stop=True)
                    last.then_inc(s_ready, 1)

                def transposes_p(b, h):
                    wait(pe, exp_ready, b.count(H0, h + 1))
                    wait(pe, pTl_ready, b.count(H0, h - 1))
                    for kc in range(TB):
                        for qc in range(TB):
                            last = pe.transpose(psP[h % 2][:, kc, qc * P:(qc + 1) * P], prob[:, h % 4, qc, kc * P:(kc + 1) * P],
                                                ident[:, :])
                    last.then_inc(p_ready, 1)

                def values(b, h):
                    g, j = h // G, h % G
                    if j == 0:
                        wait(pe, vl_ready, b.count(NG, g + 1))
                        wait(pe, o32_ready, b.count(NG, g - 1))
                    wait(pe, pTl_ready, b.count(H0, h + 1))
                    for kc in range(TB):
                        last = split_products(pe, psO[g % 2][:, 0, :], (vh[:, g % 2, kc, j, :], vl[:, g % 2, kc, j, :]),
                                              (pTh[:, h % 2, kc, :], pTl[:, h % 2, kc, :]),
                                              j == 0 and kc == 0, j == G - 1 and kc == TB - 1)
                    last.then_inc(pv_ready, 1)
                    if j == G - 1:
                        wait(pe, rden_ready, b.count(NG, g + 1))
                        for qc in range(TB):
                            last = pe.transpose(psO[g % 2][:, 1, qc * P:(qc + 1) * P],
                                                rden[:, g % 2, qc, :], ident[:, :])
                        last.then_inc(rdp_ready, 1)

                def project_out(b, t):
                    if t == 0:
                        wait(pe, oTl_ready, b.count(NG, NG))
                    nxt = b + 2
                    if t == 1:
                        wait(pe, y_bias, b.count(TB, 1))
                    elif nxt.live():
                        wait(pe, v_taken, nxt.count(TB, 1))
                    else:
                        wait(pe, v_taken, TB * B)
                        wait(pe, y_bias, (b - 1).count(TB, TB))
                    for g in range(NG):
                        last = split_products(pe, psF[:, :], (oTh[:, g, t * P:(t + 1) * P], oTl[:, g, t * P:(t + 1) * P]),
                                              [w[:, g, :] for w in WP], g == 0, g == NG - 1)
                    last.then_inc(proj_ready, 1)

                def body(b):
                    for s in range(H0):
                        for lag, stage in ((VALUES, values), (PT, transposes_p), (SCORES, scores)):
                            bb, h = head(b, s, lag)
                            if bb.live():
                                stage(bb, h)
                        if b.live():
                            transposes_qk(b, s)
                        pieces(b + 1, s, transposes_h, HT_AT)
                        pieces(b - 1, s, project_out, PROJ_AT)
                        pieces(b + 1, s, project_q, Q_AT)
                        pieces(b + 1, s, project_k, K_AT)
                        pieces(b + 1, s, project_v, V_AT)

                over_batches(pe, body)

            @block.vector
            def _(dve):
                dve.wait_ge(consts_loaded, CONSTS)
                dve.tensor_scalar(sm[:, 0:H0], sm[:, 0:H0], float(np.log(np.float32(100.0))), None, ALU.min)\
                   .then_inc(const_ready, 1)
                dve.memset(sm[:, H0:2 * H0], 1.0).then_inc(const_ready, 1)
                dve.wait_ge(const_ready, 6)

                def layer_norm(b, t):
                    dve.wait_ge(x_loaded[b.par], b.half * 16 + 16)
                    x = xin[:, b.par, t, :]
                    dve.bn_stats(stats[:, :], x).then_inc(stats_ready, 1)
                    dve.wait_ge(stats_ready, b.count(TB, t + 1))
                    dve.memset(spacer[:, 4:5], 0.0)
                    dve.bn_aggr(mv[:, :], stats[:, :]).then_inc(mean_ready, 1)
                    dve.wait_ge(mean_ready, b.count(TB, t + 1))
                    dve.tensor_scalar(var[:, :], mv[:, 1:2], LN_EPS, None, ALU.add).then_inc(var_ready, 1)
                    if t == 0:
                        wait(dve, hT_ready, (b - 1).count(2, 2))
                    dve.wait_ge(rstd_ready, b.count(TB, t + 1))
                    dve.tensor_scalar(xn[:, t, :], x, mv[:, 0:1], rstd[:, 0:1], ALU.subtract, ALU.mult).then_inc(xn_ready, 1)

                def low_h(b, pair):
                    for i in range(2):
                        c = 2 * pair + i
                        dve.wait_ge(hh_ready, b.count(CC, c + 1))
                        dve.tensor_tensor(hl[:, c, :], h32[:, i, :], hh[:, c, :].bitcast(F32), ALU.subtract).then_inc(hl_ready, 1)

                def take_q(b, t):
                    dve.wait_ge(q_ready, b.count(TB, t + 1))
                    wait(dve, unit_ready, b.count(TB, t))
                    dve.tensor_tensor(qk[:, 0:C], psF[:, :], qbias[:, :], ALU.add).then_inc(q_taken, 1)

                def take_v(b, t):
                    dve.wait_ge(v_ready, b.count(TB, t + 1))
                    wait(dve, vl_ready, (b - 2).count(NG, NG))
                    dve.tensor_tensor(v32[:, b.par, t, :], psF[:, :], vbias[:, :], ALU.add).then_inc(v_taken, 1)

                def square_sums(b, t):
                    dve.wait_ge(sq_ready, b.count(TB, t + 1))
                    dve.tensor_reduce(ss[:, :], square[:, :].rearrange("p (h d) -> p h d", d=D0), AX, ALU.add).then_inc(ss_ready, 1)
                    dve.wait_ge(ss_ready, b.count(TB, t + 1))
                    dve.tensor_scalar(norm[:, :], ss[:, :], 1e-24, None, ALU.max).then_inc(norm_ready, 1)

                def make_unit(b, t):
                    dve.wait_ge(pow_ready, b.count(TB, t + 1))
                    dve.tensor_tensor(inv[:, :], norm[:, :], sm[:, :], ALU.mult).then_inc(inv_ready, 1)
                    dve.wait_ge(inv_ready, b.count(TB, t + 1))
                    if t == 0:
                        wait(dve, stack_ready, (b - 1).count(NG, 0))
                    for i in range(2):
                        heads = qk[:, i * C:(i + 1) * C].rearrange("p (g j d) -> p g j d", g=NG, j=G)
                        scale = inv[:, i * H0:(i + 1) * H0].rearrange("p (g j) -> p g j", g=NG).unsqueeze(3)\
                            .to_broadcast([P, NG, G, D0])
                        ins = dve.tensor_tensor(unit[:, b.par, :, i, t * G:(t + 1) * G, :], heads, scale, ALU.mult)
                    ins.then_inc(unit_ready, 1)

                def take_heads(b, h):
                    dve.wait_ge(t_ready, b.count(H0, h + 1))
                    wait(dve, s_ready, b.count(H0, h - 1))
                    dve.tensor_copy(qkT[:, h % 2, :, :], psT[:, :, :]).then_inc(t_taken[1], 1)

                def score_max(b, h):
                    dve.wait_ge(s_ready, b.count(H0, h + 1))
                    wait(dve, p_ready, b.count(H0, h - 3))
                    dve.memset(spacer[:, h % 4:h % 4 + 1], 0.0)
                    for qc in range(TB):
                        ins = dve.tensor_tensor_reduce(prob[:, h % 4, qc, :], psS[h % 2][:, qc, :], mask[:, qc, :], -1.0, 3e38,
                                                       ALU.add, ALU.min, nmax[:, h % 4, qc:qc + 1])
                    ins.then_inc(max_ready, 1)

                def probs_low(b, h):
                    dve.wait_ge(pTh_ready, b.count(H0, h + 1))
                    dve.tensor_tensor(pTl[:, h % 2, :, :], psP[h % 2][:, :, :], pTh[:, h % 2, :, :].bitcast(F32), ALU.subtract)\
                       .then_inc(pTl_ready, 1)

                def denominators(b, g):
                    dve.wait_ge(exp_ready, b.count(H0, (g + 1) * G))
                    wait(dve, rdp_ready, b.count(NG, g - 1))
                    dve.reciprocal(rd[:, :, :], den[:, g % 2, :, :]).then_inc(rd_ready, 1)
                    dve.wait_ge(rd_ready, b.count(NG, g + 1))
                    dve.tensor_copy(rden[:, g % 2, :, :].rearrange("p q (j d) -> p q j d", j=G),
                                    rd[:, :, :].unsqueeze(3).to_broadcast([P, TB, G, D0])).then_inc(rden_ready, 1)

                def group_output(b, g):
                    dve.wait_ge(rdT_ready, b.count(NG, g + 1))
                    wait(dve, oTl_ready, b.count(NG, g))
                    dve.tensor_tensor(o32[:, :], psO[g % 2][:, 0, :], rdT[:, :], ALU.mult).then_inc(o32_ready, 1)

                def output_low(b, g):
                    dve.wait_ge(oTh_ready, b.count(NG, g + 1))
                    dve.tensor_tensor(oTl[:, g, :], o32[:, :], oTh[:, g, :].bitcast(F32), ALU.subtract).then_inc(oTl_ready, 1)

                def add_bias(b, t):
                    dve.wait_ge(proj_ready, b.count(TB, t + 1))
                    wait(dve, stored[t], (b - 1).count(16, 16))
                    dve.tensor_tensor(y[:, t, :], psF[:, :], pbias[:, :], ALU.add).then_inc(y_bias, 1)

                def body(b):
                    for s in range(H0):
                        for lag, stage in ((OUT_SPLIT, output_low), (OUT, group_output)):
                            bb, h = head(b, s, lag)
                            if bb.live() and h % G == G - 1:
                                stage(bb, h // G)
                        for lag, stage in ((SPLIT, probs_low), (SCORES, score_max)):
                            bb, h = head(b, s, lag)
                            if bb.live():
                                stage(bb, h)
                        bb, h = head(b, s, PT)
                        if bb.live() and h % G == G - 1:
                            denominators(bb, h // G)
                        if b.live() and s % 2 == 1:
                            take_heads(b, s)
                        pieces(b + 1, s, layer_norm, LN_AT)
                        pieces(b + 1, s, low_h, HT_AT)
                        pieces(b + 1, s, take_q, Q_AT)
                        pieces(b + 1, s, take_v, V_AT)
                        pieces(b + 1, s, square_sums, NORM_AT)
                        pieces(b + 1, s, make_unit, UNIT_AT)
                        pieces(b - 1, s, add_bias, PROJ_AT)

                over_batches(dve, body)



def over_blocks(eng, body):
    over_batches(eng, body, B // 2)


def mlp_l0(nc, io, scratch):
    with ExitStack() as ctx:
        def sb(name, shape, dt=F32):
            return ctx.enter_context(nc.sbuf_tensor("m0_" + name, shape, dt))

        def pb(name, shape):
            return ctx.enter_context(nc.psum_tensor("m0_" + name, shape, F32))

        sem = ctx.enter_context(semaphores(nc, "m0"))

        NJ = HID // P
        TT = 2 * TB
        T = TT * P
        NB = B // 2
        DOWN, ACT_LAG = 3, 1
        w1 = [sb(f"w1{i}", [P, CC * HID], F32R) for i in range(2)]
        w2 = [sb(f"w2{i}", [P, NJ * C], F32R) for i in range(2)]
        load_split_weights(nc, sem, [(io["Wfc1T"], w1[0], w1[1]), (io["Wfc2T"], w2[0], w2[1])])
        W1 = [w[:, :].rearrange("p (k n) -> p k n", k=CC) for w in w1]
        W2 = [w[:, :].rearrange("p (k n) -> p k n", k=NJ) for w in w2]

        xin = sb("xin", [P, 2, C])
        xres = sb("xres", [P, 2, C])
        mod = sb("mod", [P, 2, 2, 2 * CC])
        gamma = sb("gamma", [P, 2, C])
        b1 = sb("b1", [P, NJ])
        b2 = sb("b2", [P, C])
        ident = sb("ident", [P, P])
        minus_half = sb("minus_half", [P, 1])
        xn = sb("xn", [P, TT, C])
        h32 = sb("h32", [P, 2, T])
        hh = sb("hh", [P, CC, T], F32R)
        hl = sb("hl", [P, CC, T], F32R)
        act32 = sb("act32", [P, 2, T])
        uh = sb("uh", [P, 4, T], F32R)
        ul = sb("ul", [P, 4, T], F32R)
        y = sb("y", [P, TT, C])
        spacer = sb("spacer", [P, 1])
        stats, mv, var, rstd = sb("stats", [P, 6]), sb("mv", [P, 2]), sb("var", [P, 1]), sb("rstd", [P, 1])

        psT = [pb(f"psT{i}", [P, T]) for i in range(2)]
        psU = [pb(f"psU{i}", [P, T]) for i in range(2)]
        psD = [pb(f"psD{i}", [P, C]) for i in range(TT)]

        consts_loaded, const_ready = sem("consts_loaded"), sem("const_ready")
        x_loaded = [sem(f"x_loaded{i}") for i in range(2)]
        res_loaded = [sem(f"res_loaded{i}") for i in range(2)]
        stored = [sem(f"stored{i}") for i in range(TT)]
        mod_loaded = [sem(f"mod_loaded{i}") for i in range(2)]
        gamma_loaded = sem("gamma_loaded")
        stats_ready, mean_ready, var_ready, rstd_ready, xn_ready = sem("stats"), sem("mean"), sem("var"), sem("rstd"), sem("xn")
        hT_ready, h32_ready, hh_ready, hl_ready = sem("hT"), sem("h32"), sem("hh"), sem("hl")
        up_ready, act_ready, uh_ready, ul_ready, down_ready = sem("up"), sem("act"), sem("uh"), sem("ul"), sem("down")
        y_bias, y_gamma, y_ready = sem("y_bias"), sem("y_gamma"), sem("y_ready")

        LN_AT = {4: 0, 6: 1, 8: 2, 10: 3}
        HT_AT = {12: 0, 13: 1, 14: 2, 15: 3}
        OUT_AT = 3

        def chunk(b, s, lag):
            return (b, s - lag) if s >= lag else (b - 1, NJ + s - lag)

        def pieces(b, s, fn, table):
            if s in table and b.live(NB):
                fn(b, table[s])

        with nc.Block() as block:
            @block.sync
            def _(sp):
                for dst, src in [(b1[:, :], io["bfc1F"]), (b2[:, :], io["bfc2"].partition_broadcast(P)),
                                 (ident[:, :], io["ident"])]:
                    sp.dma_start(dst, src).then_inc(consts_loaded, 16)

                def load_front(b, t):
                    if t == 0:
                        wait(sp, h32_ready, (b - 2).count(CC, CC))
                        sp.dma_start(mod[:, b.par, :, :].rearrange("p b s -> p (b s)"),
                                     scratch["mod0"][1, :, bass.ds(b.value() * 2, 2), :].rearrange("p b s -> p (b s)"))\
                          .then_inc(mod_loaded[b.par], 16)
                    wait(sp, xn_ready, b.count(TT, t - 1))
                    sp.dma_start(xin[:, t % 2, :], scratch["x1"][bass.ds((b.value() * TT + t) * P, P), :])\
                      .then_inc(x_loaded[t % 2], 16)

                def back(b, t):
                    if t == 0:
                        wait(sp, y_gamma, (b - 1).count(TT, TT))
                        for i in range(2):
                            sp.dma_start(gamma[:, i, :], scratch["gamma"][bass.ds(b.value() * 2 + i, 1), GAMMA2 * C:(GAMMA2 + 1) * C]
                                         .partition_broadcast(P).rearrange("p a c -> p (a c)")).then_inc(gamma_loaded, 16)
                    wait(sp, y_ready, b.count(TT, t - 1))
                    sp.dma_start(xres[:, t % 2, :], scratch["x1"][bass.ds((b.value() * TT + t) * P, P), :])\
                      .then_inc(res_loaded[t % 2], 16)

                def store(b, t):
                    wait(sp, y_ready, b.count(TT, t + 1))
                    sp.dma_start(scratch["x2"][bass.ds((b.value() * TT + t) * P, P), :], y[:, t, :]).then_inc(stored[t], 16)

                def body(b):
                    for t in range(TT):
                        if (b - 1).live(NB):
                            back(b - 1, t)
                            if t > 0:
                                store(b - 1, t - 1)
                    if (b - 1).live(NB):
                        store(b - 1, TT - 1)
                    for t in range(TT):
                        if (b + 1).live(NB):
                            load_front(b + 1, t)

                over_blocks(sp, body)
                for t in range(TT):
                    sp.wait_ge(stored[t], 16 * NB)

            @block.gpsimd
            def _(pool):
                pool.memset(minus_half[:, :], -0.5).then_inc(const_ready, 1)
                pool.wait_ge(const_ready, 1)

                def layer_norm(b, t):
                    pool.wait_ge(var_ready, b.count(TT, t + 1))
                    pool.tensor_tensor(rstd[:, :], var[:, :], minus_half[:, :], ALU.pow).then_inc(rstd_ready, 1)

                def residual(b, t):
                    pool.wait_ge(gamma_loaded, b.count(32, 32))
                    pool.wait_ge(y_bias, b.count(TT, t + 1))
                    pool.tensor_tensor(y[:, t, :], y[:, t, :], gamma[:, t // TB, :], ALU.mult).then_inc(y_gamma, 1)
                    pool.wait_ge(res_loaded[t % 2], b.count(32, 16 * (t // 2 + 1)))
                    pool.wait_ge(y_gamma, b.count(TT, t + 1))
                    pool.tensor_tensor(y[:, t, :], y[:, t, :], xres[:, t % 2, :], ALU.add).then_inc(y_ready, 1)

                def body(b):
                    for s in range(NJ):
                        if s == OUT_AT and (b - 1).live(NB):
                            for t in range(TT):
                                residual(b - 1, t)
                        pieces(b + 1, s, layer_norm, LN_AT)

                over_blocks(pool, body)

            @block.scalar
            def _(act):
                act.wait_ge(consts_loaded, 48)

                def gelu(b, j):
                    act.wait_ge(up_ready, b.count(NJ, j + 1))
                    wait(act, ul_ready, b.count(NJ, j - 1))
                    act.activation(act32[:, j % 2, :], psU[j % 2][:, :], ACT.Gelu_apprx_tanh, bias=b1[:, j:j + 1]).then_inc(act_ready, 1)
                    act.wait_ge(act_ready, b.count(NJ, j + 1))
                    wait(act, down_ready, b.count(NJ, j - 3))
                    act.activation(uh[:, j % 4, :], act32[:, j % 2, :], ACT.Copy).then_inc(uh_ready, 1)

                def modulate(b, c):
                    if c == 0:
                        act.wait_ge(mod_loaded[b.par], b.half * 16 + 16)
                    act.wait_ge(hT_ready, b.count(CC, c + 1))
                    wait(act, hl_ready, b.count(CC, c - 1))
                    for i in range(2):
                        ins = act.activation(h32[:, c % 2, i * L:(i + 1) * L], psT[c % 2][:, i * L:(i + 1) * L], ACT.Identity,
                                             bias=mod[:, b.par, i, CC + c:CC + c + 1], scale=mod[:, b.par, i, c:c + 1])
                    ins.then_inc(h32_ready, 1)
                    if c == 0:
                        wait(act, up_ready, (b - 1).count(NJ, NJ))
                    act.wait_ge(h32_ready, b.count(CC, c + 1))
                    act.activation(hh[:, c, :], h32[:, c % 2, :], ACT.Copy).then_inc(hh_ready, 1)

                def body(b):
                    for s in range(NJ):
                        bb, j = chunk(b, s, ACT_LAG)
                        if bb.live(NB):
                            gelu(bb, j)
                        if s == NJ - 1 and (b + 1).live(NB):
                            for c in range(CC):
                                modulate(b + 1, c)

                over_blocks(act, body)

            @block.tensor
            def _(pe):
                pe.wait_ge(consts_loaded, 48)

                def transposes_h(b, c):
                    if c == 0:
                        pe.wait_ge(xn_ready, b.count(TT, TT))
                    wait(pe, h32_ready, b.count(CC, c - 1))
                    for t in range(TT):
                        last = pe.transpose(psT[c % 2][:, t * P:(t + 1) * P], xn[:, t, c * P:(c + 1) * P], ident[:, :])
                    last.then_inc(hT_ready, 1)

                def up(b, j):
                    wait(pe, act_ready, b.count(NJ, j - 1))
                    for k in range(CC):
                        if j == 0:
                            pe.wait_ge(hl_ready, b.count(CC, k + 1))
                        last = split_products(pe, psU[j % 2][:, :], [w[:, k, j * P:(j + 1) * P] for w in W1],
                                              (hh[:, k, :], hl[:, k, :]), k == 0, k == CC - 1)
                    last.then_inc(up_ready, 1)

                def down(b, j):
                    pe.wait_ge(ul_ready, b.count(NJ, j + 1))
                    for t in range(TT):
                        if j == 0:
                            wait(pe, y_bias, (b - 1).count(TT, t + 1))
                        last = split_products(pe, psD[t][:, :], (uh[:, j % 4, t * P:(t + 1) * P], ul[:, j % 4, t * P:(t + 1) * P]),
                                              [w[:, j, :] for w in W2], j == 0, j == NJ - 1)
                    last.then_inc(down_ready, 1)

                def body(b):
                    for s in range(NJ):
                        if b.live(NB):
                            up(b, s)
                        bb, j = chunk(b, s, DOWN)
                        if bb.live(NB):
                            down(bb, j)
                        pieces(b + 1, s, transposes_h, HT_AT)

                over_blocks(pe, body)

            @block.vector
            def _(dve):
                dve.wait_ge(consts_loaded, 48)

                def layer_norm(b, t):
                    dve.wait_ge(x_loaded[t % 2], b.count(32, 16 * (t // 2 + 1)))
                    x = xin[:, t % 2, :]
                    dve.bn_stats(stats[:, :], x).then_inc(stats_ready, 1)
                    dve.wait_ge(stats_ready, b.count(TT, t + 1))
                    dve.memset(spacer[:, :], 0.0)
                    dve.bn_aggr(mv[:, :], stats[:, :]).then_inc(mean_ready, 1)
                    dve.wait_ge(mean_ready, b.count(TT, t + 1))
                    dve.tensor_scalar(var[:, :], mv[:, 1:2], LN_EPS, None, ALU.add).then_inc(var_ready, 1)
                    if t == 0:
                        wait(dve, hT_ready, (b - 1).count(CC, CC))
                    dve.wait_ge(rstd_ready, b.count(TT, t + 1))
                    dve.tensor_scalar(xn[:, t, :], x, mv[:, 0:1], rstd[:, 0:1], ALU.subtract, ALU.mult).then_inc(xn_ready, 1)

                def low_h(b, c):
                    dve.wait_ge(hh_ready, b.count(CC, c + 1))
                    dve.tensor_tensor(hl[:, c, :], h32[:, c % 2, :], hh[:, c, :].bitcast(F32), ALU.subtract).then_inc(hl_ready, 1)

                def low_u(b, j):
                    dve.wait_ge(uh_ready, b.count(NJ, j + 1))
                    dve.tensor_tensor(ul[:, j % 4, :], act32[:, j % 2, :], uh[:, j % 4, :].bitcast(F32), ALU.subtract).then_inc(ul_ready, 1)

                def add_bias(b, t):
                    dve.wait_ge(down_ready, b.count(NJ, NJ))
                    wait(dve, stored[t], b.count(16, 0))
                    dve.tensor_tensor(y[:, t, :], psD[t][:, :], b2[:, :], ALU.add).then_inc(y_bias, 1)

                def body(b):
                    for s in range(NJ):
                        if s == OUT_AT and (b - 1).live(NB):
                            for t in range(TT):
                                add_bias(b - 1, t)
                        bb, j = chunk(b, s, ACT_LAG)
                        if bb.live(NB):
                            low_u(bb, j)
                        pieces(b + 1, s, layer_norm, LN_AT)
                        if s == NJ - 1 and (b + 1).live(NB):
                            for c in range(CC):
                                low_h(b + 1, c)

                over_blocks(dve, body)


def attention_l1(nc, io, scratch):
    with ExitStack() as ctx:
        def sb(name, shape, dt=F32):
            return ctx.enter_context(nc.sbuf_tensor("a1_" + name, shape, dt))

        def pb(name, shape):
            return ctx.enter_context(nc.psum_tensor("a1_" + name, shape, F32))

        sem = ctx.enter_context(semaphores(nc, "a1"))

        G = 2
        NG = H1 // G
        KV = 2 * D1
        NQ = C + KV
        HK = H1 + 1
        SCALE = float(D1) ** -0.5
        wqkv = [sb(f"wqkv{i}", [P, CC * NQ], F32R) for i in range(2)]
        wo = [sb(f"wo{i}", [P, CC * C], F32R) for i in range(2)]
        load_split_weights(nc, sem, [(io["Wqkv1T"], wqkv[0], wqkv[1]), (io["WoT"], wo[0], wo[1])])
        W = [w[:, :].rearrange("p (k n) -> p k n", k=CC) for w in wqkv]
        WO = [w[:, :].rearrange("p (k n) -> p k n", k=CC) for w in wo]

        xin = sb("xin", [P, 2, TB, C])
        xres = sb("xres", [P, TB, C])
        mod = sb("mod", [P, 2, CC])
        rope = sb("rope", [P, 2, TB, 2, D1 // 2])
        xn = sb("xn", [P, TB, C])
        h32 = sb("h32", [P, CC, L])
        hh = sb("hh", [P, CC, L], F32R)
        hl = sb("hl", [P, CC, L], F32R)
        raw = sb("raw", [P, TB, HK + 1, 2, D1 // 2])
        by_cos = sb("by_cos", [P, TB, HK, 2, D1 // 2])
        by_sin = sb("by_sin", [P, TB, HK, 2, D1 // 2])
        qs = sb("qs", [P, 2, TB, H1, 2, D1], F32R)
        ks = sb("ks", [P, TB, 2, 2, D1], F32R)
        vh = sb("vh", [P, 2, TB, G, P], F32R)
        vl = sb("vl", [P, 2, TB, G, P], F32R)
        qT = sb("qT", [P, 2, G, L], F32R)
        kT = sb("kT", [P, 2, 2, L], F32R)
        prob = sb("prob", [P, 4, TB, L])
        pTh = sb("pTh", [P, 2, TB, L], F32R)
        pTl = sb("pTl", [P, 2, TB, L], F32R)
        rdT = sb("rdT", [P, L])
        o32 = sb("o32", [P, L])
        oTh = sb("oTh", [P, 2, NG, L], F32R)
        oTl = sb("oTl", [P, 2, NG, L], F32R)
        y = sb("y", [P, TB, C])
        ident = sb("ident", [P, P])
        minus_half = sb("minus_half", [P, 1])
        spacer = sb("spacer", [P, 1])
        stats, mv, square = sb("stats", [P, 6]), sb("mv", [P, 2]), sb("square", [P, 1])
        var, rstd = sb("var", [P, 1]), sb("rstd", [P, 1])
        rmax = sb("rmax", [P, 4, TB])
        nmax = sb("nmax", [P, 4, TB])
        den = sb("den", [P, 2, TB, G])
        rd = sb("rd", [P, TB, G])
        rden = sb("rden", [P, 2, TB, G * D1])

        psT = pb("psT", [P, G, L])
        psF = pb("psF", [P, C])
        psS = [pb(f"psS{i}", [P, TB, L]) for i in range(2)]
        psP = [pb(f"psP{i}", [P, TB, L]) for i in range(2)]
        psO = [pb(f"psO{i}", [P, 2, L]) for i in range(2)]

        consts_loaded, const_ready = sem("consts_loaded"), sem("const_ready")
        x_loaded = [sem(f"x_loaded{i}") for i in range(2)]
        mod_loaded = [sem(f"mod_loaded{i}") for i in range(2)]
        rope_loaded = [sem(f"rope_loaded{i}") for i in range(2)]
        res_loaded = [sem(f"res_loaded{i}") for i in range(TB)]
        stored = [sem(f"stored{i}") for i in range(TB)]
        stats_ready, mean_ready, square_ready, var_ready = sem("stats"), sem("mean"), sem("square"), sem("var")
        rstd_ready, xn_ready = sem("rstd"), sem("xn")
        hT_ready, h32_ready, hh_ready, hl_ready = sem("hT"), sem("h32"), sem("hh"), sem("hl")
        q_ready, kv_ready, q_taken, kv_taken = sem("q_ready"), sem("kv_ready"), sem("q_taken"), sem("kv_taken")
        vh_ready, vl_ready = sem("vh"), sem("vl")
        sin_ready, rot_ready, high_ready, low_ready = sem("sin"), sem("rot"), sem("high"), sem("low")
        kT_ready, kT_taken = sem("kT_ready"), sem("kT_taken")
        t_ready, t_taken = sem("t_ready"), [sem("t_taken_act"), sem("t_taken_dve")]
        s_ready, rmax_ready, max_ready, exp_ready = sem("s_ready"), sem("rmax"), sem("max_ready"), sem("exp_ready")
        p_ready, pTh_ready, pTl_ready, pv_ready = sem("p_ready"), sem("pTh"), sem("pTl"), sem("pv")
        rden_ready, rdp_ready, rdT_ready = sem("rden"), sem("rdp"), sem("rdT")
        rd_ready = sem("rd")
        o32_ready, oTh_ready, oTl_ready = sem("o32"), sem("oTh"), sem("oTl")
        proj_ready, y_ready = sem("proj"), sem("y_ready")

        LN_AT = {5: 0, 6: 1}
        HT_EARLY, HT_LATE = {0: 0}, {0: 1}
        Q_LATE, KV_EARLY = {1: 0, 2: 1}, {2: 0, 3: 1}
        ANGLES_LATE, SPLIT_EARLY = {2: 0, 3: 1}, {3: 0, 4: 1}
        KT_EARLY, V_LATE = {6: 0}, {5: 0}
        PROJ_LATE = {6: 0, 7: 1}
        SCORES, EXP, PT, SPLIT, VALUES, OUT, OUT_SPLIT = 1, 2, 3, 4, 5, 6, 7

        def head(b, s, lag):
            return (b, s - lag) if s >= lag else (b - 1, H1 + s - lag)

        def pieces(b, s, fn, table):
            if s in table and b.live():
                fn(b, table[s])

        def stage(b, s, lag, fn):
            bb, h = head(b, s, lag)
            if bb.live():
                fn(bb, h)

        def group_stage(b, s, lag, fn):
            bb, h = head(b, s, lag)
            if bb.live() and h % G == G - 1:
                fn(bb, h // G)

        def v_place(tile, b, j):
            return tile[:, b.par, :, j, j * D1:(j + 1) * D1]

        v_rows = raw[:, :, HK, :, :].rearrange("p t i f -> p t (i f)")

        with nc.Block() as block:
            @block.sync
            def _(sp):
                sp.dma_start(ident[:, :], io["ident"]).then_inc(consts_loaded, 16)

                def load_front(b):
                    wait(sp, xn_ready, (b - 2).count(TB, TB))
                    sp.dma_start(xin[:, b.par, :, :], scratch["x2"][bass.ds(b.value() * L, L), :].rearrange("(t p) c -> p t c", p=P))\
                      .then_inc(x_loaded[b.par], 16)
                    wait(sp, h32_ready, (b - 2).count(CC, CC))
                    sp.dma_start(mod[:, b.par, :], scratch["mod1"][0, :, bass.ds(b.value(), 1), :].rearrange("p b s -> p (b s)"))\
                      .then_inc(mod_loaded[b.par], 16)
                    wait(sp, sin_ready, (b - 2).count(TB, TB))
                    sp.dma_start(rope[:, b.par, :, :, :].rearrange("p t s f -> p t (s f)"),
                                 scratch["rope"][:, bass.ds(b.value() * TB, TB), :]).then_inc(rope_loaded[b.par], 16)

                def back(b):
                    for t in range(TB):
                        wait(sp, y_ready, (b - 1).count(TB, t + 1))
                        sp.dma_start(xres[:, t, :], scratch["x2"][bass.ds(b.value() * L + t * P, P), :]).then_inc(res_loaded[t], 16)
                    for t in range(TB):
                        wait(sp, y_ready, b.count(TB, t + 1))
                        sp.dma_start(scratch["x3"][bass.ds(b.value() * L + t * P, P), :], y[:, t, :]).then_inc(stored[t], 16)

                def body(b):
                    if (b + 2).live():
                        load_front(b + 2)
                    if (b - 1).live():
                        back(b - 1)

                over_batches(sp, body)
                for t in range(TB):
                    sp.wait_ge(stored[t], 16 * B)

            @block.gpsimd
            def _(pool):
                pool.memset(minus_half[:, :], -0.5).then_inc(const_ready, 1)
                pool.memset(vh[:, :, :, :, :].bitcast(F32), 0.0).then_inc(const_ready, 1)
                pool.memset(vl[:, :, :, :, :].bitcast(F32), 0.0).then_inc(const_ready, 1)
                pool.wait_ge(const_ready, 3)

                def root_mean_square(b, t):
                    pool.wait_ge(var_ready, b.count(TB, t + 1))
                    pool.tensor_tensor(rstd[:, :], var[:, :], minus_half[:, :], ALU.pow).then_inc(rstd_ready, 1)

                def rotate(b, t):
                    pool.wait_ge(sin_ready, b.count(TB, t + 1))
                    pool.tensor_tensor(by_cos[:, t, :, 0, :], by_cos[:, t, :, 0, :], by_sin[:, t, :, 0, :], ALU.subtract)
                    pool.tensor_tensor(by_cos[:, t, :, 1, :], by_cos[:, t, :, 1, :], by_sin[:, t, :, 1, :], ALU.add)\
                        .then_inc(rot_ready, 1)

                def low(b, t):
                    pool.wait_ge(high_ready, b.count(TB, t + 1))
                    rot = by_cos[:, t, :, :, :].rearrange("p h i f -> p h (i f)")
                    pool.tensor_tensor(qs[:, b.par, t, :, 1, :], rot[:, 0:H1, :], qs[:, b.par, t, :, 0, :].bitcast(F32), ALU.subtract)
                    pool.tensor_tensor(ks[:, t, 1, :, :], rot[:, H1:HK, :].to_broadcast([P, 2, D1]),
                                       ks[:, t, 0, :, :].bitcast(F32), ALU.subtract).then_inc(low_ready, 1)

                def body(b):
                    for s in range(H1):
                        pieces(b + 1, s, low, SPLIT_EARLY)
                        pieces(b + 1, s, rotate, ANGLES_LATE)
                        pieces(b + 2, s, root_mean_square, LN_AT)

                over_batches(pool, body)

            @block.scalar
            def _(act):
                act.wait_ge(const_ready, 3)

                def modulate(b, pair):
                    if pair == 0:
                        act.wait_ge(mod_loaded[b.par], b.half * 16 + 16)
                        wait(act, hl_ready, (b - 1).count(CC, CC))
                    act.wait_ge(hT_ready, b.count(2, pair + 1))
                    for i in range(2):
                        c = 2 * pair + i
                        act.activation(h32[:, c, :], psF[:, i * L:(i + 1) * L], ACT.Copy, scale=mod[:, b.par, c:c + 1])\
                           .then_inc(h32_ready, 1)
                    if pair == 0:
                        wait(act, kv_ready, (b - 1).count(TB, TB))
                    for i in range(2):
                        c = 2 * pair + i
                        act.wait_ge(h32_ready, b.count(CC, c + 1))
                        act.activation(hh[:, c, :], h32[:, c, :], ACT.Copy).then_inc(hh_ready, 1)

                def take_q(b, t):
                    act.wait_ge(q_ready, b.count(TB, t + 1))
                    wait(act, sin_ready, (b - 1).count(TB, t + 1))
                    act.activation(raw[:, t, 0:H1, :, :].rearrange("p h i f -> p (h i f)"), psF[:, :], ACT.Copy).then_inc(q_taken, 1)

                def take_kv(b, t):
                    act.wait_ge(kv_ready, b.count(TB, t + 1))
                    wait(act, vl_ready, (b - 1).count(1, 1))
                    act.activation(raw[:, t, H1:HK + 1, :, :].rearrange("p h i f -> p (h i f)"), psF[:, 0:KV], ACT.Copy)\
                       .then_inc(kv_taken, 1)

                def values_high(b, _):
                    wait(act, pv_ready, (b - 2).count(H1, H1))
                    act.wait_ge(kv_taken, b.count(TB, TB))
                    for j in range(G):
                        ins = act.activation(v_place(vh, b, j), v_rows, ACT.Copy)
                    ins.then_inc(vh_ready, 1)

                def high(b, t):
                    act.wait_ge(rot_ready, b.count(TB, t + 1))
                    wait(act, t_ready, (b - 2).count(NG, NG))
                    wait(act, kT_ready, (b - 1).count(1, 1))
                    rot = by_cos[:, t, :, :, :].rearrange("p h i f -> p h (i f)")
                    act.activation(qs[:, b.par, t, :, 0, :], rot[:, 0:H1, :], ACT.Copy)
                    act.activation(ks[:, t, 0, :, :], rot[:, H1:HK, :].to_broadcast([P, 2, D1]), ACT.Copy).then_inc(high_ready, 1)

                def take_kT(b, _):
                    act.wait_ge(kT_ready, b.count(1, 1))
                    wait(act, s_ready, (b - 1).count(H1, 0))
                    act.activation(kT[:, b.par, :, :].rearrange("p s l -> p (s l)"), psF[:, :], ACT.Copy).then_inc(kT_taken, 1)

                def take_qT(b, g):
                    act.wait_ge(t_ready, b.count(NG, g + 1))
                    wait(act, s_ready, b.count(H1, (g - 1) * G))
                    act.activation(qT[:, g % 2, :, :], psT[:, :, :], ACT.Copy).then_inc(t_taken[0], 1)

                def softmax(b, h):
                    g, j = h // G, h % G
                    act.wait_ge(max_ready, b.count(H1, h + 1))
                    wait(act, p_ready, b.count(H1, h - 3))
                    if j == 0:
                        wait(act, rden_ready, b.count(NG, g - 1))
                    for qc in range(TB):
                        ins = act.activation(prob[:, h % 4, qc, :], psS[h % 2][:, qc, :], ACT.Exp, scale=SCALE,
                                             bias=nmax[:, h % 4, qc:qc + 1], accum_out=den[:, g % 2, qc, j:j + 1])
                    ins.then_inc(exp_ready, 1)

                def probs_high(b, h):
                    act.wait_ge(p_ready, b.count(H1, h + 1))
                    wait(act, pv_ready, b.count(H1, h - 1))
                    act.activation(pTh[:, h % 2, :, :], psP[h % 2][:, :, :], ACT.Copy).then_inc(pTh_ready, 1)

                def take_denominators(b, g):
                    act.wait_ge(rdp_ready, b.count(NG, g + 1))
                    wait(act, o32_ready, b.count(NG, g))
                    act.activation(rdT[:, :], psO[g % 2][:, 1, :], ACT.Copy).then_inc(rdT_ready, 1)

                def output_high(b, g):
                    act.wait_ge(o32_ready, b.count(NG, g + 1))
                    if g == 0:
                        wait(act, proj_ready, (b - 2).count(TB, TB))
                    act.activation(oTh[:, b.par, g, :], o32[:, :], ACT.Copy).then_inc(oTh_ready, 1)

                def body(b):
                    for s in range(H1):
                        group_stage(b, s, OUT_SPLIT, output_high)
                        group_stage(b, s, OUT, take_denominators)
                        stage(b, s, SPLIT, probs_high)
                        pieces(b + 1, s, modulate, HT_EARLY)
                        pieces(b + 1, s, take_kv, KV_EARLY)
                        pieces(b + 1, s, take_kT, KT_EARLY)
                        pieces(b + 1, s, high, SPLIT_EARLY)
                        stage(b, s, EXP, softmax)
                        if b.live() and s % 4 == 0:
                            take_qT(b, s // G)
                        pieces(b + 1, s, values_high, V_LATE)
                        pieces(b + 1, s, modulate, HT_LATE)
                        pieces(b + 1, s, take_q, Q_LATE)

                over_batches(act, body)

            @block.tensor
            def _(pe):
                pe.wait_ge(consts_loaded, 16)

                def transposes_h(b, pair):
                    if pair == 0:
                        pe.wait_ge(xn_ready, b.count(TB, TB))
                        if (b - 3).live():
                            pe.wait_ge(y_ready, (b - 3).count(TB, TB))
                        else:
                            wait(pe, kT_taken, (b - 1).count(1, 1))
                    else:
                        pe.wait_ge(h32_ready, b.count(CC, 2))
                    for i in range(2):
                        for t in range(TB):
                            c = 2 * pair + i
                            last = pe.transpose(psF[:, i * L + t * P:i * L + (t + 1) * P], xn[:, t, c * P:(c + 1) * P], ident[:, :])
                    last.then_inc(hT_ready, 1)

                def project_q(b, t):
                    if t == 0:
                        pe.wait_ge(hl_ready, b.count(CC, CC))
                    else:
                        pe.wait_ge(kv_taken, b.count(TB, t))
                    for k in range(CC):
                        last = split_products(pe, psF[:, :], (hh[:, k, t * P:(t + 1) * P], hl[:, k, t * P:(t + 1) * P]),
                                              [w[:, k, 0:C] for w in W], k == 0, k == CC - 1)
                    last.then_inc(q_ready, 1)

                def project_kv(b, t):
                    pe.wait_ge(q_taken, b.count(TB, t + 1))
                    for k in range(CC):
                        last = split_products(pe, psF[:, 0:KV], (hh[:, k, t * P:(t + 1) * P], hl[:, k, t * P:(t + 1) * P]),
                                              [w[:, k, C:NQ] for w in W], k == 0, k == CC - 1)
                    last.then_inc(kv_ready, 1)

                def transposes_k(b, _):
                    pe.wait_ge(low_ready, b.count(TB, TB))
                    pe.wait_ge(kv_taken, b.count(TB, TB))
                    for i in range(2):
                        for t in range(TB):
                            last = pe.transpose(psF[:, i * L + t * P:i * L + (t + 1) * P],
                                                ks[:, t, i, :, :].rearrange("p r d -> p (r d)").bitcast(F32), ident[:, :])
                    last.then_inc(kT_ready, 1)

                def transposes_q(b, g):
                    if g == 0:
                        pe.wait_ge(low_ready, b.count(TB, TB))
                    wait(pe, t_taken[(g - 1) % 2], b.count(NG // 2, (g + 1) // 2))
                    for j in range(G):
                        for t in range(TB):
                            last = pe.transpose(psT[:, j, t * P:(t + 1) * P],
                                                qs[:, b.par, t, g * G + j, :, :].rearrange("p s d -> p (s d)").bitcast(F32), ident[:, :])
                    last.then_inc(t_ready, 1)

                def scores(b, h):
                    g, j = h // G, h % G
                    if h == 0:
                        pe.wait_ge(kT_taken, b.count(1, 1))
                    pe.wait_ge(t_taken[g % 2], b.count(NG // 2, g // 2 + 1))
                    wait(pe, exp_ready, b.count(H1, h - 1))
                    for qc in range(TB):
                        for i in range(2):
                            last = pe.matmul(psS[h % 2][:, qc, :], qT[:, g % 2, j, qc * P:(qc + 1) * P], kT[:, b.par, i, :],
                                             start=(i == 0), stop=(i == 1))
                    last.then_inc(s_ready, 1)

                def transposes_p(b, h):
                    pe.wait_ge(exp_ready, b.count(H1, h + 1))
                    wait(pe, pTl_ready, b.count(H1, h - 1))
                    for kc in range(TB):
                        for qc in range(TB):
                            last = pe.transpose(psP[h % 2][:, kc, qc * P:(qc + 1) * P], prob[:, h % 4, qc, kc * P:(kc + 1) * P],
                                                ident[:, :])
                    last.then_inc(p_ready, 1)

                def values(b, h):
                    g, j = h // G, h % G
                    if j == 0:
                        pe.wait_ge(vl_ready, b.count(1, 1))
                        wait(pe, o32_ready, b.count(NG, g - 1))
                    pe.wait_ge(pTl_ready, b.count(H1, h + 1))
                    for kc in range(TB):
                        last = split_products(pe, psO[g % 2][:, 0, :], (vh[:, b.par, kc, j, :], vl[:, b.par, kc, j, :]),
                                              (pTh[:, h % 2, kc, :], pTl[:, h % 2, kc, :]),
                                              j == 0 and kc == 0, j == G - 1 and kc == TB - 1)
                    last.then_inc(pv_ready, 1)
                    if j == G - 1:
                        pe.wait_ge(rden_ready, b.count(NG, g + 1))
                        for qc in range(TB):
                            last = pe.transpose(psO[g % 2][:, 1, qc * P:(qc + 1) * P], rden[:, g % 2, qc, :], ident[:, :])
                        last.then_inc(rdp_ready, 1)

                def project_out(b, t):
                    nxt = b + 2
                    if t == 0:
                        pe.wait_ge(oTl_ready, b.count(NG, NG))
                        if nxt.live():
                            pe.wait_ge(kT_taken, nxt.count(1, 1))
                        else:
                            pe.wait_ge(y_ready, (b - 1).count(TB, TB))
                    else:
                        pe.wait_ge(y_ready, b.count(TB, 1))
                    for g in range(NG):
                        last = split_products(pe, psF[:, :], (oTh[:, b.par, g, t * P:(t + 1) * P], oTl[:, b.par, g, t * P:(t + 1) * P]),
                                              [w[:, g, :] for w in WO], g == 0, g == NG - 1)
                    last.then_inc(proj_ready, 1)

                def body(b):
                    for s in range(H1):
                        stage(b, s, VALUES, values)
                        pieces(b + 1, s, transposes_h, HT_EARLY)
                        pieces(b + 1, s, project_kv, KV_EARLY)
                        pieces(b + 1, s, transposes_k, KT_EARLY)
                        stage(b, s, PT, transposes_p)
                        stage(b, s, SCORES, scores)
                        if b.live() and s % 2 == 0:
                            transposes_q(b, s // G)
                        pieces(b + 1, s, transposes_h, HT_LATE)
                        pieces(b + 1, s, project_q, Q_LATE)
                        pieces(b - 1, s, project_out, PROJ_LATE)

                over_batches(pe, body)

            @block.vector
            def _(dve):
                dve.wait_ge(const_ready, 3)

                def root_mean_square(b, t):
                    if t == 0:
                        dve.wait_ge(x_loaded[b.par], b.half * 16 + 16)
                    x = xin[:, b.par, t, :]
                    dve.bn_stats(stats[:, :], x).then_inc(stats_ready, 1)
                    dve.wait_ge(stats_ready, b.count(TB, t + 1))
                    dve.memset(spacer[:, :], 0.0)
                    dve.bn_aggr(mv[:, :], stats[:, :]).then_inc(mean_ready, 1)
                    dve.wait_ge(mean_ready, b.count(TB, t + 1))
                    dve.tensor_tensor(square[:, :], mv[:, 0:1], mv[:, 0:1], ALU.mult).then_inc(square_ready, 1)
                    dve.wait_ge(square_ready, b.count(TB, t + 1))
                    dve.tensor_scalar(var[:, :], square[:, :], mv[:, 1:2], RMS_EPS, ALU.add, ALU.add).then_inc(var_ready, 1)
                    if t == 0:
                        wait(dve, hT_ready, (b - 1).count(2, 2))
                    dve.wait_ge(rstd_ready, b.count(TB, t + 1))
                    dve.tensor_scalar(xn[:, t, :], x, rstd[:, 0:1], None, ALU.mult).then_inc(xn_ready, 1)

                def low_h(b, pair):
                    for i in range(2):
                        c = 2 * pair + i
                        dve.wait_ge(hh_ready, b.count(CC, c + 1))
                        dve.tensor_tensor(hl[:, c, :], h32[:, c, :], hh[:, c, :].bitcast(F32), ALU.subtract).then_inc(hl_ready, 1)

                def values_low(b, _):
                    dve.wait_ge(vh_ready, b.count(1, 1))
                    for j in range(G):
                        ins = dve.tensor_tensor(v_place(vl, b, j), v_rows, v_place(vh, b, j).bitcast(F32), ALU.subtract)
                    ins.then_inc(vl_ready, 1)

                def by_angles(b, t):
                    if t == 0:
                        dve.wait_ge(rope_loaded[b.par], b.half * 16 + 16)
                    dve.wait_ge(kv_taken, b.count(TB, t + 1))
                    wait(dve, low_ready, (b - 1).count(TB, t + 1))
                    cos = rope[:, b.par, t, 0, :].unsqueeze(1).to_broadcast([P, 2 * HK, D1 // 2])
                    sin = rope[:, b.par, t, 1, :].unsqueeze(1).to_broadcast([P, HK, D1 // 2])
                    dve.tensor_tensor(by_cos[:, t, :, :, :].rearrange("p h i f -> p (h i) f"),
                                      raw[:, t, 0:HK, :, :].rearrange("p h i f -> p (h i) f"), cos, ALU.mult)
                    for i in range(2):
                        ins = dve.tensor_tensor(by_sin[:, t, :, i, :], raw[:, t, 0:HK, 1 - i, :], sin, ALU.mult)
                    ins.then_inc(sin_ready, 1)

                def take_qT(b, g):
                    dve.wait_ge(t_ready, b.count(NG, g + 1))
                    wait(dve, s_ready, b.count(H1, (g - 1) * G))
                    dve.tensor_copy(qT[:, g % 2, :, :], psT[:, :, :]).then_inc(t_taken[1], 1)

                def score_max(b, h):
                    dve.wait_ge(s_ready, b.count(H1, h + 1))
                    dve.tensor_reduce(rmax[:, h % 4, :], psS[h % 2][:, :, :], AX, ALU.max).then_inc(rmax_ready, 1)
                    dve.wait_ge(rmax_ready, b.count(H1, h + 1))
                    dve.tensor_scalar(nmax[:, h % 4, :], rmax[:, h % 4, :], -SCALE, None, ALU.mult).then_inc(max_ready, 1)

                def probs_low(b, h):
                    dve.wait_ge(pTh_ready, b.count(H1, h + 1))
                    dve.tensor_tensor(pTl[:, h % 2, :, :], psP[h % 2][:, :, :], pTh[:, h % 2, :, :].bitcast(F32), ALU.subtract)\
                       .then_inc(pTl_ready, 1)

                def denominators(b, g):
                    dve.wait_ge(exp_ready, b.count(H1, (g + 1) * G))
                    wait(dve, rdp_ready, b.count(NG, g - 1))
                    dve.reciprocal(rd[:, :, :], den[:, g % 2, :, :]).then_inc(rd_ready, 1)
                    dve.wait_ge(rd_ready, b.count(NG, g + 1))
                    dve.tensor_copy(rden[:, g % 2, :, :].rearrange("p q (j d) -> p q j d", j=G),
                                    rd[:, :, :].unsqueeze(3).to_broadcast([P, TB, G, D1])).then_inc(rden_ready, 1)

                def group_output(b, g):
                    dve.wait_ge(rdT_ready, b.count(NG, g + 1))
                    wait(dve, oTl_ready, b.count(NG, g))
                    dve.tensor_tensor(o32[:, :], psO[g % 2][:, 0, :], rdT[:, :], ALU.mult).then_inc(o32_ready, 1)

                def output_low(b, g):
                    dve.wait_ge(oTh_ready, b.count(NG, g + 1))
                    dve.tensor_tensor(oTl[:, b.par, g, :], o32[:, :], oTh[:, b.par, g, :].bitcast(F32), ALU.subtract)\
                       .then_inc(oTl_ready, 1)

                def residual(b, t):
                    dve.wait_ge(proj_ready, b.count(TB, t + 1))
                    dve.wait_ge(res_loaded[t], b.count(16, 16))
                    wait(dve, stored[t], b.count(16, 0))
                    dve.tensor_tensor(y[:, t, :], psF[:, :], xres[:, t, :], ALU.add).then_inc(y_ready, 1)

                def body(b):
                    for s in range(H1):
                        group_stage(b, s, OUT_SPLIT, output_low)
                        group_stage(b, s, OUT, group_output)
                        stage(b, s, SPLIT, probs_low)
                        pieces(b + 1, s, low_h, HT_EARLY)
                        stage(b, s, SCORES, score_max)
                        group_stage(b, s, PT, denominators)
                        if b.live() and s % 4 == 2:
                            take_qT(b, s // G)
                        pieces(b + 1, s, by_angles, ANGLES_LATE)
                        pieces(b + 2, s, root_mean_square, LN_AT)
                        pieces(b + 1, s, low_h, HT_LATE)
                        pieces(b + 1, s, values_low, V_LATE)
                        pieces(b - 1, s, residual, PROJ_LATE)

                over_batches(dve, body)


def mlp_l1(nc, io, scratch):
    for half in range(2):
        mlp_l1_half(nc, io, scratch, half)


def mlp_l1_half(nc, io, scratch, half):
    x_in, res_in, x_out = scratch["x3"], scratch[("x3", "x3h")[half]], scratch[("x3h", "x4")[half]]
    with ExitStack() as ctx:
        def sb(name, shape, dt=F32):
            return ctx.enter_context(nc.sbuf_tensor(f"m1_{half}_{name}", shape, dt))

        def pb(name, shape):
            return ctx.enter_context(nc.psum_tensor(f"m1_{half}_{name}", shape, F32))

        sem = ctx.enter_context(semaphores(nc, f"m1_{half}"))

        NH = HID // 2
        NJ = NH // P
        TT = 2 * TB
        T = TT * P
        NB = B // 2
        DOWN = 2
        wg = [sb(f"wg{i}", [P, CC * NH], F32R) for i in range(2)]
        wu = [sb(f"wu{i}", [P, CC * NH], F32R) for i in range(2)]
        wd = [sb(f"wd{i}", [P, NJ * C], F32R) for i in range(2)]
        load_split_weights(nc, sem, [(io[f"WgT{half}"], wg[0], wg[1]), (io[f"WuT{half}"], wu[0], wu[1]),
                                (io[f"WdT{half}"], wd[0], wd[1])])
        WG = [w[:, :].rearrange("p (k n) -> p k n", k=CC) for w in wg]
        WU = [w[:, :].rearrange("p (k n) -> p k n", k=CC) for w in wu]
        WD = [w[:, :].rearrange("p (k n) -> p k n", k=NJ) for w in wd]

        xin = sb("xin", [P, 2, C])
        xres = sb("xres", [P, TT, C])
        y = sb("y", [P, TT, C])
        mod = sb("mod", [P, 2, 2, CC])
        ident = sb("ident", [P, P])
        minus_half = sb("minus_half", [P, 1])
        xn = sb("xn", [P, TT, C])
        h32 = sb("h32", [P, 2, T])
        hh = sb("hh", [P, 2, CC, T], F32R)
        hl = sb("hl", [P, 2, CC, T], F32R)
        gate = sb("gate", [P, 2, T])
        u32 = sb("u32", [P, 2, T])
        uh = sb("uh", [P, 4, T], F32R)
        ul = sb("ul", [P, 4, T], F32R)
        spacer = sb("spacer", [P, 1])
        stats, mv, square = sb("stats", [P, 6]), sb("mv", [P, 2]), sb("square", [P, 1])
        var, rstd = sb("var", [P, 1]), sb("rstd", [P, 1])

        psT = [pb(f"psT{i}", [P, T]) for i in range(2)]
        psG, psU = pb("psG", [P, T]), pb("psU", [P, T])
        psD = [pb(f"psD{i}", [P, C]) for i in range(TT)]

        consts_loaded, const_ready = sem("consts_loaded"), sem("const_ready")
        x_loaded = [sem(f"x_loaded{i}") for i in range(2)]
        res_loaded = [sem(f"res_loaded{i}") for i in range(TT)]
        stored = [sem(f"stored{i}") for i in range(TT)]
        mod_loaded = [sem(f"mod_loaded{i}") for i in range(2)]
        stats_ready, mean_ready, square_ready, var_ready = sem("stats"), sem("mean"), sem("square"), sem("var")
        rstd_ready, xn_ready = sem("rstd"), sem("xn")
        hT_ready, h32_ready, hh_ready, hl_ready = sem("hT"), sem("h32"), sem("hh"), sem("hl")
        g_ready, gate_ready, up_ready, u32_ready = sem("g"), sem("gate"), sem("up"), sem("u32")
        uh_ready, ul_ready, down_ready, y_ready = sem("uh"), sem("ul"), sem("down"), sem("y")

        LN_AT = {2: (0,), 3: (1,), 4: (2,), 5: (3,)}
        HT_AT = {6: (0, 1), 7: (2, 3)}
        OUT_AT = DOWN

        def pieces(b, s, fn, table):
            if s in table and b.live(NB):
                for t in table[s]:
                    fn(b, t)

        with nc.Block() as block:
            @block.sync
            def _(sp):
                sp.dma_start(ident[:, :], io["ident"]).then_inc(consts_loaded, 16)

                def load_front(b, t):
                    if t == 0:
                        wait(sp, h32_ready, (b - 2).count(CC, CC))
                        sp.dma_start(mod[:, b.par, :, :].rearrange("p b s -> p (b s)"),
                                     scratch["mod1"][1, :, bass.ds(b.value() * 2, 2), :].rearrange("p b s -> p (b s)"))\
                          .then_inc(mod_loaded[b.par], 16)
                    wait(sp, xn_ready, b.count(TT, t - 1))
                    sp.dma_start(xin[:, t % 2, :], x_in[bass.ds((b.value() * TT + t) * P, P), :])\
                      .then_inc(x_loaded[t % 2], 16)

                def load_residual(b, t):
                    wait(sp, y_ready, (b - 1).count(TT, t + 1))
                    sp.dma_start(xres[:, t, :], res_in[bass.ds((b.value() * TT + t) * P, P), :]).then_inc(res_loaded[t], 16)

                def store(b, t):
                    sp.wait_ge(y_ready, b.count(TT, t + 1))
                    sp.dma_start(x_out[bass.ds((b.value() * TT + t) * P, P), :], y[:, t, :]).then_inc(stored[t], 16)

                def body(b):
                    for t in range(TT):
                        if (b - 1).live(NB):
                            load_residual(b - 1, t)
                    for t in range(TT):
                        if (b + 1).live(NB) and t < 2:
                            load_front(b + 1, t)
                    for t in range(TT):
                        if (b - 1).live(NB):
                            store(b - 1, t)
                    for t in range(TT):
                        if (b + 1).live(NB) and t >= 2:
                            load_front(b + 1, t)

                over_blocks(sp, body)
                for t in range(TT):
                    sp.wait_ge(stored[t], 16 * NB)

            @block.gpsimd
            def _(pool):
                pool.memset(minus_half[:, :], -0.5).then_inc(const_ready, 1)
                pool.wait_ge(const_ready, 1)

                def root_mean_square(b, t):
                    pool.wait_ge(var_ready, b.count(TT, t + 1))
                    pool.tensor_tensor(rstd[:, :], var[:, :], minus_half[:, :], ALU.pow).then_inc(rstd_ready, 1)

                def body(b):
                    for s in range(NJ):
                        pieces(b + 1, s, root_mean_square, LN_AT)

                over_blocks(pool, body)

            @block.scalar
            def _(act):
                def silu(b, j):
                    act.wait_ge(g_ready, b.count(NJ, j + 1))
                    wait(act, u32_ready, b.count(NJ, j - 1))
                    act.activation(gate[:, j % 2, :], psG[:, :], ACT.Silu).then_inc(gate_ready, 1)

                def high_u(b, j):
                    act.wait_ge(u32_ready, b.count(NJ, j + 1))
                    wait(act, down_ready, b.count(NJ, j - 3))
                    act.activation(uh[:, j % 4, :], u32[:, j % 2, :], ACT.Copy).then_inc(uh_ready, 1)

                def modulate(b, c):
                    if c == 0:
                        act.wait_ge(mod_loaded[b.par], b.half * 16 + 16)
                        wait(act, up_ready, (b - 2).count(NJ, NJ))
                    act.wait_ge(hT_ready, b.count(CC, c + 1))
                    wait(act, hl_ready, b.count(CC, c - 1))
                    for i in range(2):
                        ins = act.activation(h32[:, c % 2, i * L:(i + 1) * L], psT[c % 2][:, i * L:(i + 1) * L], ACT.Copy,
                                             scale=mod[:, b.par, i, c:c + 1])
                    ins.then_inc(h32_ready, 1)
                    act.wait_ge(h32_ready, b.count(CC, c + 1))
                    act.activation(hh[:, b.par, c, :], h32[:, c % 2, :], ACT.Copy).then_inc(hh_ready, 1)

                def body(b):
                    for s in range(NJ):
                        pieces(b + 1, s, modulate, HT_AT)
                        if b.live(NB):
                            silu(b, s)
                            high_u(b, s)

                over_blocks(act, body)

            @block.tensor
            def _(pe):
                pe.wait_ge(consts_loaded, 16)

                def transposes_h(b, c):
                    if c == 0:
                        pe.wait_ge(xn_ready, b.count(TT, TT))
                    wait(pe, h32_ready, b.count(CC, c - 1))
                    for t in range(TT):
                        last = pe.transpose(psT[c % 2][:, t * P:(t + 1) * P], xn[:, t, c * P:(c + 1) * P], ident[:, :])
                    last.then_inc(hT_ready, 1)

                def hidden(b, j, ps, weight, ready):
                    for k in range(CC):
                        last = split_products(pe, ps[:, :], [w[:, k, j * P:(j + 1) * P] for w in weight],
                                              (hh[:, b.par, k, :], hl[:, b.par, k, :]), k == 0, k == CC - 1)
                    last.then_inc(ready, 1)

                def gate_and_up(b, j):
                    if j == 0:
                        pe.wait_ge(hl_ready, b.count(CC, CC))
                    wait(pe, gate_ready, b.count(NJ, j))
                    hidden(b, j, psG, WG, g_ready)
                    wait(pe, u32_ready, b.count(NJ, j))
                    hidden(b, j, psU, WU, up_ready)

                def down(b, j):
                    pe.wait_ge(ul_ready, b.count(NJ, j + 1))
                    for t in range(TT):
                        if j == 0:
                            wait(pe, y_ready, (b - 1).count(TT, t + 1))
                        last = split_products(pe, psD[t][:, :], (uh[:, j % 4, t * P:(t + 1) * P], ul[:, j % 4, t * P:(t + 1) * P]),
                                              [w[:, j, :] for w in WD], j == 0, j == NJ - 1)
                    last.then_inc(down_ready, 1)

                def body(b):
                    for s in range(NJ):
                        pieces(b + 1, s, transposes_h, HT_AT)
                        if b.live(NB):
                            gate_and_up(b, s)
                        bb, j = (b, s - DOWN) if s >= DOWN else (b - 1, NJ + s - DOWN)
                        if bb.live(NB):
                            down(bb, j)

                over_blocks(pe, body)

            @block.vector
            def _(dve):
                dve.wait_ge(const_ready, 1)

                def root_mean_square(b, t):
                    dve.wait_ge(x_loaded[t % 2], b.count(32, 16 * (t // 2 + 1)))
                    x = xin[:, t % 2, :]
                    dve.bn_stats(stats[:, :], x).then_inc(stats_ready, 1)
                    dve.wait_ge(stats_ready, b.count(TT, t + 1))
                    dve.memset(spacer[:, :], 0.0)
                    dve.bn_aggr(mv[:, :], stats[:, :]).then_inc(mean_ready, 1)
                    dve.wait_ge(mean_ready, b.count(TT, t + 1))
                    dve.tensor_tensor(square[:, :], mv[:, 0:1], mv[:, 0:1], ALU.mult).then_inc(square_ready, 1)
                    dve.wait_ge(square_ready, b.count(TT, t + 1))
                    dve.tensor_scalar(var[:, :], square[:, :], mv[:, 1:2], RMS_EPS, ALU.add, ALU.add).then_inc(var_ready, 1)
                    if t == 0:
                        wait(dve, hT_ready, (b - 1).count(CC, CC))
                    dve.wait_ge(rstd_ready, b.count(TT, t + 1))
                    dve.tensor_scalar(xn[:, t, :], x, rstd[:, 0:1], None, ALU.mult).then_inc(xn_ready, 1)

                def low_h(b, c):
                    dve.wait_ge(hh_ready, b.count(CC, c + 1))
                    dve.tensor_tensor(hl[:, b.par, c, :], h32[:, c % 2, :], hh[:, b.par, c, :].bitcast(F32), ALU.subtract)\
                       .then_inc(hl_ready, 1)

                def product(b, j):
                    dve.wait_ge(gate_ready, b.count(NJ, j + 1))
                    dve.wait_ge(up_ready, b.count(NJ, j + 1))
                    dve.tensor_tensor(u32[:, j % 2, :], psU[:, :], gate[:, j % 2, :], ALU.mult).then_inc(u32_ready, 1)
                    dve.wait_ge(uh_ready, b.count(NJ, j + 1))
                    dve.tensor_tensor(ul[:, j % 4, :], u32[:, j % 2, :], uh[:, j % 4, :].bitcast(F32), ALU.subtract).then_inc(ul_ready, 1)

                def residual(b, t):
                    dve.wait_ge(down_ready, b.count(NJ, NJ))
                    dve.wait_ge(res_loaded[t], b.count(16, 16))
                    wait(dve, stored[t], b.count(16, 0))
                    dve.tensor_tensor(y[:, t, :], psD[t][:, :], xres[:, t, :], ALU.add).then_inc(y_ready, 1)

                def body(b):
                    for s in range(NJ):
                        if s == OUT_AT and (b - 1).live(NB):
                            for t in range(TT):
                                residual(b - 1, t)
                        pieces(b + 1, s, low_h, HT_AT)
                        if b.live(NB):
                            product(b, s)
                        pieces(b + 1, s, root_mean_square, LN_AT)

                over_blocks(dve, body)


def two_layers(nc, io, x4):
    shapes = {"mod0": [2, P, B, 2 * CC], "mod1": [2, P, B, CC], "gamma": [B, 2 * C], "rope": [P, B * TB, D1],
              "x1": [B * L, C], "x2": [B * L, C], "x3": [B * L, C], "x3h": [B * L, C]}
    scratch = {n: nc.dram_tensor(n, shape, F32, kind="Internal").ap() for n, shape in shapes.items()}
    scratch["x4"] = x4
    modulation(nc, io, scratch)
    attention_l0(nc, io, scratch)
    mlp_l0(nc, io, scratch)
    attention_l1(nc, io, scratch)
    mlp_l1(nc, io, scratch)


def by_contraction(w):
    w = np.asarray(w)
    return np.ascontiguousarray(w.T.reshape(w.shape[1] // P, P, w.shape[0]).transpose(1, 0, 2))


def lay_out(a):
    flat = lambda w: by_contraction(w).reshape(P, -1)
    feat = lambda v: np.asarray(v).reshape(-1, P).T
    cont = np.ascontiguousarray
    NH = HID // 2
    halves = {f"W{n}T{i}": by_contraction(a[f"L1_cond_W{n}"])[:, :, i * NH:(i + 1) * NH].reshape(P, -1) for n in "gu" for i in range(2)}
    NK = NH // P
    halves |= {f"WdT{i}": by_contraction(a["L1_cond_Wd"])[:, i * NK:(i + 1) * NK].reshape(P, -1) for i in range(2)}
    return {k: cont(v) for k, v in {
        **halves,
        "x": np.asarray(a["x"]).reshape(B * L, C),
        "condT": flat(a["cond_2048"]),
        "badaF": feat(a["L0_cond_bada"]),
        "lnwF": np.stack([feat(a["L1_cond_ln1_w"]), feat(a["L1_cond_ln2_w"])], 1),
        "posT": np.asarray(a["pos_BxS"]).reshape(B * TB, P).T,
        "freq": (1.0 / np.float32(10000.0) ** (np.arange(0, D1, 2, dtype=np.float32) / np.float32(D1))).astype(np.float32),
        "bada_gamma": np.asarray(a["L0_cond_bada"])[0:2 * C],
        "tw1T": by_contraction(a["L1_cond_ln1_tw"]),
        "tw2T": by_contraction(a["L1_cond_ln2_tw"]),
        "WadaT": by_contraction(a["L0_cond_Wada"]),
        "WqkvT": flat(a["L0_cond_Wqkv"]),
        "WprojT": flat(a["L0_cond_Wproj"]),
        "Wfc1T": flat(a["L0_cond_Wfc1"]),
        "Wfc2T": flat(a["L0_cond_Wfc2"]),
        "Wqkv1T": flat(np.concatenate([np.asarray(a[f"L1_cond_W{n}"]) for n in "qkv"])),
        "WoT": flat(a["L1_cond_Wo"]),
        "bfc1F": feat(a["L0_cond_bfc1"]),
        "bfc2": np.asarray(a["L0_cond_bfc2"]),
        "mask": np.asarray(a["mask_1x1xSxS_ff0"]).reshape(TB, P, L).transpose(1, 0, 2),
        "q_bias": np.asarray(a["L0_cond_q_bias"]),
        "v_bias": np.asarray(a["L0_cond_v_bias"]),
        "bproj": np.asarray(a["L0_cond_bproj"]),
        "scale_mul_log": np.asarray(a["L0_cond_scale_mul_log"]).reshape(H0),
        "ident": np.eye(P, dtype=np.float32),
    }.items()}


def kernel(**inputs):
    import concourse.bacc as bacc
    from concourse.bass_utils import run_bass_kernel_spmd

    arrays = lay_out(inputs)
    nc = bacc.Bacc("TRN2", target_bir_lowering=False, num_devices=1)
    io = {n: nc.dram_tensor(n, a.shape, mybir.dt.from_np(a.dtype), kind="ExternalInput").ap() for n, a in arrays.items()}
    x4 = nc.dram_tensor("x4", (B * L, C), F32, kind="ExternalOutput").ap()
    two_layers(nc, io, x4)
    r = run_bass_kernel_spmd(nc, [arrays], core_ids=[0])
    return r.results[0]["x4"].reshape(B, L, C)
```

```python
from contextlib import ExitStack, contextmanager

import numpy as np

import concourse.bass as bass
from concourse import mybir

F32 = mybir.dt.float32
F32R = mybir.dt.float32r
I32 = mybir.dt.int32
ACT = mybir.ActivationFunctionType
ALU = mybir.AluOpType
AX = mybir.AxisListType.X

P = 128
B, L, C = 16, 256, 512
CC = C // P
TB = L // P
H0, D0 = 16, C // 16
H1, D1 = 8, 64
HID = 4 * C
LN_EPS = 1e-6
RMS_EPS = 1e-6
GAMMA1, GAMMA2, SCALE1, SCALE2, SHIFT1, SHIFT2 = range(6)
TWO_PI_HI = 6.28125
TWO_PI_MID = 0.0019350051879882812
TWO_PI_LO = float(2 * np.pi - TWO_PI_HI - TWO_PI_MID)
ROUND = 12582912.0


@contextmanager
def semaphores(nc, prefix):
    made = []

    def sem(name):
        made.append(nc.alloc_semaphore(name=f"{prefix}_{name}"))
        return made[-1]

    yield sem
    nc.clear_and_free_semaphores(made)
    nc.all_engine_barrier()


class At:

    def __init__(self, half, par):
        self.half, self.par = half + par // 2 if par // 2 else half, par % 2

    def __add__(self, k):
        return At(self.half, self.par + k)

    def __sub__(self, k):
        return At(self.half - 4, self.par + 8 - k)

    def count(self, per, k):
        return self.half * (2 * per) + (self.par * per + k)

    def value(self):
        return self.half * 2 + self.par

    def first(self):
        return isinstance(self.half, int) and self.value() == 0

    def live(self, n=B):
        return not isinstance(self.half, int) or 0 <= self.value() < n


def wait(eng, sem, value):
    if not isinstance(value, int) or value > 0:
        eng.wait_ge(sem, value)


def over_batches(eng, body, n=B):
    for b in range(-2, 2):
        body(At(b // 2, b % 2))
    with eng.Fori(1, n // 2 - 1) as half:
        for par in range(2):
            body(At(half, par))
    for b in range(n - 2, n + 1):
        body(At(b // 2, b % 2))


def split_products(eng, out, stat, mov, first, last):
    eng.matmul(out, stat[0], mov[0], start=first, stop=False)
    eng.matmul(out, stat[0], mov[1], start=False, stop=False)
    return eng.matmul(out, stat[1], mov[0], start=False, stop=last)


class SplitWeights:
    W = 1024

    def __init__(self, sem, parts, slots, name="w"):
        self.slots = slots
        self.pieces = [(d, h, lo, c, min(self.W, d.shape[1] - c)) for d, h, lo in parts for c in range(0, d.shape[1], self.W)]
        self.ends = [sum(-(-d.shape[1] // self.W) for d, _, _ in parts[:i + 1]) for i in range(len(parts))]
        self.all = len(self.pieces)
        self.loaded = [sem(f"{name}_loaded{i}") for i in range(len(slots))]
        self.high_ready, self.low_ready = sem(f"{name}_high"), sem(f"{name}_low")

    def slot(self, n):
        return self.slots[n % len(self.slots)][:, 0:self.pieces[n][4]]

    def load_and_round(self, act, first, last):
        ring = len(self.slots)

        def load(n):
            d, _, _, c, w = self.pieces[n]
            act.dma_start(self.slot(n), d[:, c:c + w]).then_inc(self.loaded[n % ring], 16)

        if first == 0:
            for n in range(min(ring, len(self.pieces))):
                load(n)
        for n in range(first, last):
            _, h, _, c, w = self.pieces[n]
            act.wait_ge(self.loaded[n % ring], 16 * (n // ring + 1))
            act.activation(h[:, c:c + w], self.slot(n), ACT.Copy).then_inc(self.high_ready, 1)
            if n > 0 and n - 1 + ring < len(self.pieces):
                act.wait_ge(self.low_ready, n)
                load(n - 1 + ring)

    def take_rest(self, dve, first, last):
        for n in range(first, last):
            _, h, lo, c, w = self.pieces[n]
            dve.wait_ge(self.high_ready, n + 1)
            dve.tensor_tensor(lo[:, c:c + w], self.slot(n), h[:, c:c + w].bitcast(F32), ALU.subtract).then_inc(self.low_ready, 1)

    def wait_for(self, eng, part):
        eng.wait_ge(self.low_ready, self.ends[part])


def modulation(nc, io, scratch):
    NT = B * TB
    with ExitStack() as ctx:
        def sb(name, shape, dt=F32):
            return ctx.enter_context(nc.sbuf_tensor("mod_" + name, shape, dt))

        sem = ctx.enter_context(semaphores(nc, "mod"))
        cond = sb("cond", [P, CC * B])
        silu = sb("silu", [P, CC * B])
        bada = sb("bada", [B, 6 * C])
        lnw = sb("lnw", [P, 2, CC])
        ident = sb("ident", [P, P])
        mod0 = [sb(f"mod0_{s}", [P, B, 2, CC]) for s in range(2)]
        mod1 = [sb(f"mod1_{s}", [P, B, CC]) for s in range(2)]
        gam = sb("gam", [B, 2 * C])
        NS = 8
        NF = 6
        ADA = [SCALE1, SHIFT1, SCALE2, SHIFT2, None, None, GAMMA1, GAMMA2]
        weight = [sb(f"weight{i}", [P, CC, C]) for i in range(NS)]
        rows = sb("rows", [B, NF, C])
        pos = sb("pos", [P, NT], I32)
        posf = sb("posf", [P, NT])
        freq = sb("freq", [P, D1 // 2])
        ang = sb("ang", [P, NT, D1 // 2])
        turns = sb("turns", [P, NT, D1 // 2])
        half = sb("half", [P, NT, D1 // 2])
        rope = sb("rope", [P, NT, 2, D1 // 2])
        ps_rows = [ctx.enter_context(nc.psum_tensor(f"mod_ps_rows{i}", [B, C], F32)) for i in range(2)]
        ps_f = [ctx.enter_context(nc.psum_tensor(f"mod_ps_f{i}", [P, C // B, B], F32)) for i in range(NF)]
        loaded, silu_ready = sem("loaded"), sem("silu")
        weight_loaded = [sem(f"weight_loaded{i}") for i in range(NS)]
        product_ready, row_ready, transposed, feat_ready = sem("product"), sem("row"), sem("transposed"), sem("feat")
        step, sines, rope_ready, stored = sem("angle_step"), sem("sines"), sem("rope_ready"), sem("stored")
        SMALL = 16 * 6
        ANGLES, STEPS = 8, 9

        with nc.Block() as block:
            @block.sync
            def _(sp):
                for dst, src in [(cond[:, :], io["condT"]), (pos[:, :], io["posT"]),
                                 (freq[:, :], io["freq"].partition_broadcast(P)),
                                 (bada[:, :], io["bada"].partition_broadcast(B)),
                                 (lnw[:, :, :], io["lnwF"]), (ident[:, :], io["ident"])]:
                    sp.dma_start(dst, src).then_inc(loaded, 16)
                for i, section in enumerate(ADA):
                    src = io[f"tw{i - 3}T"] if section is None else io["WadaT"][:, :, section * C:(section + 1) * C]
                    sp.dma_start(weight[i][:, :, :], src).then_inc(weight_loaded[i], 16)
                sp.wait_ge(rope_ready, 1)
                sp.dma_start(scratch["rope"], rope[:, :, :, :].rearrange("p t s f -> p t (s f)")).then_inc(stored, 16)
                sp.wait_ge(feat_ready, NF)
                for s in range(2):
                    sp.dma_start(scratch["mod0"][s], mod0[s][:, :, :, :].rearrange("p b s c -> p b (s c)")).then_inc(stored, 16)
                    sp.dma_start(scratch["mod1"][s], mod1[s][:, :, :]).then_inc(stored, 16)
                sp.wait_ge(row_ready, NS)
                sp.dma_start(scratch["gamma"], gam[:, :]).then_inc(stored, 16)
                sp.wait_ge(stored, 16 * 6)

            @block.scalar
            def _(act):
                act.wait_ge(loaded, SMALL)
                act.activation(silu[:, :], cond[:, :], ACT.Silu).then_inc(silu_ready, 1)
                act.wait_ge(step, ANGLES)
                act.activation(rope[:, :, 1, :], ang[:, :, :], ACT.Sin).then_inc(sines, 1)
                act.activation(half[:, :, :], ang[:, :, :], ACT.Sin, scale=0.5).then_inc(sines, 1)

            @block.tensor
            def _(pe):
                pe.wait_ge(loaded, SMALL)
                pe.wait_ge(silu_ready, 1)

                def transposes(i):
                    pe.wait_ge(row_ready, i + 1)
                    for c in range(CC):
                        last = pe.transpose(ps_f[i][:, c, :], rows[:, i, c * P:(c + 1) * P], ident[0:B, 0:B])
                    last.then_inc(transposed, 1)

                for i in range(NS):
                    x = cond if ADA[i] is None else silu
                    pe.wait_ge(weight_loaded[i], 16)
                    wait(pe, row_ready, i - 1)
                    for k in range(CC):
                        last = pe.matmul(ps_rows[i % 2][:, :], x[:, k * B:(k + 1) * B], weight[i][:, k, :],
                                         start=(k == 0), stop=(k == CC - 1))
                    last.then_inc(product_ready, 1)
                    if 1 <= i <= NF:
                        transposes(i - 1)

            @block.vector
            def _(dve):
                done = 0

                def chain(ins):
                    nonlocal done
                    done += 1
                    ins.then_inc(step, 1)
                    dve.wait_ge(step, done)

                dve.wait_ge(loaded, SMALL)
                chain(dve.tensor_copy(posf[:, :], pos[:, :]))
                chain(dve.tensor_tensor(ang[:, :, :], posf[:, :].unsqueeze(2).to_broadcast([P, NT, D1 // 2]),
                                        freq[:, :].unsqueeze(1).to_broadcast([P, NT, D1 // 2]), ALU.mult))
                chain(dve.tensor_scalar(turns[:, :, :], ang[:, :, :], float(1 / (2 * np.pi)), ROUND, ALU.mult, ALU.add))
                chain(dve.tensor_scalar(turns[:, :, :], turns[:, :, :], -ROUND, None, ALU.add))
                for part in (TWO_PI_HI, TWO_PI_MID, TWO_PI_LO):
                    chain(dve.scalar_tensor_tensor(out=ang[:, :, :], in0=turns[:, :, :], scalar=-part,
                                                   in1=ang[:, :, :], op0=ALU.mult, op1=ALU.add))
                chain(dve.tensor_scalar(ang[:, :, :], ang[:, :, :], 3.1415925, -3.1415925, ALU.min, ALU.max))
                assert done == ANGLES, done

                def by_feature(i):
                    dve.wait_ge(transposed, i + 1)
                    src = ps_f[i][:, 0:CC, :].rearrange("p c b -> p b c")
                    if i < 4:
                        ins = dve.tensor_scalar(mod0[i // 2][:, :, i % 2, :], src, 1.0 - i % 2, None, ALU.add)
                    else:
                        ins = dve.tensor_tensor(mod1[i - 4][:, :, :], src,
                                                lnw[:, i - 4, :].unsqueeze(1).to_broadcast([P, B, CC]), ALU.mult)
                    ins.then_inc(feat_ready, 1)

                for i, section in enumerate(ADA):
                    dve.wait_ge(product_ready, i + 1)
                    if section is None:
                        ins = dve.tensor_scalar(rows[:, i, :], ps_rows[i % 2][:, :], 1.0, None, ALU.add)
                    else:
                        dst = rows[:, i, :] if i < NF else gam[:, (i - NF) * C:(i - NF + 1) * C]
                        ins = dve.tensor_tensor(dst, ps_rows[i % 2][:, :], bada[:, section * C:(section + 1) * C], ALU.add)
                    ins.then_inc(row_ready, 1)
                    if 1 <= i <= NF:
                        by_feature(i - 1)
                dve.wait_ge(sines, 2)
                chain(dve.tensor_tensor(half[:, :, :], half[:, :, :], half[:, :, :], ALU.mult))
                dve.tensor_scalar(rope[:, :, 0, :], half[:, :, :], -2.0, 1.0, ALU.mult, ALU.add).then_inc(rope_ready, 1)
                assert done == STEPS, done


def attention_l0(nc, io, scratch):
    with ExitStack() as ctx:
        def sb(name, shape, dt=F32):
            return ctx.enter_context(nc.sbuf_tensor("a0_" + name, shape, dt))

        def pb(name, shape):
            return ctx.enter_context(nc.psum_tensor("a0_" + name, shape, F32))

        sem = ctx.enter_context(semaphores(nc, "a0"))

        G = 4
        NG = H0 // G
        NQ = 3 * C
        wqkv = [sb(f"wqkv{i}", [P, CC * NQ], F32R) for i in range(2)]
        wproj = [sb(f"wproj{i}", [P, CC * C], F32R) for i in range(2)]
        W = [w[:, :].rearrange("p (k n) -> p k n", k=CC) for w in wqkv]
        WP = [w[:, :].rearrange("p (k n) -> p k n", k=CC) for w in wproj]

        xin = sb("xin", [P, 2, TB, C])
        xres = sb("xres", [P, TB, C])
        mod = sb("mod", [P, 2, 2, CC])
        gamma = sb("gamma", [P, 2, C])
        xn = sb("xn", [P, TB, C])
        h32 = sb("h32", [P, 2, L])
        hh = sb("hh", [P, CC, L], F32R)
        hl = sb("hl", [P, CC, L], F32R)
        qk = sb("qk", [P, 2 * C])
        square = sb("square", [P, 2 * C])
        unit = sb("unit", [P, 2, NG, 2, TB * G, D0])
        stack = sb("stack", [P, 2, 2, TB * G, P], F32R)
        v32 = sb("v32", [P, 2, TB, C])
        vh = sb("vh", [P, 2, TB, G, P], F32R)
        vl = sb("vl", [P, 2, TB, G, P], F32R)
        qkT = sb("qkT", [P, 2, 2, L], F32R)
        prob = sb("prob", [P, 4, TB, L])
        pTh = sb("pTh", [P, 2, TB, L], F32R)
        pTl = sb("pTl", [P, 2, TB, L], F32R)
        rdT = sb("rdT", [P, L])
        o32 = sb("o32", [P, L])
        oTh = sb("oTh", [P, NG, L], F32R)
        oTl = sb("oTl", [P, NG, L], F32R)
        y = sb("y", [P, TB, C])
        mask = sb("mask", [P, TB, L])
        qbias, vbias, pbias = sb("qbias", [P, C]), sb("vbias", [P, C]), sb("pbias", [P, C])
        ident = sb("ident", [P, P])
        sm = sb("sm", [P, 2 * H0])
        minus_half = sb("minus_half", [P, 2 * H0])
        spacer = sb("spacer", [P, 5])
        stats = sb("stats", [P, 6])
        mv = sb("mv", [P, 2])
        var = sb("var", [P, 1])
        rstd = sb("rstd", [P, 1])
        ss = sb("ss", [P, 2 * H0])
        norm = sb("norm", [P, 2 * H0])
        inv = sb("inv", [P, 2 * H0])
        nmax = sb("nmax", [P, 4, TB])
        den = sb("den", [P, 2, TB, G])
        rd = sb("rd", [P, TB, G])
        rden = sb("rden", [P, 2, TB, G * D0])

        psT = pb("psT", [P, 2, L])
        psF = pb("psF", [P, C])
        psS = [pb(f"psS{i}", [P, TB, L]) for i in range(2)]
        psP = [pb(f"psP{i}", [P, TB, L]) for i in range(2)]
        psO = [pb(f"psO{i}", [P, 2, L]) for i in range(2)]

        consts_loaded, const_ready = sem("consts_loaded"), sem("const_ready")
        x_loaded = [sem(f"x_loaded{i}") for i in range(2)]
        mod_loaded = [sem(f"mod_loaded{i}") for i in range(2)]
        gamma_loaded = [sem(f"gamma_loaded{i}") for i in range(2)]
        res_loaded = [sem(f"res_loaded{i}") for i in range(TB)]
        stored = [sem(f"stored{i}") for i in range(TB)]
        mean_ready, var_ready, rstd_ready, xn_ready = sem("mean"), sem("var"), sem("rstd"), sem("xn")
        stats_ready = sem("stats")
        hT_ready, h32_ready, hh_ready, hl_ready = sem("hT"), sem("h32"), sem("hh"), sem("hl")
        q_ready, k_ready, v_ready = sem("q_ready"), sem("k_ready"), sem("v_ready")
        q_taken, k_taken, v_taken = sem("q_taken"), sem("k_taken"), sem("v_taken")
        sq_ready, ss_ready, norm_ready = sem("sq"), sem("ss"), sem("norm")
        pow_ready, inv_ready, unit_ready = sem("pow"), sem("inv"), sem("unit")
        stack_high_ready, stack_ready = sem("stack_high"), sem("stack")
        t_ready, t_taken = sem("t_ready"), [sem("t_taken_act"), sem("t_taken_dve")]
        s_ready, max_ready, exp_ready = sem("s_ready"), sem("max_ready"), sem("exp_ready")
        p_ready, pTh_ready, pTl_ready = sem("p_ready"), sem("pTh"), sem("pTl")
        vh_ready, vl_ready, pv_ready = sem("vh"), sem("vl"), sem("pv")
        rden_ready, rdp_ready, rdT_ready = sem("rden"), sem("rdp"), sem("rdT")
        rd_ready = sem("rd")
        o32_ready, oTh_ready, oTl_ready = sem("o32"), sem("oTh"), sem("oTl")
        proj_ready, y_bias, y_gamma, y_ready = sem("proj"), sem("y_bias"), sem("y_gamma"), sem("y_ready")
        CONSTS = 16 * 6
        flat_prob = prob[:, :, :, :].rearrange("p a t l -> p (a t l)")
        weights = SplitWeights(sem, [(io["WqkvT"], wqkv[0], wqkv[1]), (io["WprojT"], wproj[0], wproj[1])],
                               [flat_prob[:, 0:1024], flat_prob[:, 1024:2048], y[:, :, :].rearrange("p t c -> p (t c)"),
                                square[:, :]])

        LN_AT, XN_AT = {3: 0, 9: 1}, {5: 0, 10: 1}
        HT_AT = {0: 0, 1: 1}
        Q_AT, K_AT, V_AT = {2: 0, 9: 1}, {3: 0, 10: 1}, {5: 0, 13: 1}
        NORM_AT, UNIT_AT = {4: 0, 11: 1}, {6: 0, 13: 1}
        PROJ_AT = {7: 0, 8: 1}
        SCORES, EXP, PT, SPLIT, VALUES, OUT, OUT_SPLIT = 1, 2, 3, 4, 5, 6, 7

        def head(b, s, lag):
            return (b, s - lag) if s >= lag else (b - 1, H0 + s - lag)

        def stack_parts(g, i):
            if i == 0:
                rows = stack[:, g % 2, i, :, :].rearrange("p n (r s d) -> p n r s d", r=2, s=2)
                return rows[:, :, :, 0, :], rows[:, :, :, 1, :]
            rows = stack[:, g % 2, i, :, :].rearrange("p n (s r d) -> p n s r d", r=2, s=2)
            return rows[:, :, 0, :, :], rows[:, :, 1, :, :]

        def next_group(b, s):
            return (b, s // G + 1) if s < H0 - G else (b + 1, 0)

        def pieces(b, s, fn, table):
            if s in table and b.live():
                fn(b, table[s])

        with nc.Block() as block:
            @block.sync
            def _(sp):
                for dst, src in [(mask[:, :, :], io["mask"]), (qbias[:, :], io["q_bias"].partition_broadcast(P)),
                                 (vbias[:, :], io["v_bias"].partition_broadcast(P)),
                                 (pbias[:, :], io["bproj"].partition_broadcast(P)),
                                 (sm[:, 0:H0], io["scale_mul_log"].partition_broadcast(P)),
                                 (ident[:, :], io["ident"])]:
                    sp.dma_start(dst, src).then_inc(consts_loaded, 16)

                def load_front(b):
                    wait(sp, xn_ready, (b - 2).count(TB, TB))
                    sp.dma_start(xin[:, b.par, :, :], io["x"][bass.ds(b.value() * L, L), :].rearrange("(t p) c -> p t c", p=P))\
                      .then_inc(x_loaded[b.par], 16)
                    wait(sp, h32_ready, (b - 2).count(CC, CC))
                    sp.dma_start(mod[:, b.par, :, :].rearrange("p s c -> p (s c)"),
                                 scratch["mod0"][0, :, bass.ds(b.value(), 1), :].rearrange("p b s -> p (b s)"))\
                      .then_inc(mod_loaded[b.par], 16)

                def load_back(b):
                    wait(sp, y_gamma, (b - 1).count(TB, TB))
                    sp.dma_start(gamma[:, b.par, :],
                                 scratch["gamma"][bass.ds(b.value(), 1), GAMMA1 * C:(GAMMA1 + 1) * C].partition_broadcast(P)
                                 .rearrange("p a c -> p (a c)"))\
                      .then_inc(gamma_loaded[b.par], 16)
                    for t in range(TB):
                        wait(sp, y_ready, (b - 1).count(TB, t + 1))
                        sp.dma_start(xres[:, t, :], io["x"][bass.ds(b.value() * L + t * P, P), :]).then_inc(res_loaded[t], 16)

                def store(b):
                    for t in range(TB):
                        wait(sp, y_ready, b.count(TB, t + 1))
                        sp.dma_start(scratch["x1"][bass.ds(b.value() * L + t * P, P), :], y[:, t, :]).then_inc(stored[t], 16)

                def body(b):
                    if (b + 2).live():
                        load_front(b + 2)
                    if (b - 1).live():
                        load_back(b - 1)
                        store(b - 1)

                over_batches(sp, body)
                for t in range(TB):
                    sp.wait_ge(stored[t], 16 * B)

            @block.gpsimd
            def _(pool):
                pool.memset(minus_half[:, :], -0.5).then_inc(const_ready, 1)
                pool.memset(vh[:, :, :, :, :].bitcast(F32), 0.0).then_inc(const_ready, 1)
                pool.memset(vl[:, :, :, :, :].bitcast(F32), 0.0).then_inc(const_ready, 1)
                pool.wait_ge(const_ready, 3)

                def layer_norm(b, t):
                    wait(pool, var_ready, b.count(TB, t + 1))
                    pool.tensor_tensor(rstd[:, :], var[:, :], minus_half[:, 0:1], ALU.pow).then_inc(rstd_ready, 1)

                def unit_heads(b, t):
                    wait(pool, norm_ready, b.count(TB, t + 1))
                    pool.tensor_tensor(norm[:, :], norm[:, :], minus_half[:, :], ALU.pow).then_inc(pow_ready, 1)

                def stack_low(b, g):
                    wait(pool, stack_high_ready, b.count(NG, g + 1))
                    for i in range(2):
                        src = unit[:, b.par, g, i, :, :].unsqueeze(2).to_broadcast([P, TB * G, 2, D0])
                        high, low = stack_parts(g, i)
                        ins = pool.tensor_tensor(low, src, high.bitcast(F32), ALU.subtract)
                    ins.then_inc(stack_ready, 1)

                def values_low(b, g):
                    wait(pool, vh_ready, b.count(NG, g + 1))
                    for j in range(G):
                        src = (slice(None), g % 2, slice(None), j, slice(D0 * j, D0 * j + D0))
                        ins = pool.tensor_tensor(vl[src], v32[:, b.par, :, (g * G + j) * D0:(g * G + j + 1) * D0],
                                                 vh[src].bitcast(F32), ALU.subtract)
                    ins.then_inc(vl_ready, 1)

                def residual(b, t):
                    wait(pool, y_bias, b.count(TB, t + 1))
                    pool.wait_ge(gamma_loaded[b.par], b.half * 16 + 16)
                    pool.tensor_tensor(y[:, t, :], y[:, t, :], gamma[:, b.par, :], ALU.mult).then_inc(y_gamma, 1)
                    pool.wait_ge(res_loaded[t], b.count(16, 16))
                    wait(pool, y_gamma, b.count(TB, t + 1))
                    pool.tensor_tensor(y[:, t, :], y[:, t, :], xres[:, t, :], ALU.add).then_inc(y_ready, 1)

                def body(b):
                    for s in range(H0):
                        if b.live() and s % G == 1:
                            values_low(b, s // G)
                        if s % G == 2:
                            bb, g = next_group(b, s)
                            if bb.live():
                                stack_low(bb, g)
                        pieces(b + 2, s, layer_norm, LN_AT)
                        pieces(b + 1, s, unit_heads, NORM_AT)
                        pieces(b - 1, s, residual, PROJ_AT)

                over_batches(pool, body)

            @block.scalar
            def _(act):

                def modulate(b, pair):
                    act.wait_ge(mod_loaded[b.par], b.half * 16 + 16)
                    wait(act, hT_ready, b.count(2, pair + 1))
                    for i in range(2):
                        c = 2 * pair + i
                        wait(act, hl_ready, b.count(CC, c - 1))
                        act.activation(h32[:, i, :], psF[:, i * L:(i + 1) * L], ACT.Identity,
                                       bias=mod[:, b.par, 1, c:c + 1], scale=mod[:, b.par, 0, c:c + 1]).then_inc(h32_ready, 1)
                    if pair == 0:
                        wait(act, v_ready, (b - 1).count(TB, TB))
                    for i in range(2):
                        c = 2 * pair + i
                        act.wait_ge(h32_ready, b.count(CC, c + 1))
                        act.activation(hh[:, c, :], h32[:, i, :], ACT.Copy).then_inc(hh_ready, 1)

                def take_k(b, t):
                    wait(act, k_ready, b.count(TB, t + 1))
                    wait(act, unit_ready, b.count(TB, t))
                    act.activation(qk[:, C:2 * C], psF[:, :], ACT.Copy).then_inc(k_taken, 1)

                def unit_heads(b, t):
                    wait(act, q_taken, b.count(TB, t + 1))
                    wait(act, k_taken, b.count(TB, t + 1))
                    wait(act, ss_ready, b.count(TB, t))
                    act.activation(square[:, :], qk[:, :], ACT.Square).then_inc(sq_ready, 1)

                def stack_high(b, g):
                    if g == 0:
                        wait(act, unit_ready, b.count(TB, TB))
                    wait(act, t_ready, b.count(H0, (g - 1) * G))
                    for i in range(2):
                        src = unit[:, b.par, g, i, :, :].unsqueeze(2).to_broadcast([P, TB * G, 2, D0])
                        ins = act.activation(stack_parts(g, i)[0], src, ACT.Copy)
                    ins.then_inc(stack_high_ready, 1)

                def values_high(b, g):
                    if g == 0:
                        wait(act, v_taken, b.count(TB, TB))
                    wait(act, pv_ready, b.count(H0, (g - 1) * G))
                    for j in range(G):
                        ins = act.activation(vh[:, g % 2, :, j, D0 * j:D0 * j + D0],
                                             v32[:, b.par, :, (g * G + j) * D0:(g * G + j + 1) * D0], ACT.Copy)
                    ins.then_inc(vh_ready, 1)

                def take_heads(b, h):
                    wait(act, t_ready, b.count(H0, h + 1))
                    wait(act, s_ready, b.count(H0, h - 1))
                    act.activation(qkT[:, h % 2, :, :], psT[:, :, :], ACT.Copy).then_inc(t_taken[0], 1)

                def softmax(b, h):
                    g, j = h // G, h % G
                    wait(act, max_ready, b.count(H0, h + 1))
                    if j == 0:
                        wait(act, rden_ready, b.count(NG, g - 1))
                    for qc in range(TB):
                        ins = act.activation(prob[:, h % 4, qc, :], prob[:, h % 4, qc, :], ACT.Exp, scale=-1.0,
                                             bias=nmax[:, h % 4, qc:qc + 1], accum_out=den[:, g % 2, qc, j:j + 1])
                    ins.then_inc(exp_ready, 1)

                def probs_high(b, h):
                    wait(act, p_ready, b.count(H0, h + 1))
                    wait(act, pv_ready, b.count(H0, h - 1))
                    act.activation(pTh[:, h % 2, :, :], psP[h % 2][:, :, :], ACT.Copy).then_inc(pTh_ready, 1)

                def take_denominators(b, g):
                    wait(act, rdp_ready, b.count(NG, g + 1))
                    wait(act, o32_ready, b.count(NG, g))
                    act.activation(rdT[:, :], psO[g % 2][:, 1, :], ACT.Copy).then_inc(rdT_ready, 1)

                def output_high(b, g):
                    act.wait_ge(o32_ready, b.count(NG, g + 1))
                    if g == 0:
                        wait(act, proj_ready, (b - 1).count(TB, TB))
                    act.activation(oTh[:, g, :], o32[:, :], ACT.Copy).then_inc(oTh_ready, 1)

                weights.load_and_round(act, 0, weights.all)
                act.wait_ge(const_ready, 5)
                act.activation(sm[:, 0:H0], sm[:, 0:H0], ACT.Exp).then_inc(const_ready, 1)

                def body(b):
                    for s in range(H0):
                        for lag, stage in ((SPLIT, probs_high), (EXP, softmax)):
                            bb, h = head(b, s, lag)
                            if bb.live():
                                stage(bb, h)
                        for lag, stage in ((OUT_SPLIT, output_high), (OUT, take_denominators)):
                            bb, h = head(b, s, lag)
                            if bb.live() and h % G == G - 1:
                                stage(bb, h // G)
                        if b.live():
                            if s % 2 == 0:
                                take_heads(b, s)
                            if s % G == 1:
                                values_high(b, s // G)
                        if s % G == 2:
                            bb, g = next_group(b, s)
                            if bb.live():
                                stack_high(bb, g)
                        pieces(b + 1, s, modulate, HT_AT)
                        pieces(b + 1, s, take_k, K_AT)
                        pieces(b + 1, s, unit_heads, NORM_AT)

                over_batches(act, body)

            @block.tensor
            def _(pe):
                pe.wait_ge(consts_loaded, CONSTS)
                pe.wait_ge(const_ready, 5)

                def transposes_h(b, pair):
                    if pair == 0:
                        wait(pe, xn_ready, b.count(TB, TB))
                        wait(pe, v_taken, (b - 1).count(TB, TB))
                    else:
                        wait(pe, h32_ready, b.count(CC, 2))
                    for i in range(2):
                        for t in range(TB):
                            c = 2 * pair + i
                            last = pe.transpose(psF[:, i * L + t * P:i * L + (t + 1) * P], xn[:, t, c * P:(c + 1) * P], ident[:, :])
                    last.then_inc(hT_ready, 1)

                def project(b, t, section, ready):
                    for k in range(CC):
                        last = split_products(pe, psF[:, :], (hh[:, k, t * P:(t + 1) * P], hl[:, k, t * P:(t + 1) * P]),
                                              [w[:, k, section * C:(section + 1) * C] for w in W], k == 0, k == CC - 1)
                    last.then_inc(ready, 1)

                def project_q(b, t):
                    if b.first() and t == 0:
                        weights.wait_for(pe, 0)
                    if t == 0:
                        wait(pe, hl_ready, b.count(CC, CC))
                    elif (b - 2).live():
                        wait(pe, y_bias, (b - 2).count(TB, TB))
                    else:
                        wait(pe, v_taken, b.count(TB, t))
                    project(b, t, 0, q_ready)

                def project_k(b, t):
                    wait(pe, q_taken, b.count(TB, t + 1))
                    project(b, t, 1, k_ready)

                def project_v(b, t):
                    wait(pe, k_taken, b.count(TB, t + 1))
                    project(b, t, 2, v_ready)

                def transposes_qk(b, h):
                    g, j = h // G, h % G
                    if j == 0:
                        wait(pe, stack_ready, b.count(NG, g + 1))
                    wait(pe, t_taken[(h - 1) % 2], b.count(H0 // 2, (h + 1) // 2))
                    for i in range(2):
                        for t in range(TB):
                            last = pe.transpose(psT[:, i, t * P:(t + 1) * P], stack[:, g % 2, i, t * G + j, :].bitcast(F32),
                                                ident[:, :])
                    last.then_inc(t_ready, 1)

                def scores(b, h):
                    wait(pe, t_taken[h % 2], b.count(H0 // 2, h // 2 + 1))
                    wait(pe, max_ready, b.count(H0, h - 1))
                    for qc in range(TB):
                        last = pe.matmul(psS[h % 2][:, qc, :], qkT[:, h % 2, 0, qc * P:(qc + 1) * P], qkT[:, h % 2, 1, :],
                                         start=True, stop=True)
                    last.then_inc(s_ready, 1)

                def transposes_p(b, h):
                    wait(pe, exp_ready, b.count(H0, h + 1))
                    wait(pe, pTl_ready, b.count(H0, h - 1))
                    for kc in range(TB):
                        for qc in range(TB):
                            last = pe.transpose(psP[h % 2][:, kc, qc * P:(qc + 1) * P], prob[:, h % 4, qc, kc * P:(kc + 1) * P],
                                                ident[:, :])
                    last.then_inc(p_ready, 1)

                def values(b, h):
                    g, j = h // G, h % G
                    if j == 0:
                        wait(pe, vl_ready, b.count(NG, g + 1))
                        wait(pe, o32_ready, b.count(NG, g - 1))
                    wait(pe, pTl_ready, b.count(H0, h + 1))
                    for kc in range(TB):
                        last = split_products(pe, psO[g % 2][:, 0, :], (vh[:, g % 2, kc, j, :], vl[:, g % 2, kc, j, :]),
                                              (pTh[:, h % 2, kc, :], pTl[:, h % 2, kc, :]),
                                              j == 0 and kc == 0, j == G - 1 and kc == TB - 1)
                    last.then_inc(pv_ready, 1)
                    if j == G - 1:
                        wait(pe, rden_ready, b.count(NG, g + 1))
                        for qc in range(TB):
                            last = pe.transpose(psO[g % 2][:, 1, qc * P:(qc + 1) * P],
                                                rden[:, g % 2, qc, :], ident[:, :])
                        last.then_inc(rdp_ready, 1)

                def project_out(b, t):
                    if b.first() and t == 0:
                        weights.wait_for(pe, 1)
                    if t == 0:
                        wait(pe, oTl_ready, b.count(NG, NG))
                    nxt = b + 2
                    if t == 1:
                        wait(pe, y_bias, b.count(TB, 1))
                    elif nxt.live():
                        wait(pe, v_taken, nxt.count(TB, 1))
                    else:
                        wait(pe, v_taken, TB * B)
                        wait(pe, y_bias, (b - 1).count(TB, TB))
                    for g in range(NG):
                        last = split_products(pe, psF[:, :], (oTh[:, g, t * P:(t + 1) * P], oTl[:, g, t * P:(t + 1) * P]),
                                              [w[:, g, :] for w in WP], g == 0, g == NG - 1)
                    last.then_inc(proj_ready, 1)

                def body(b):
                    for s in range(H0):
                        for lag, stage in ((VALUES, values), (PT, transposes_p), (SCORES, scores)):
                            bb, h = head(b, s, lag)
                            if bb.live():
                                stage(bb, h)
                        if b.live():
                            transposes_qk(b, s)
                        pieces(b + 1, s, transposes_h, HT_AT)
                        pieces(b - 1, s, project_out, PROJ_AT)
                        pieces(b + 1, s, project_q, Q_AT)
                        pieces(b + 1, s, project_k, K_AT)
                        pieces(b + 1, s, project_v, V_AT)

                over_batches(pe, body)

            @block.vector
            def _(dve):
                dve.wait_ge(consts_loaded, CONSTS)
                dve.tensor_scalar(sm[:, 0:H0], sm[:, 0:H0], float(np.log(np.float32(100.0))), None, ALU.min)\
                   .then_inc(const_ready, 1)
                dve.memset(sm[:, H0:2 * H0], 1.0).then_inc(const_ready, 1)

                def layer_norm(b, t):
                    dve.wait_ge(x_loaded[b.par], b.half * 16 + 16)
                    x = xin[:, b.par, t, :]
                    dve.bn_stats(stats[:, :], x).then_inc(stats_ready, 1)
                    dve.wait_ge(stats_ready, b.count(TB, t + 1))
                    dve.memset(spacer[:, 4:5], 0.0)
                    dve.bn_aggr(mv[:, :], stats[:, :]).then_inc(mean_ready, 1)
                    dve.wait_ge(mean_ready, b.count(TB, t + 1))
                    dve.tensor_scalar(var[:, :], mv[:, 1:2], LN_EPS, None, ALU.add).then_inc(var_ready, 1)

                def normalise(b, t):
                    if t == 0:
                        wait(dve, hT_ready, (b - 1).count(2, 2))
                    dve.wait_ge(rstd_ready, b.count(TB, t + 1))
                    dve.tensor_scalar(xn[:, t, :], xin[:, b.par, t, :], mv[:, 0:1], rstd[:, 0:1], ALU.subtract, ALU.mult).then_inc(xn_ready, 1)

                def low_h(b, pair):
                    for i in range(2):
                        c = 2 * pair + i
                        dve.wait_ge(hh_ready, b.count(CC, c + 1))
                        dve.tensor_tensor(hl[:, c, :], h32[:, i, :], hh[:, c, :].bitcast(F32), ALU.subtract).then_inc(hl_ready, 1)

                def take_q(b, t):
                    dve.wait_ge(q_ready, b.count(TB, t + 1))
                    wait(dve, unit_ready, b.count(TB, t))
                    dve.tensor_tensor(qk[:, 0:C], psF[:, :], qbias[:, :], ALU.add).then_inc(q_taken, 1)

                def take_v(b, t):
                    dve.wait_ge(v_ready, b.count(TB, t + 1))
                    wait(dve, vl_ready, (b - 2).count(NG, NG))
                    dve.tensor_tensor(v32[:, b.par, t, :], psF[:, :], vbias[:, :], ALU.add).then_inc(v_taken, 1)

                def square_sums(b, t):
                    dve.wait_ge(sq_ready, b.count(TB, t + 1))
                    dve.tensor_reduce(ss[:, :], square[:, :].rearrange("p (h d) -> p h d", d=D0), AX, ALU.add).then_inc(ss_ready, 1)
                    dve.wait_ge(ss_ready, b.count(TB, t + 1))
                    dve.tensor_scalar(norm[:, :], ss[:, :], 1e-24, None, ALU.max).then_inc(norm_ready, 1)

                def make_unit(b, t):
                    dve.wait_ge(pow_ready, b.count(TB, t + 1))
                    dve.tensor_tensor(inv[:, :], norm[:, :], sm[:, :], ALU.mult).then_inc(inv_ready, 1)
                    dve.wait_ge(inv_ready, b.count(TB, t + 1))
                    if t == 0:
                        wait(dve, stack_ready, (b - 1).count(NG, 0))
                    for i in range(2):
                        heads = qk[:, i * C:(i + 1) * C].rearrange("p (g j d) -> p g j d", g=NG, j=G)
                        scale = inv[:, i * H0:(i + 1) * H0].rearrange("p (g j) -> p g j", g=NG).unsqueeze(3)\
                            .to_broadcast([P, NG, G, D0])
                        ins = dve.tensor_tensor(unit[:, b.par, :, i, t * G:(t + 1) * G, :], heads, scale, ALU.mult)
                    ins.then_inc(unit_ready, 1)

                def take_heads(b, h):
                    dve.wait_ge(t_ready, b.count(H0, h + 1))
                    wait(dve, s_ready, b.count(H0, h - 1))
                    dve.tensor_copy(qkT[:, h % 2, :, :], psT[:, :, :]).then_inc(t_taken[1], 1)

                def score_max(b, h):
                    dve.wait_ge(s_ready, b.count(H0, h + 1))
                    wait(dve, p_ready, b.count(H0, h - 3))
                    dve.memset(spacer[:, h % 4:h % 4 + 1], 0.0)
                    for qc in range(TB):
                        ins = dve.tensor_tensor_reduce(prob[:, h % 4, qc, :], psS[h % 2][:, qc, :], mask[:, qc, :], -1.0, 3e38,
                                                       ALU.add, ALU.min, nmax[:, h % 4, qc:qc + 1])
                    ins.then_inc(max_ready, 1)

                def probs_low(b, h):
                    dve.wait_ge(pTh_ready, b.count(H0, h + 1))
                    dve.tensor_tensor(pTl[:, h % 2, :, :], psP[h % 2][:, :, :], pTh[:, h % 2, :, :].bitcast(F32), ALU.subtract)\
                       .then_inc(pTl_ready, 1)

                def denominators(b, g):
                    dve.wait_ge(exp_ready, b.count(H0, (g + 1) * G))
                    wait(dve, rdp_ready, b.count(NG, g - 1))
                    dve.reciprocal(rd[:, :, :], den[:, g % 2, :, :]).then_inc(rd_ready, 1)
                    dve.wait_ge(rd_ready, b.count(NG, g + 1))
                    dve.tensor_copy(rden[:, g % 2, :, :].rearrange("p q (j d) -> p q j d", j=G),
                                    rd[:, :, :].unsqueeze(3).to_broadcast([P, TB, G, D0])).then_inc(rden_ready, 1)

                def group_output(b, g):
                    dve.wait_ge(rdT_ready, b.count(NG, g + 1))
                    wait(dve, oTl_ready, b.count(NG, g))
                    dve.tensor_tensor(o32[:, :], psO[g % 2][:, 0, :], rdT[:, :], ALU.mult).then_inc(o32_ready, 1)

                def output_low(b, g):
                    dve.wait_ge(oTh_ready, b.count(NG, g + 1))
                    dve.tensor_tensor(oTl[:, g, :], o32[:, :], oTh[:, g, :].bitcast(F32), ALU.subtract).then_inc(oTl_ready, 1)

                def add_bias(b, t):
                    dve.wait_ge(proj_ready, b.count(TB, t + 1))
                    wait(dve, stored[t], (b - 1).count(16, 16))
                    dve.tensor_tensor(y[:, t, :], psF[:, :], pbias[:, :], ALU.add).then_inc(y_bias, 1)

                for t in range(TB):
                    weights.take_rest(dve, 2 * t, 2 * (t + 1))
                    layer_norm(At(0, 0), t)
                    normalise(At(0, 0), t)
                weights.take_rest(dve, 2 * TB, weights.all)
                dve.wait_ge(const_ready, 6)

                def body(b):
                    for s in range(H0):
                        for lag, stage in ((SPLIT, probs_low), (SCORES, score_max)):
                            bb, h = head(b, s, lag)
                            if bb.live():
                                stage(bb, h)
                        bb, h = head(b, s, PT)
                        if bb.live() and h % G == G - 1:
                            denominators(bb, h // G)
                        for lag, stage in ((OUT_SPLIT, output_low), (OUT, group_output)):
                            bb, h = head(b, s, lag)
                            if bb.live() and h % G == G - 1:
                                stage(bb, h // G)
                        if b.live() and s % 2 == 1:
                            take_heads(b, s)
                        if not (b + 2).first():
                            pieces(b + 2, s, layer_norm, LN_AT)
                            pieces(b + 2, s, normalise, XN_AT)
                        pieces(b + 1, s, low_h, HT_AT)
                        pieces(b + 1, s, take_q, Q_AT)
                        pieces(b + 1, s, take_v, V_AT)
                        pieces(b + 1, s, square_sums, NORM_AT)
                        pieces(b + 1, s, make_unit, UNIT_AT)
                        pieces(b - 1, s, add_bias, PROJ_AT)

                over_batches(dve, body)



def over_blocks(eng, body):
    over_batches(eng, body, B // 2)


def mlp_l0(nc, io, scratch):
    with ExitStack() as ctx:
        def sb(name, shape, dt=F32):
            return ctx.enter_context(nc.sbuf_tensor("m0_" + name, shape, dt))

        def pb(name, shape):
            return ctx.enter_context(nc.psum_tensor("m0_" + name, shape, F32))

        sem = ctx.enter_context(semaphores(nc, "m0"))

        NJ = HID // P
        TT = 2 * TB
        T = TT * P
        NB = B // 2
        DOWN, ACT_LAG = 3, 1
        w1 = [sb(f"w1{i}", [P, CC * HID], F32R) for i in range(2)]
        w2 = [sb(f"w2{i}", [P, NJ * C], F32R) for i in range(2)]
        W1 = [w[:, :].rearrange("p (k n) -> p k n", k=CC) for w in w1]
        W2 = [w[:, :].rearrange("p (k n) -> p k n", k=NJ) for w in w2]

        xin = sb("xin", [P, TT, C])
        xres = sb("xres", [P, 2, C])
        mod = sb("mod", [P, 2, 2, 2 * CC])
        gamma = sb("gamma", [P, 2, C])
        b1 = sb("b1", [P, NJ])
        b2 = sb("b2", [P, C])
        ident = sb("ident", [P, P])
        minus_half = sb("minus_half", [P, 1])
        xn = sb("xn", [P, TT, C])
        h32 = sb("h32", [P, 2, T])
        hh = sb("hh", [P, CC, T], F32R)
        hl = sb("hl", [P, CC, T], F32R)
        act32 = sb("act32", [P, 2, T])
        uh = sb("uh", [P, 4, T], F32R)
        ul = sb("ul", [P, 4, T], F32R)
        y = sb("y", [P, TT, C])
        spacer = sb("spacer", [P, 1])
        stats, mv, var, rstd = sb("stats", [P, 6]), sb("mv", [P, 2]), sb("var", [P, 1]), sb("rstd", [P, 1])

        psT = [pb(f"psT{i}", [P, T]) for i in range(2)]
        psU = [pb(f"psU{i}", [P, T]) for i in range(2)]
        psD = [pb(f"psD{i}", [P, C]) for i in range(TT)]

        consts_loaded, const_ready = sem("consts_loaded"), sem("const_ready")
        x_loaded = [sem(f"x_loaded{i}") for i in range(TT)]
        res_loaded = [sem(f"res_loaded{i}") for i in range(2)]
        stored = [sem(f"stored{i}") for i in range(TT)]
        mod_loaded = [sem(f"mod_loaded{i}") for i in range(2)]
        gamma_loaded = sem("gamma_loaded")
        stats_ready, mean_ready, var_ready, rstd_ready, xn_ready = sem("stats"), sem("mean"), sem("var"), sem("rstd"), sem("xn")
        hT_ready, h32_ready, hh_ready, hl_ready = sem("hT"), sem("h32"), sem("hh"), sem("hl")
        up_ready, act_ready, uh_ready, ul_ready, down_ready = sem("up"), sem("act"), sem("uh"), sem("ul"), sem("down")
        y_bias, y_gamma, y_ready = sem("y_bias"), sem("y_gamma"), sem("y_ready")

        flat = [sb("stage", [P, 1024]), act32[:, :, :].rearrange("p i t -> p (i t)"), y[:, :, :].rearrange("p t c -> p (t c)")]
        weights = SplitWeights(sem, [(io["Wfc1T"], w1[0], w1[1]), (io["Wfc2T"], w2[0], w2[1])],
                               [tile[:, c:c + 1024] for tile in flat for c in range(0, tile.shape[1], 1024)])

        LN_AT = {4: 0, 6: 1, 8: 2, 10: 3}
        HT_AT = {12: 0, 13: 1, 14: 2, 15: 3}
        OUT_AT = 3

        def chunk(b, s, lag):
            return (b, s - lag) if s >= lag else (b - 1, NJ + s - lag)

        def pieces(b, s, fn, table):
            if s in table and b.live(NB):
                fn(b, table[s])

        with nc.Block() as block:
            @block.sync
            def _(sp):
                for dst, src in [(b1[:, :], io["bfc1F"]), (b2[:, :], io["bfc2"].partition_broadcast(P)),
                                 (ident[:, :], io["ident"])]:
                    sp.dma_start(dst, src).then_inc(consts_loaded, 16)

                def load_front(b, t):
                    if t == 0:
                        wait(sp, h32_ready, (b - 2).count(CC, CC))
                        sp.dma_start(mod[:, b.par, :, :].rearrange("p b s -> p (b s)"),
                                     scratch["mod0"][1, :, bass.ds(b.value() * 2, 2), :].rearrange("p b s -> p (b s)"))\
                          .then_inc(mod_loaded[b.par], 16)
                    wait(sp, xn_ready, (b - 1).count(TT, t + 1))
                    sp.dma_start(xin[:, t, :], scratch["x1"][bass.ds((b.value() * TT + t) * P, P), :])\
                      .then_inc(x_loaded[t], 16)

                def back(b, t):
                    if t == 0:
                        wait(sp, y_gamma, (b - 1).count(TT, TT))
                        for i in range(2):
                            sp.dma_start(gamma[:, i, :], scratch["gamma"][bass.ds(b.value() * 2 + i, 1), GAMMA2 * C:(GAMMA2 + 1) * C]
                                         .partition_broadcast(P).rearrange("p a c -> p (a c)")).then_inc(gamma_loaded, 16)
                    wait(sp, y_ready, b.count(TT, t - 1))
                    sp.dma_start(xres[:, t % 2, :], scratch["x1"][bass.ds((b.value() * TT + t) * P, P), :])\
                      .then_inc(res_loaded[t % 2], 16)

                def store(b, t):
                    wait(sp, y_ready, b.count(TT, t + 1))
                    sp.dma_start(scratch["x2"][bass.ds((b.value() * TT + t) * P, P), :], y[:, t, :]).then_inc(stored[t], 16)

                def body(b):
                    for t in range(TT):
                        if (b - 1).live(NB):
                            back(b - 1, t)
                            if t > 0:
                                store(b - 1, t - 1)
                    if (b - 1).live(NB):
                        store(b - 1, TT - 1)
                    for t in range(TT):
                        if (b + 1).live(NB):
                            load_front(b + 1, t)

                over_blocks(sp, body)
                for t in range(TT):
                    sp.wait_ge(stored[t], 16 * NB)

            @block.gpsimd
            def _(pool):
                pool.memset(minus_half[:, :], -0.5).then_inc(const_ready, 1)
                pool.wait_ge(const_ready, 1)

                def layer_norm(b, t):
                    pool.wait_ge(var_ready, b.count(TT, t + 1))
                    pool.tensor_tensor(rstd[:, :], var[:, :], minus_half[:, :], ALU.pow).then_inc(rstd_ready, 1)

                def residual(b, t):
                    pool.wait_ge(gamma_loaded, b.count(32, 32))
                    pool.wait_ge(y_bias, b.count(TT, t + 1))
                    pool.tensor_tensor(y[:, t, :], y[:, t, :], gamma[:, t // TB, :], ALU.mult).then_inc(y_gamma, 1)
                    pool.wait_ge(res_loaded[t % 2], b.count(32, 16 * (t // 2 + 1)))
                    pool.wait_ge(y_gamma, b.count(TT, t + 1))
                    pool.tensor_tensor(y[:, t, :], y[:, t, :], xres[:, t % 2, :], ALU.add).then_inc(y_ready, 1)

                def body(b):
                    for s in range(NJ):
                        if s == OUT_AT and (b - 1).live(NB):
                            for t in range(TT):
                                residual(b - 1, t)
                        pieces(b + 1, s, layer_norm, LN_AT)

                over_blocks(pool, body)

            @block.scalar
            def _(act):
                act.wait_ge(consts_loaded, 48)

                def gelu(b, j):
                    act.wait_ge(up_ready, b.count(NJ, j + 1))
                    wait(act, ul_ready, b.count(NJ, j - 1))
                    if b.first() and j == 0:
                        weights.wait_for(act, 1)
                    act.activation(act32[:, j % 2, :], psU[j % 2][:, :], ACT.Gelu_apprx_tanh, bias=b1[:, j:j + 1]).then_inc(act_ready, 1)
                    act.wait_ge(act_ready, b.count(NJ, j + 1))
                    wait(act, down_ready, b.count(NJ, j - 3))
                    act.activation(uh[:, j % 4, :], act32[:, j % 2, :], ACT.Copy).then_inc(uh_ready, 1)

                def modulate(b, c):
                    if c == 0:
                        act.wait_ge(mod_loaded[b.par], b.half * 16 + 16)
                    act.wait_ge(hT_ready, b.count(CC, c + 1))
                    wait(act, hl_ready, b.count(CC, c - 1))
                    for i in range(2):
                        ins = act.activation(h32[:, c % 2, i * L:(i + 1) * L], psT[c % 2][:, i * L:(i + 1) * L], ACT.Identity,
                                             bias=mod[:, b.par, i, CC + c:CC + c + 1], scale=mod[:, b.par, i, c:c + 1])
                    ins.then_inc(h32_ready, 1)
                    if c == 0:
                        wait(act, up_ready, (b - 1).count(NJ, NJ))
                    act.wait_ge(h32_ready, b.count(CC, c + 1))
                    act.activation(hh[:, c, :], h32[:, c % 2, :], ACT.Copy).then_inc(hh_ready, 1)

                weights.load_and_round(act, 0, weights.ends[0])
                for c in range(CC):
                    modulate(At(0, 0), c)
                weights.load_and_round(act, weights.ends[0], weights.all)

                def body(b):
                    for s in range(NJ):
                        bb, j = chunk(b, s, ACT_LAG)
                        if bb.live(NB):
                            gelu(bb, j)
                        if s == NJ - 1 and (b + 1).live(NB) and not (b + 1).first():
                            for c in range(CC):
                                modulate(b + 1, c)

                over_blocks(act, body)

            @block.tensor
            def _(pe):
                pe.wait_ge(consts_loaded, 48)

                def transposes_h(b, c):
                    if c == 0:
                        pe.wait_ge(xn_ready, b.count(TT, TT))
                    wait(pe, h32_ready, b.count(CC, c - 1))
                    for t in range(TT):
                        last = pe.transpose(psT[c % 2][:, t * P:(t + 1) * P], xn[:, t, c * P:(c + 1) * P], ident[:, :])
                    last.then_inc(hT_ready, 1)

                def up(b, j):
                    if b.first() and j == 0:
                        weights.wait_for(pe, 0)
                    wait(pe, act_ready, b.count(NJ, j - 1))
                    for k in range(CC):
                        if j == 0:
                            pe.wait_ge(hl_ready, b.count(CC, k + 1))
                        last = split_products(pe, psU[j % 2][:, :], [w[:, k, j * P:(j + 1) * P] for w in W1],
                                              (hh[:, k, :], hl[:, k, :]), k == 0, k == CC - 1)
                    last.then_inc(up_ready, 1)

                def down(b, j):
                    if b.first() and j == 0:
                        weights.wait_for(pe, 1)
                    pe.wait_ge(ul_ready, b.count(NJ, j + 1))
                    for t in range(TT):
                        if j == 0:
                            wait(pe, y_bias, (b - 1).count(TT, t + 1))
                        last = split_products(pe, psD[t][:, :], (uh[:, j % 4, t * P:(t + 1) * P], ul[:, j % 4, t * P:(t + 1) * P]),
                                              [w[:, j, :] for w in W2], j == 0, j == NJ - 1)
                    last.then_inc(down_ready, 1)

                def body(b):
                    for s in range(NJ):
                        if b.live(NB):
                            up(b, s)
                        bb, j = chunk(b, s, DOWN)
                        if bb.live(NB):
                            down(bb, j)
                        pieces(b + 1, s, transposes_h, HT_AT)

                over_blocks(pe, body)

            @block.vector
            def _(dve):
                dve.wait_ge(consts_loaded, 48)

                def layer_norm(b, t):
                    dve.wait_ge(x_loaded[t], b.count(16, 16))
                    x = xin[:, t, :]
                    dve.bn_stats(stats[:, :], x).then_inc(stats_ready, 1)
                    dve.wait_ge(stats_ready, b.count(TT, t + 1))
                    dve.memset(spacer[:, :], 0.0)
                    dve.bn_aggr(mv[:, :], stats[:, :]).then_inc(mean_ready, 1)
                    dve.wait_ge(mean_ready, b.count(TT, t + 1))
                    dve.tensor_scalar(var[:, :], mv[:, 1:2], LN_EPS, None, ALU.add).then_inc(var_ready, 1)
                    if t == 0:
                        wait(dve, hT_ready, (b - 1).count(CC, CC))
                    dve.wait_ge(rstd_ready, b.count(TT, t + 1))
                    dve.tensor_scalar(xn[:, t, :], x, mv[:, 0:1], rstd[:, 0:1], ALU.subtract, ALU.mult).then_inc(xn_ready, 1)

                def low_h(b, c):
                    dve.wait_ge(hh_ready, b.count(CC, c + 1))
                    dve.tensor_tensor(hl[:, c, :], h32[:, c % 2, :], hh[:, c, :].bitcast(F32), ALU.subtract).then_inc(hl_ready, 1)

                def low_u(b, j):
                    dve.wait_ge(uh_ready, b.count(NJ, j + 1))
                    dve.tensor_tensor(ul[:, j % 4, :], act32[:, j % 2, :], uh[:, j % 4, :].bitcast(F32), ALU.subtract).then_inc(ul_ready, 1)

                def add_bias(b, t):
                    dve.wait_ge(down_ready, b.count(NJ, NJ))
                    wait(dve, stored[t], b.count(16, 0))
                    dve.tensor_tensor(y[:, t, :], psD[t][:, :], b2[:, :], ALU.add).then_inc(y_bias, 1)

                for t in range(TT):
                    layer_norm(At(0, 0), t)
                    weights.take_rest(dve, 2 * t, 2 * (t + 1))
                weights.take_rest(dve, 2 * TT, weights.ends[0])
                for c in range(CC):
                    low_h(At(0, 0), c)
                weights.take_rest(dve, weights.ends[0], weights.all)

                def body(b):
                    for s in range(NJ):
                        if s == OUT_AT and (b - 1).live(NB):
                            for t in range(TT):
                                add_bias(b - 1, t)
                        bb, j = chunk(b, s, ACT_LAG)
                        if bb.live(NB):
                            low_u(bb, j)
                        if not (b + 1).first():
                            pieces(b + 1, s, layer_norm, LN_AT)
                        if s == NJ - 1 and (b + 1).live(NB) and not (b + 1).first():
                            for c in range(CC):
                                low_h(b + 1, c)

                over_blocks(dve, body)


def attention_l1(nc, io, scratch):
    with ExitStack() as ctx:
        def sb(name, shape, dt=F32):
            return ctx.enter_context(nc.sbuf_tensor("a1_" + name, shape, dt))

        def pb(name, shape):
            return ctx.enter_context(nc.psum_tensor("a1_" + name, shape, F32))

        sem = ctx.enter_context(semaphores(nc, "a1"))

        G = 2
        NG = H1 // G
        KV = 2 * D1
        NQ = C + KV
        HK = H1 + 1
        SCALE = float(D1) ** -0.5
        wqkv = [sb(f"wqkv{i}", [P, CC * NQ], F32R) for i in range(2)]
        wo = [sb(f"wo{i}", [P, CC * C], F32R) for i in range(2)]
        W = [w[:, :].rearrange("p (k n) -> p k n", k=CC) for w in wqkv]
        WO = [w[:, :].rearrange("p (k n) -> p k n", k=CC) for w in wo]

        xin = sb("xin", [P, 2, TB, C])
        xres = sb("xres", [P, TB, C])
        mod = sb("mod", [P, 2, CC])
        rope = sb("rope", [P, 2, TB, 2, D1 // 2])
        xn = sb("xn", [P, TB, C])
        h32 = sb("h32", [P, CC, L])
        hh = sb("hh", [P, CC, L], F32R)
        hl = sb("hl", [P, CC, L], F32R)
        raw = sb("raw", [P, TB, HK + 1, 2, D1 // 2])
        by_cos = sb("by_cos", [P, TB, HK, 2, D1 // 2])
        by_sin = sb("by_sin", [P, TB, HK, 2, D1 // 2])
        qs = sb("qs", [P, 2, TB, H1, 2, D1], F32R)
        ks = sb("ks", [P, TB, 2, 2, D1], F32R)
        vh = sb("vh", [P, 2, TB, G, P], F32R)
        vl = sb("vl", [P, 2, TB, G, P], F32R)
        qT = sb("qT", [P, 2, G, L], F32R)
        kT = sb("kT", [P, 2, 2, L], F32R)
        prob = sb("prob", [P, 4, TB, L])
        pTh = sb("pTh", [P, 2, TB, L], F32R)
        pTl = sb("pTl", [P, 2, TB, L], F32R)
        rdT = sb("rdT", [P, L])
        o32 = sb("o32", [P, L])
        oTh = sb("oTh", [P, 2, NG, L], F32R)
        oTl = sb("oTl", [P, 2, NG, L], F32R)
        y = sb("y", [P, TB, C])
        ident = sb("ident", [P, P])
        minus_half = sb("minus_half", [P, 1])
        spacer = sb("spacer", [P, 1])
        stats, mv, square = sb("stats", [P, 6]), sb("mv", [P, 2]), sb("square", [P, 1])
        var, rstd = sb("var", [P, 1]), sb("rstd", [P, 1])
        rmax = sb("rmax", [P, 4, TB])
        nmax = sb("nmax", [P, 4, TB])
        den = sb("den", [P, 2, TB, G])
        rd = sb("rd", [P, TB, G])
        rden = sb("rden", [P, 2, TB, G * D1])

        psT = pb("psT", [P, G, L])
        psF = pb("psF", [P, C])
        psS = [pb(f"psS{i}", [P, TB, L]) for i in range(2)]
        psP = [pb(f"psP{i}", [P, TB, L]) for i in range(2)]
        psO = [pb(f"psO{i}", [P, 2, L]) for i in range(2)]

        consts_loaded, const_ready = sem("consts_loaded"), sem("const_ready")
        x_loaded = [sem(f"x_loaded{i}") for i in range(2)]
        mod_loaded = [sem(f"mod_loaded{i}") for i in range(2)]
        rope_loaded = [sem(f"rope_loaded{i}") for i in range(2)]
        res_loaded = [sem(f"res_loaded{i}") for i in range(TB)]
        stored = [sem(f"stored{i}") for i in range(TB)]
        stats_ready, mean_ready, square_ready, var_ready = sem("stats"), sem("mean"), sem("square"), sem("var")
        rstd_ready, xn_ready = sem("rstd"), sem("xn")
        hT_ready, h32_ready, hh_ready, hl_ready = sem("hT"), sem("h32"), sem("hh"), sem("hl")
        q_ready, kv_ready, q_taken, kv_taken = sem("q_ready"), sem("kv_ready"), sem("q_taken"), sem("kv_taken")
        vh_ready, vl_ready = sem("vh"), sem("vl")
        sin_ready, rot_ready, high_ready, low_ready = sem("sin"), sem("rot"), sem("high"), sem("low")
        kT_ready, kT_taken = sem("kT_ready"), sem("kT_taken")
        t_ready, t_taken = sem("t_ready"), [sem("t_taken_act"), sem("t_taken_dve")]
        s_ready, rmax_ready, max_ready, exp_ready = sem("s_ready"), sem("rmax"), sem("max_ready"), sem("exp_ready")
        p_ready, pTh_ready, pTl_ready, pv_ready = sem("p_ready"), sem("pTh"), sem("pTl"), sem("pv")
        rden_ready, rdp_ready, rdT_ready = sem("rden"), sem("rdp"), sem("rdT")
        rd_ready = sem("rd")
        o32_ready, oTh_ready, oTl_ready = sem("o32"), sem("oTh"), sem("oTl")
        proj_ready, y_ready = sem("proj"), sem("y_ready")

        stage = sb("stage", [P, 4 * 1024])
        weights = SplitWeights(sem, [(io["Wqkv1T"], wqkv[0], wqkv[1]), (io["WoT"], wo[0], wo[1])],
                               [stage[:, c * 1024:(c + 1) * 1024] for c in range(4)])

        LN_AT, XN_AT = {3: 0, 5: 1}, {4: 0, 6: 1}
        HT_EARLY, HT_LATE = {0: 0}, {0: 1}
        Q_LATE, KV_EARLY = {1: 0, 2: 1}, {2: 0, 3: 1}
        ANGLES_LATE, SPLIT_EARLY = {2: 0, 3: 1}, {4: 0, 5: 1}
        KT_EARLY, V_LATE = {6: 0}, {6: 0}
        PROJ_LATE = {6: 0, 7: 1}
        SCORES, EXP, PT, SPLIT, VALUES, OUT, OUT_SPLIT = 1, 2, 3, 4, 5, 6, 7

        def head(b, s, lag):
            return (b, s - lag) if s >= lag else (b - 1, H1 + s - lag)

        def pieces(b, s, fn, table):
            if s in table and b.live():
                fn(b, table[s])

        def stage(b, s, lag, fn):
            bb, h = head(b, s, lag)
            if bb.live():
                fn(bb, h)

        def group_stage(b, s, lag, fn):
            bb, h = head(b, s, lag)
            if bb.live() and h % G == G - 1:
                fn(bb, h // G)

        def v_place(tile, b, j):
            return tile[:, b.par, :, j, j * D1:(j + 1) * D1]

        v_rows = raw[:, :, HK, :, :].rearrange("p t i f -> p t (i f)")

        with nc.Block() as block:
            @block.sync
            def _(sp):
                sp.dma_start(ident[:, :], io["ident"]).then_inc(consts_loaded, 16)

                def load_front(b):
                    wait(sp, xn_ready, (b - 2).count(TB, TB))
                    sp.dma_start(xin[:, b.par, :, :], scratch["x2"][bass.ds(b.value() * L, L), :].rearrange("(t p) c -> p t c", p=P))\
                      .then_inc(x_loaded[b.par], 16)
                    wait(sp, h32_ready, (b - 2).count(CC, CC))
                    sp.dma_start(mod[:, b.par, :], scratch["mod1"][0, :, bass.ds(b.value(), 1), :].rearrange("p b s -> p (b s)"))\
                      .then_inc(mod_loaded[b.par], 16)
                    wait(sp, sin_ready, (b - 2).count(TB, TB))
                    sp.dma_start(rope[:, b.par, :, :, :].rearrange("p t s f -> p t (s f)"),
                                 scratch["rope"][:, bass.ds(b.value() * TB, TB), :]).then_inc(rope_loaded[b.par], 16)

                def back(b):
                    for t in range(TB):
                        wait(sp, y_ready, (b - 1).count(TB, t + 1))
                        sp.dma_start(xres[:, t, :], scratch["x2"][bass.ds(b.value() * L + t * P, P), :]).then_inc(res_loaded[t], 16)
                    for t in range(TB):
                        wait(sp, y_ready, b.count(TB, t + 1))
                        sp.dma_start(scratch["x3"][bass.ds(b.value() * L + t * P, P), :], y[:, t, :]).then_inc(stored[t], 16)

                def body(b):
                    if (b + 2).live():
                        load_front(b + 2)
                    if (b - 1).live():
                        back(b - 1)

                over_batches(sp, body)
                for t in range(TB):
                    sp.wait_ge(stored[t], 16 * B)

            @block.gpsimd
            def _(pool):
                pool.memset(minus_half[:, :], -0.5).then_inc(const_ready, 1)
                pool.memset(vh[:, :, :, :, :].bitcast(F32), 0.0).then_inc(const_ready, 1)
                pool.memset(vl[:, :, :, :, :].bitcast(F32), 0.0).then_inc(const_ready, 1)
                pool.wait_ge(const_ready, 3)

                def root_mean_square(b, t):
                    pool.wait_ge(var_ready, b.count(TB, t + 1))
                    pool.tensor_tensor(rstd[:, :], var[:, :], minus_half[:, :], ALU.pow).then_inc(rstd_ready, 1)

                def rotate(b, t):
                    pool.wait_ge(sin_ready, b.count(TB, t + 1))
                    pool.tensor_tensor(by_cos[:, t, :, 0, :], by_cos[:, t, :, 0, :], by_sin[:, t, :, 0, :], ALU.subtract)
                    pool.tensor_tensor(by_cos[:, t, :, 1, :], by_cos[:, t, :, 1, :], by_sin[:, t, :, 1, :], ALU.add)\
                        .then_inc(rot_ready, 1)

                def low(b, t):
                    pool.wait_ge(high_ready, b.count(TB, t + 1))
                    rot = by_cos[:, t, :, :, :].rearrange("p h i f -> p h (i f)")
                    pool.tensor_tensor(qs[:, b.par, t, :, 1, :], rot[:, 0:H1, :], qs[:, b.par, t, :, 0, :].bitcast(F32), ALU.subtract)
                    pool.tensor_tensor(ks[:, t, 1, :, :], rot[:, H1:HK, :].to_broadcast([P, 2, D1]),
                                       ks[:, t, 0, :, :].bitcast(F32), ALU.subtract).then_inc(low_ready, 1)

                def body(b):
                    for s in range(H1):
                        pieces(b + 1, s, low, SPLIT_EARLY)
                        pieces(b + 1, s, rotate, ANGLES_LATE)
                        pieces(b + 2, s, root_mean_square, LN_AT)

                over_batches(pool, body)

            @block.scalar
            def _(act):
                act.wait_ge(const_ready, 3)

                def modulate(b, pair):
                    if pair == 0:
                        act.wait_ge(mod_loaded[b.par], b.half * 16 + 16)
                        wait(act, hl_ready, (b - 1).count(CC, CC))
                    act.wait_ge(hT_ready, b.count(2, pair + 1))
                    for i in range(2):
                        c = 2 * pair + i
                        act.activation(h32[:, c, :], psF[:, i * L:(i + 1) * L], ACT.Copy, scale=mod[:, b.par, c:c + 1])\
                           .then_inc(h32_ready, 1)
                    if pair == 0:
                        wait(act, kv_ready, (b - 1).count(TB, TB))
                    for i in range(2):
                        c = 2 * pair + i
                        act.wait_ge(h32_ready, b.count(CC, c + 1))
                        act.activation(hh[:, c, :], h32[:, c, :], ACT.Copy).then_inc(hh_ready, 1)

                def take_q(b, t):
                    act.wait_ge(q_ready, b.count(TB, t + 1))
                    wait(act, sin_ready, (b - 1).count(TB, t + 1))
                    act.activation(raw[:, t, 0:H1, :, :].rearrange("p h i f -> p (h i f)"), psF[:, :], ACT.Copy).then_inc(q_taken, 1)

                def take_kv(b, t):
                    act.wait_ge(kv_ready, b.count(TB, t + 1))
                    wait(act, vl_ready, (b - 1).count(1, 1))
                    act.activation(raw[:, t, H1:HK + 1, :, :].rearrange("p h i f -> p (h i f)"), psF[:, 0:KV], ACT.Copy)\
                       .then_inc(kv_taken, 1)

                def values_high(b, _):
                    wait(act, pv_ready, (b - 2).count(H1, H1))
                    act.wait_ge(kv_taken, b.count(TB, TB))
                    for j in range(G):
                        ins = act.activation(v_place(vh, b, j), v_rows, ACT.Copy)
                    ins.then_inc(vh_ready, 1)

                def high(b, t):
                    act.wait_ge(rot_ready, b.count(TB, t + 1))
                    wait(act, t_ready, (b - 2).count(NG, NG))
                    wait(act, kT_ready, (b - 1).count(1, 1))
                    rot = by_cos[:, t, :, :, :].rearrange("p h i f -> p h (i f)")
                    act.activation(qs[:, b.par, t, :, 0, :], rot[:, 0:H1, :], ACT.Copy)
                    act.activation(ks[:, t, 0, :, :], rot[:, H1:HK, :].to_broadcast([P, 2, D1]), ACT.Copy).then_inc(high_ready, 1)

                def take_kT(b, _):
                    act.wait_ge(kT_ready, b.count(1, 1))
                    wait(act, s_ready, (b - 1).count(H1, 0))
                    act.activation(kT[:, b.par, :, :].rearrange("p s l -> p (s l)"), psF[:, :], ACT.Copy).then_inc(kT_taken, 1)

                def take_qT(b, g):
                    act.wait_ge(t_ready, b.count(NG, g + 1))
                    wait(act, s_ready, b.count(H1, (g - 1) * G))
                    act.activation(qT[:, g % 2, :, :], psT[:, :, :], ACT.Copy).then_inc(t_taken[0], 1)

                def softmax(b, h):
                    g, j = h // G, h % G
                    act.wait_ge(max_ready, b.count(H1, h + 1))
                    wait(act, p_ready, b.count(H1, h - 3))
                    if j == 0:
                        wait(act, rden_ready, b.count(NG, g - 1))
                    for qc in range(TB):
                        ins = act.activation(prob[:, h % 4, qc, :], psS[h % 2][:, qc, :], ACT.Exp, scale=SCALE,
                                             bias=nmax[:, h % 4, qc:qc + 1], accum_out=den[:, g % 2, qc, j:j + 1])
                    ins.then_inc(exp_ready, 1)

                def probs_high(b, h):
                    act.wait_ge(p_ready, b.count(H1, h + 1))
                    wait(act, pv_ready, b.count(H1, h - 1))
                    act.activation(pTh[:, h % 2, :, :], psP[h % 2][:, :, :], ACT.Copy).then_inc(pTh_ready, 1)

                def take_denominators(b, g):
                    act.wait_ge(rdp_ready, b.count(NG, g + 1))
                    wait(act, o32_ready, b.count(NG, g))
                    act.activation(rdT[:, :], psO[g % 2][:, 1, :], ACT.Copy).then_inc(rdT_ready, 1)

                def output_high(b, g):
                    act.wait_ge(o32_ready, b.count(NG, g + 1))
                    if g == 0:
                        wait(act, proj_ready, (b - 1).count(TB, 1))
                    act.activation(oTh[:, b.par, g, :], o32[:, :], ACT.Copy).then_inc(oTh_ready, 1)

                weights.load_and_round(act, 0, weights.all)

                def body(b):
                    for s in range(H1):
                        group_stage(b, s, OUT_SPLIT, output_high)
                        group_stage(b, s, OUT, take_denominators)
                        stage(b, s, SPLIT, probs_high)
                        pieces(b + 1, s, modulate, HT_EARLY)
                        pieces(b + 1, s, take_kv, KV_EARLY)
                        pieces(b + 1, s, take_kT, KT_EARLY)
                        pieces(b + 1, s, high, SPLIT_EARLY)
                        stage(b, s, EXP, softmax)
                        if b.live() and s % 4 == 0:
                            take_qT(b, s // G)
                        pieces(b + 1, s, values_high, V_LATE)
                        pieces(b + 1, s, modulate, HT_LATE)
                        pieces(b + 1, s, take_q, Q_LATE)

                over_batches(act, body)

            @block.tensor
            def _(pe):
                pe.wait_ge(consts_loaded, 16)

                def transposes_h(b, pair):
                    if pair == 0:
                        pe.wait_ge(xn_ready, b.count(TB, TB))
                        if (b - 3).live():
                            pe.wait_ge(y_ready, (b - 3).count(TB, TB))
                        else:
                            wait(pe, kT_taken, (b - 1).count(1, 1))
                    else:
                        pe.wait_ge(h32_ready, b.count(CC, 2))
                    for i in range(2):
                        for t in range(TB):
                            c = 2 * pair + i
                            last = pe.transpose(psF[:, i * L + t * P:i * L + (t + 1) * P], xn[:, t, c * P:(c + 1) * P], ident[:, :])
                    last.then_inc(hT_ready, 1)

                def project_q(b, t):
                    if b.first() and t == 0:
                        weights.wait_for(pe, 0)
                    if t == 0:
                        pe.wait_ge(hl_ready, b.count(CC, CC))
                    else:
                        pe.wait_ge(kv_taken, b.count(TB, t))
                    for k in range(CC):
                        last = split_products(pe, psF[:, :], (hh[:, k, t * P:(t + 1) * P], hl[:, k, t * P:(t + 1) * P]),
                                              [w[:, k, 0:C] for w in W], k == 0, k == CC - 1)
                    last.then_inc(q_ready, 1)

                def project_kv(b, t):
                    pe.wait_ge(q_taken, b.count(TB, t + 1))
                    for k in range(CC):
                        last = split_products(pe, psF[:, 0:KV], (hh[:, k, t * P:(t + 1) * P], hl[:, k, t * P:(t + 1) * P]),
                                              [w[:, k, C:NQ] for w in W], k == 0, k == CC - 1)
                    last.then_inc(kv_ready, 1)

                def transposes_k(b, _):
                    pe.wait_ge(low_ready, b.count(TB, TB))
                    pe.wait_ge(kv_taken, b.count(TB, TB))
                    for i in range(2):
                        for t in range(TB):
                            last = pe.transpose(psF[:, i * L + t * P:i * L + (t + 1) * P],
                                                ks[:, t, i, :, :].rearrange("p r d -> p (r d)").bitcast(F32), ident[:, :])
                    last.then_inc(kT_ready, 1)

                def transposes_q(b, g):
                    if g == 0:
                        pe.wait_ge(low_ready, b.count(TB, TB))
                    wait(pe, t_taken[(g - 1) % 2], b.count(NG // 2, (g + 1) // 2))
                    for j in range(G):
                        for t in range(TB):
                            last = pe.transpose(psT[:, j, t * P:(t + 1) * P],
                                                qs[:, b.par, t, g * G + j, :, :].rearrange("p s d -> p (s d)").bitcast(F32), ident[:, :])
                    last.then_inc(t_ready, 1)

                def scores(b, h):
                    g, j = h // G, h % G
                    if h == 0:
                        pe.wait_ge(kT_taken, b.count(1, 1))
                    pe.wait_ge(t_taken[g % 2], b.count(NG // 2, g // 2 + 1))
                    wait(pe, exp_ready, b.count(H1, h - 1))
                    for qc in range(TB):
                        for i in range(2):
                            last = pe.matmul(psS[h % 2][:, qc, :], qT[:, g % 2, j, qc * P:(qc + 1) * P], kT[:, b.par, i, :],
                                             start=(i == 0), stop=(i == 1))
                    last.then_inc(s_ready, 1)

                def transposes_p(b, h):
                    pe.wait_ge(exp_ready, b.count(H1, h + 1))
                    wait(pe, pTl_ready, b.count(H1, h - 1))
                    for kc in range(TB):
                        for qc in range(TB):
                            last = pe.transpose(psP[h % 2][:, kc, qc * P:(qc + 1) * P], prob[:, h % 4, qc, kc * P:(kc + 1) * P],
                                                ident[:, :])
                    last.then_inc(p_ready, 1)

                def values(b, h):
                    g, j = h // G, h % G
                    if j == 0:
                        pe.wait_ge(vl_ready, b.count(1, 1))
                        wait(pe, o32_ready, b.count(NG, g - 1))
                    pe.wait_ge(pTl_ready, b.count(H1, h + 1))
                    for kc in range(TB):
                        last = split_products(pe, psO[g % 2][:, 0, :], (vh[:, b.par, kc, j, :], vl[:, b.par, kc, j, :]),
                                              (pTh[:, h % 2, kc, :], pTl[:, h % 2, kc, :]),
                                              j == 0 and kc == 0, j == G - 1 and kc == TB - 1)
                    last.then_inc(pv_ready, 1)
                    if j == G - 1:
                        pe.wait_ge(rden_ready, b.count(NG, g + 1))
                        for qc in range(TB):
                            last = pe.transpose(psO[g % 2][:, 1, qc * P:(qc + 1) * P], rden[:, g % 2, qc, :], ident[:, :])
                        last.then_inc(rdp_ready, 1)

                def project_out(b, t):
                    if b.first() and t == 0:
                        weights.wait_for(pe, 1)
                    nxt = b + 2
                    if t == 0:
                        pe.wait_ge(oTl_ready, b.count(NG, NG))
                        if nxt.live():
                            pe.wait_ge(kT_taken, nxt.count(1, 1))
                        else:
                            pe.wait_ge(y_ready, (b - 1).count(TB, TB))
                    else:
                        pe.wait_ge(y_ready, b.count(TB, 1))
                    for g in range(NG):
                        last = split_products(pe, psF[:, :], (oTh[:, b.par, g, t * P:(t + 1) * P], oTl[:, b.par, g, t * P:(t + 1) * P]),
                                              [w[:, g, :] for w in WO], g == 0, g == NG - 1)
                    last.then_inc(proj_ready, 1)

                def body(b):
                    for s in range(H1):
                        stage(b, s, VALUES, values)
                        stage(b, s, PT, transposes_p)
                        pieces(b + 1, s, transposes_h, HT_EARLY)
                        pieces(b + 1, s, project_kv, KV_EARLY)
                        pieces(b + 1, s, transposes_k, KT_EARLY)
                        stage(b, s, SCORES, scores)
                        if b.live() and s % 2 == 0:
                            transposes_q(b, s // G)
                        pieces(b + 1, s, transposes_h, HT_LATE)
                        pieces(b + 1, s, project_q, Q_LATE)
                        pieces(b - 1, s, project_out, PROJ_LATE)

                over_batches(pe, body)

            @block.vector
            def _(dve):
                dve.wait_ge(const_ready, 3)

                def root_mean_square(b, t):
                    if t == 0:
                        dve.wait_ge(x_loaded[b.par], b.half * 16 + 16)
                    x = xin[:, b.par, t, :]
                    dve.bn_stats(stats[:, :], x).then_inc(stats_ready, 1)
                    dve.wait_ge(stats_ready, b.count(TB, t + 1))
                    dve.memset(spacer[:, :], 0.0)
                    dve.bn_aggr(mv[:, :], stats[:, :]).then_inc(mean_ready, 1)
                    dve.wait_ge(mean_ready, b.count(TB, t + 1))
                    dve.tensor_tensor(square[:, :], mv[:, 0:1], mv[:, 0:1], ALU.mult).then_inc(square_ready, 1)
                    dve.wait_ge(square_ready, b.count(TB, t + 1))
                    dve.tensor_scalar(var[:, :], square[:, :], mv[:, 1:2], RMS_EPS, ALU.add, ALU.add).then_inc(var_ready, 1)

                def normalise(b, t):
                    if t == 0:
                        wait(dve, hT_ready, (b - 1).count(2, 2))
                    dve.wait_ge(rstd_ready, b.count(TB, t + 1))
                    dve.tensor_scalar(xn[:, t, :], xin[:, b.par, t, :], rstd[:, 0:1], None, ALU.mult).then_inc(xn_ready, 1)

                def low_h(b, pair):
                    for i in range(2):
                        c = 2 * pair + i
                        dve.wait_ge(hh_ready, b.count(CC, c + 1))
                        dve.tensor_tensor(hl[:, c, :], h32[:, c, :], hh[:, c, :].bitcast(F32), ALU.subtract).then_inc(hl_ready, 1)

                def values_low(b, _):
                    dve.wait_ge(vh_ready, b.count(1, 1))
                    for j in range(G):
                        ins = dve.tensor_tensor(v_place(vl, b, j), v_rows, v_place(vh, b, j).bitcast(F32), ALU.subtract)
                    ins.then_inc(vl_ready, 1)

                def by_angles(b, t):
                    if t == 0:
                        dve.wait_ge(rope_loaded[b.par], b.half * 16 + 16)
                    dve.wait_ge(kv_taken, b.count(TB, t + 1))
                    wait(dve, low_ready, (b - 1).count(TB, t + 1))
                    cos = rope[:, b.par, t, 0, :].unsqueeze(1).to_broadcast([P, 2 * HK, D1 // 2])
                    sin = rope[:, b.par, t, 1, :].unsqueeze(1).to_broadcast([P, HK, D1 // 2])
                    dve.tensor_tensor(by_cos[:, t, :, :, :].rearrange("p h i f -> p (h i) f"),
                                      raw[:, t, 0:HK, :, :].rearrange("p h i f -> p (h i) f"), cos, ALU.mult)
                    for i in range(2):
                        ins = dve.tensor_tensor(by_sin[:, t, :, i, :], raw[:, t, 0:HK, 1 - i, :], sin, ALU.mult)
                    ins.then_inc(sin_ready, 1)

                def take_qT(b, g):
                    dve.wait_ge(t_ready, b.count(NG, g + 1))
                    wait(dve, s_ready, b.count(H1, (g - 1) * G))
                    dve.tensor_copy(qT[:, g % 2, :, :], psT[:, :, :]).then_inc(t_taken[1], 1)

                def score_max(b, h):
                    dve.wait_ge(s_ready, b.count(H1, h + 1))
                    dve.tensor_reduce(rmax[:, h % 4, :], psS[h % 2][:, :, :], AX, ALU.max).then_inc(rmax_ready, 1)
                    dve.wait_ge(rmax_ready, b.count(H1, h + 1))
                    dve.tensor_scalar(nmax[:, h % 4, :], rmax[:, h % 4, :], -SCALE, None, ALU.mult).then_inc(max_ready, 1)

                def probs_low(b, h):
                    dve.wait_ge(pTh_ready, b.count(H1, h + 1))
                    dve.tensor_tensor(pTl[:, h % 2, :, :], psP[h % 2][:, :, :], pTh[:, h % 2, :, :].bitcast(F32), ALU.subtract)\
                       .then_inc(pTl_ready, 1)

                def denominators(b, g):
                    dve.wait_ge(exp_ready, b.count(H1, (g + 1) * G))
                    wait(dve, rdp_ready, b.count(NG, g - 1))
                    dve.reciprocal(rd[:, :, :], den[:, g % 2, :, :]).then_inc(rd_ready, 1)
                    dve.wait_ge(rd_ready, b.count(NG, g + 1))
                    dve.tensor_copy(rden[:, g % 2, :, :].rearrange("p q (j d) -> p q j d", j=G),
                                    rd[:, :, :].unsqueeze(3).to_broadcast([P, TB, G, D1])).then_inc(rden_ready, 1)

                def group_output(b, g):
                    dve.wait_ge(rdT_ready, b.count(NG, g + 1))
                    wait(dve, oTl_ready, b.count(NG, g))
                    dve.tensor_tensor(o32[:, :], psO[g % 2][:, 0, :], rdT[:, :], ALU.mult).then_inc(o32_ready, 1)

                def output_low(b, g):
                    dve.wait_ge(oTh_ready, b.count(NG, g + 1))
                    dve.tensor_tensor(oTl[:, b.par, g, :], o32[:, :], oTh[:, b.par, g, :].bitcast(F32), ALU.subtract)\
                       .then_inc(oTl_ready, 1)

                def residual(b, t):
                    dve.wait_ge(proj_ready, b.count(TB, t + 1))
                    dve.wait_ge(res_loaded[t], b.count(16, 16))
                    wait(dve, stored[t], b.count(16, 0))
                    dve.tensor_tensor(y[:, t, :], psF[:, :], xres[:, t, :], ALU.add).then_inc(y_ready, 1)

                for t in range(TB):
                    weights.take_rest(dve, 2 * t, 2 * (t + 1))
                    root_mean_square(At(0, 0), t)
                    normalise(At(0, 0), t)
                weights.take_rest(dve, 2 * TB, weights.all)

                def body(b):
                    for s in range(H1):
                        group_stage(b, s, OUT_SPLIT, output_low)
                        group_stage(b, s, OUT, group_output)
                        stage(b, s, SPLIT, probs_low)
                        pieces(b + 1, s, low_h, HT_EARLY)
                        stage(b, s, SCORES, score_max)
                        group_stage(b, s, PT, denominators)
                        if b.live() and s % 4 == 2:
                            take_qT(b, s // G)
                        pieces(b + 1, s, by_angles, ANGLES_LATE)
                        if not (b + 2).first():
                            pieces(b + 2, s, root_mean_square, LN_AT)
                            pieces(b + 2, s, normalise, XN_AT)
                        pieces(b + 1, s, low_h, HT_LATE)
                        pieces(b + 1, s, values_low, V_LATE)
                        pieces(b - 1, s, residual, PROJ_LATE)

                over_batches(dve, body)


def mlp_l1(nc, io, scratch):
    with ExitStack() as ctx:
        def sb(name, shape, dt=F32):
            return ctx.enter_context(nc.sbuf_tensor(f"m1_{name}", shape, dt))

        def pb(name, shape):
            return ctx.enter_context(nc.psum_tensor(f"m1_{name}", shape, F32))

        sem = ctx.enter_context(semaphores(nc, "m1"))

        NH = HID // 2
        NJ = NH // P
        TT = 2 * TB
        T = TT * P
        NB = B // 2
        NV = 2 * NB
        DOWN = 2
        wg = [sb(f"wg{i}", [P, CC * NH], F32R) for i in range(2)]
        wu = [sb(f"wu{i}", [P, CC * NH], F32R) for i in range(2)]
        wd = [sb(f"wd{i}", [P, NJ * C], F32R) for i in range(2)]
        WG = [w[:, :].rearrange("p (k n) -> p k n", k=CC) for w in wg]
        WU = [w[:, :].rearrange("p (k n) -> p k n", k=CC) for w in wu]
        WD = [w[:, :].rearrange("p (k n) -> p k n", k=NJ) for w in wd]

        xin = sb("xin", [P, TT, C])
        xres = sb("xres", [P, TT, C])
        y = sb("y", [P, TT, C])
        mod = sb("mod", [P, 2, 2, CC])
        ident = sb("ident", [P, P])
        minus_half = sb("minus_half", [P, 1])
        xn = sb("xn", [P, TT, C])
        h32 = sb("h32", [P, 2, T])
        hh = sb("hh", [P, 2, CC, T], F32R)
        hl = sb("hl", [P, 2, CC, T], F32R)
        gate = sb("gate", [P, 2, T])
        u32 = sb("u32", [P, 2, T])
        uh = sb("uh", [P, 4, T], F32R)
        ul = sb("ul", [P, 4, T], F32R)
        spacer = sb("spacer", [P, 1])
        stats, mv, square = sb("stats", [P, 6]), sb("mv", [P, 2]), sb("square", [P, 1])
        var, rstd = sb("var", [P, 1]), sb("rstd", [P, 1])

        psT = [pb(f"psT{i}", [P, T]) for i in range(2)]
        psG, psU = pb("psG", [P, T]), pb("psU", [P, T])
        psD = [pb(f"psD{i}", [P, C]) for i in range(TT)]

        consts_loaded, const_ready = sem("consts_loaded"), sem("const_ready")
        x_loaded = [sem(f"x_loaded{i}") for i in range(TT)]
        res_loaded = [sem(f"res_loaded{i}") for i in range(TT)]
        stored = [sem(f"stored{i}") for i in range(TT)]
        mod_loaded = [sem(f"mod_loaded{i}") for i in range(2)]
        stats_ready, mean_ready, square_ready, var_ready = sem("stats"), sem("mean"), sem("square"), sem("var")
        rstd_ready, xn_ready = sem("rstd"), sem("xn")
        hT_ready, h32_ready, hh_ready, hl_ready = sem("hT"), sem("h32"), sem("hh"), sem("hl")
        g_ready, gate_ready, up_ready, u32_ready = sem("g"), sem("gate"), sem("up"), sem("u32")
        uh_ready, ul_ready, down_ready, y_ready = sem("uh"), sem("ul"), sem("down"), sem("y")

        flat = [sb("stage", [P, 4 * 1024]), y[:, :, :].rearrange("p t c -> p (t c)")]
        slots = [tile[:, c:c + 1024] for tile in flat for c in range(0, tile.shape[1], 1024)]
        weights, weights2 = [SplitWeights(sem, [(io[f"WgT{half}"], wg[0], wg[1]), (io[f"WuT{half}"], wu[0], wu[1]),
                                                (io[f"WdT{half}"], wd[0], wd[1])], slots[0:6 - 2 * half], f"w{half}") for half in range(2)]

        LN_AT = {1: (0,), 2: (1,), 3: (2,), 4: (3,)}
        HT_AT = {6: (0, 1), 7: (2, 3)}
        OUT_AT = DOWN

        steady_half = [0]

        def half_of(b):
            return b.value() // NB if isinstance(b.half, int) else steady_half[0]

        def turns(b):
            return isinstance(b.half, int) and b.value() == NB

        def block_rows(b, t):
            return bass.ds(((b - NB * half_of(b)).value() * TT + t) * P, P)

        def over_both_halves(eng, body):
            for half in range(2):
                steady_half[0] = half
                start = half * NB
                for b in range(start - 2 if half == 0 else start, start + 2):
                    body(At(b // 2, b % 2))
                with eng.Fori(start // 2 + 1, start // 2 + NB // 2 - 1) as pair:
                    for par in range(2):
                        body(At(pair, par))
                for b in range(start + NB - 2, start + NB if half == 0 else start + NB + 1):
                    body(At(b // 2, b % 2))

        def pieces(b, s, fn, table):
            if s in table and b.live(NV):
                for t in table[s]:
                    fn(b, t)

        with nc.Block() as block:
            @block.sync
            def _(sp):
                sp.dma_start(ident[:, :], io["ident"]).then_inc(consts_loaded, 16)

                def load_front(b, t):
                    if t == 0:
                        wait(sp, h32_ready, (b - 2).count(CC, CC))
                        sp.dma_start(mod[:, b.par, :, :].rearrange("p b s -> p (b s)"),
                                     scratch["mod1"][1, :, bass.ds((b - NB * half_of(b)).value() * 2, 2), :].rearrange("p b s -> p (b s)"))\
                          .then_inc(mod_loaded[b.par], 16)
                    wait(sp, xn_ready, (b - 1).count(TT, t + 1))
                    sp.dma_start(xin[:, t, :], scratch["x3"][block_rows(b, t), :])\
                      .then_inc(x_loaded[t], 16)

                def load_residual(b, t):
                    wait(sp, y_ready, (b - 1).count(TT, t + 1))
                    if half_of(b) == 1:
                        sp.wait_ge(stored[t], (b - NB).count(16, 16))
                    src = scratch[("x3", "x3h")[half_of(b)]]
                    sp.dma_start(xres[:, t, :], src[block_rows(b, t), :]).then_inc(res_loaded[t], 16)

                def store(b, t):
                    sp.wait_ge(y_ready, b.count(TT, t + 1))
                    dst = scratch[("x3h", "x4")[half_of(b)]]
                    sp.dma_start(dst[block_rows(b, t), :], y[:, t, :]).then_inc(stored[t], 16)

                def body(b):
                    for piece, bb in ((load_residual, b - 1), (load_front, b + 1), (store, b - 1)):
                        if bb.live(NV):
                            for t in range(TT):
                                piece(bb, t)

                over_both_halves(sp, body)
                for t in range(TT):
                    sp.wait_ge(stored[t], 16 * NV)

            @block.gpsimd
            def _(pool):
                pool.memset(minus_half[:, :], -0.5).then_inc(const_ready, 1)
                pool.wait_ge(const_ready, 1)

                def root_mean_square(b, t):
                    pool.wait_ge(var_ready, b.count(TT, t + 1))
                    pool.tensor_tensor(rstd[:, :], var[:, :], minus_half[:, :], ALU.pow).then_inc(rstd_ready, 1)

                def body(b):
                    for s in range(NJ):
                        pieces(b + 1, s, root_mean_square, LN_AT)

                over_both_halves(pool, body)

            @block.scalar
            def _(act):
                def silu(b, j):
                    act.wait_ge(g_ready, b.count(NJ, j + 1))
                    wait(act, u32_ready, b.count(NJ, j - 1))
                    act.activation(gate[:, j % 2, :], psG[:, :], ACT.Silu).then_inc(gate_ready, 1)

                def high_u(b, j):
                    act.wait_ge(u32_ready, b.count(NJ, j + 1))
                    wait(act, down_ready, b.count(NJ, j - 3))
                    act.activation(uh[:, j % 4, :], u32[:, j % 2, :], ACT.Copy).then_inc(uh_ready, 1)

                def modulate(b, c):
                    if c == 0:
                        act.wait_ge(mod_loaded[b.par], b.half * 16 + 16)
                        wait(act, up_ready, (b - 2).count(NJ, NJ))
                    act.wait_ge(hT_ready, b.count(CC, c + 1))
                    wait(act, hl_ready, b.count(CC, c - 1))
                    for i in range(2):
                        ins = act.activation(h32[:, c % 2, i * L:(i + 1) * L], psT[c % 2][:, i * L:(i + 1) * L], ACT.Copy,
                                             scale=mod[:, b.par, i, c:c + 1])
                    ins.then_inc(h32_ready, 1)
                    act.wait_ge(h32_ready, b.count(CC, c + 1))
                    act.activation(hh[:, b.par, c, :], h32[:, c % 2, :], ACT.Copy).then_inc(hh_ready, 1)

                def body(b):
                    for s in range(NJ):
                        if not (b + 1).first():
                            pieces(b + 1, s, modulate, HT_AT)
                        if turns(b) and s == 0:
                            act.wait_ge(weights.low_ready, weights.all)
                            act.wait_ge(g_ready, b.count(NJ, 0))
                            weights2.load_and_round(act, 0, weights.ends[0])
                            act.wait_ge(up_ready, b.count(NJ, 0))
                            weights2.load_and_round(act, weights.ends[0], weights.ends[1])
                        if turns(b) and s == DOWN:
                            act.wait_ge(down_ready, b.count(NJ, 0))
                            weights2.load_and_round(act, weights.ends[1], weights.all)
                        if b.live(NV):
                            silu(b, s)
                            high_u(b, s)

                weights.load_and_round(act, 0, weights.ends[0])
                for c in range(CC):
                    modulate(At(0, 0), c)
                weights.load_and_round(act, weights.ends[0], weights.all)
                over_both_halves(act, body)

            @block.tensor
            def _(pe):
                pe.wait_ge(consts_loaded, 16)

                def transposes_h(b, c):
                    if c == 0:
                        pe.wait_ge(xn_ready, b.count(TT, TT))
                    wait(pe, h32_ready, b.count(CC, c - 1))
                    for t in range(TT):
                        last = pe.transpose(psT[c % 2][:, t * P:(t + 1) * P], xn[:, t, c * P:(c + 1) * P], ident[:, :])
                    last.then_inc(hT_ready, 1)

                def hidden(b, j, ps, weight, ready):
                    for k in range(CC):
                        last = split_products(pe, ps[:, :], [w[:, k, j * P:(j + 1) * P] for w in weight],
                                              (hh[:, b.par, k, :], hl[:, b.par, k, :]), k == 0, k == CC - 1)
                    last.then_inc(ready, 1)

                def gate_and_up(b, j):
                    if j == 0:
                        pe.wait_ge(hl_ready, b.count(CC, CC))
                        if b.first():
                            weights.wait_for(pe, 0)
                        if turns(b):
                            weights2.wait_for(pe, 0)
                    wait(pe, gate_ready, b.count(NJ, j))
                    hidden(b, j, psG, WG, g_ready)
                    if b.first() and j == 0:
                        weights.wait_for(pe, 1)
                    if turns(b) and j == 0:
                        weights2.wait_for(pe, 1)
                    wait(pe, u32_ready, b.count(NJ, j))
                    hidden(b, j, psU, WU, up_ready)

                def down(b, j):
                    if b.first() and j == 0:
                        weights.wait_for(pe, 2)
                    if turns(b) and j == 0:
                        weights2.wait_for(pe, 2)
                    pe.wait_ge(ul_ready, b.count(NJ, j + 1))
                    for t in range(TT):
                        if j == 0:
                            wait(pe, y_ready, (b - 1).count(TT, t + 1))
                        last = split_products(pe, psD[t][:, :], (uh[:, j % 4, t * P:(t + 1) * P], ul[:, j % 4, t * P:(t + 1) * P]),
                                              [w[:, j, :] for w in WD], j == 0, j == NJ - 1)
                    last.then_inc(down_ready, 1)

                def body(b):
                    for s in range(NJ):
                        pieces(b + 1, s, transposes_h, HT_AT)
                        if b.live(NV):
                            gate_and_up(b, s)
                        bb, j = (b, s - DOWN) if s >= DOWN else (b - 1, NJ + s - DOWN)
                        if bb.live(NV):
                            down(bb, j)

                over_both_halves(pe, body)

            @block.vector
            def _(dve):
                dve.wait_ge(const_ready, 1)

                def root_mean_square(b, t):
                    dve.wait_ge(x_loaded[t], b.count(16, 16))
                    x = xin[:, t, :]
                    dve.bn_stats(stats[:, :], x).then_inc(stats_ready, 1)
                    dve.wait_ge(stats_ready, b.count(TT, t + 1))
                    dve.memset(spacer[:, :], 0.0)
                    dve.bn_aggr(mv[:, :], stats[:, :]).then_inc(mean_ready, 1)
                    dve.wait_ge(mean_ready, b.count(TT, t + 1))
                    dve.tensor_tensor(square[:, :], mv[:, 0:1], mv[:, 0:1], ALU.mult).then_inc(square_ready, 1)
                    dve.wait_ge(square_ready, b.count(TT, t + 1))
                    dve.tensor_scalar(var[:, :], square[:, :], mv[:, 1:2], RMS_EPS, ALU.add, ALU.add).then_inc(var_ready, 1)
                    if t == 0:
                        wait(dve, hT_ready, (b - 1).count(CC, CC))
                    dve.wait_ge(rstd_ready, b.count(TT, t + 1))
                    dve.tensor_scalar(xn[:, t, :], x, rstd[:, 0:1], None, ALU.mult).then_inc(xn_ready, 1)

                def low_h(b, c):
                    dve.wait_ge(hh_ready, b.count(CC, c + 1))
                    dve.tensor_tensor(hl[:, b.par, c, :], h32[:, c % 2, :], hh[:, b.par, c, :].bitcast(F32), ALU.subtract)\
                       .then_inc(hl_ready, 1)

                def product(b, j):
                    dve.wait_ge(gate_ready, b.count(NJ, j + 1))
                    dve.wait_ge(up_ready, b.count(NJ, j + 1))
                    dve.tensor_tensor(u32[:, j % 2, :], psU[:, :], gate[:, j % 2, :], ALU.mult).then_inc(u32_ready, 1)
                    dve.wait_ge(uh_ready, b.count(NJ, j + 1))
                    dve.tensor_tensor(ul[:, j % 4, :], u32[:, j % 2, :], uh[:, j % 4, :].bitcast(F32), ALU.subtract).then_inc(ul_ready, 1)

                def residual(b, t):
                    dve.wait_ge(down_ready, b.count(NJ, NJ))
                    dve.wait_ge(res_loaded[t], b.count(16, 16))
                    wait(dve, stored[t], b.count(16, 0))
                    dve.tensor_tensor(y[:, t, :], psD[t][:, :], xres[:, t, :], ALU.add).then_inc(y_ready, 1)

                for t in range(TT):
                    root_mean_square(At(0, 0), t)
                    weights.take_rest(dve, 1 * t, 1 * (t + 1))
                weights.take_rest(dve, 1 * TT, weights.ends[0])
                for c in range(CC):
                    low_h(At(0, 0), c)
                weights.take_rest(dve, weights.ends[0], weights.all)

                def body(b):
                    for s in range(NJ):
                        if s == OUT_AT and (b - 1).live(NV):
                            for t in range(TT):
                                residual(b - 1, t)
                        if turns(b) and s == 0:
                            weights2.take_rest(dve, 0, weights.ends[1])
                        if turns(b) and s == DOWN:
                            weights2.take_rest(dve, weights.ends[1], weights.all)
                        if not (b + 1).first():
                            pieces(b + 1, s, low_h, HT_AT)
                        if b.live(NV):
                            product(b, s)
                        if not (b + 1).first():
                            pieces(b + 1, s, root_mean_square, LN_AT)

                over_both_halves(dve, body)


def two_layers(nc, io, x4):
    shapes = {"mod0": [2, P, B, 2 * CC], "mod1": [2, P, B, CC], "gamma": [B, 2 * C], "rope": [P, B * TB, D1],
              "x1": [B * L, C], "x2": [B * L, C], "x3": [B * L, C], "x3h": [B * L, C]}
    scratch = {n: nc.dram_tensor(n, shape, F32, kind="Internal").ap() for n, shape in shapes.items()}
    scratch["x4"] = x4
    modulation(nc, io, scratch)
    attention_l0(nc, io, scratch)
    mlp_l0(nc, io, scratch)
    attention_l1(nc, io, scratch)
    mlp_l1(nc, io, scratch)


def by_contraction(w):
    w = np.asarray(w)
    return np.ascontiguousarray(w.T.reshape(w.shape[1] // P, P, w.shape[0]).transpose(1, 0, 2))


def lay_out(a):
    flat = lambda w: by_contraction(w).reshape(P, -1)
    feat = lambda v: np.asarray(v).reshape(-1, P).T
    cont = np.ascontiguousarray
    NH = HID // 2
    halves = {f"W{n}T{i}": by_contraction(a[f"L1_cond_W{n}"])[:, :, i * NH:(i + 1) * NH].reshape(P, -1) for n in "gu" for i in range(2)}
    NK = NH // P
    halves |= {f"WdT{i}": by_contraction(a["L1_cond_Wd"])[:, i * NK:(i + 1) * NK].reshape(P, -1) for i in range(2)}
    return {k: cont(v) for k, v in {
        **halves,
        "x": np.asarray(a["x"]).reshape(B * L, C),
        "condT": flat(a["cond_2048"]),
        "lnwF": np.stack([feat(a["L1_cond_ln1_w"]), feat(a["L1_cond_ln2_w"])], 1),
        "posT": np.asarray(a["pos_BxS"]).reshape(B * TB, P).T,
        "freq": (1.0 / np.float32(10000.0) ** (np.arange(0, D1, 2, dtype=np.float32) / np.float32(D1))).astype(np.float32),
        "bada": np.asarray(a["L0_cond_bada"]),
        "tw1T": by_contraction(a["L1_cond_ln1_tw"]),
        "tw2T": by_contraction(a["L1_cond_ln2_tw"]),
        "WadaT": by_contraction(a["L0_cond_Wada"]),
        "WqkvT": flat(a["L0_cond_Wqkv"]),
        "WprojT": flat(a["L0_cond_Wproj"]),
        "Wfc1T": flat(a["L0_cond_Wfc1"]),
        "Wfc2T": flat(a["L0_cond_Wfc2"]),
        "Wqkv1T": flat(np.concatenate([np.asarray(a[f"L1_cond_W{n}"]) for n in "qkv"])),
        "WoT": flat(a["L1_cond_Wo"]),
        "bfc1F": feat(a["L0_cond_bfc1"]),
        "bfc2": np.asarray(a["L0_cond_bfc2"]),
        "mask": np.asarray(a["mask_1x1xSxS_ff0"]).reshape(TB, P, L).transpose(1, 0, 2),
        "q_bias": np.asarray(a["L0_cond_q_bias"]),
        "v_bias": np.asarray(a["L0_cond_v_bias"]),
        "bproj": np.asarray(a["L0_cond_bproj"]),
        "scale_mul_log": np.asarray(a["L0_cond_scale_mul_log"]).reshape(H0),
        "ident": np.eye(P, dtype=np.float32),
    }.items()}


def kernel(**inputs):
    import concourse.bacc as bacc
    from concourse.bass_utils import run_bass_kernel_spmd

    arrays = lay_out(inputs)
    nc = bacc.Bacc("TRN2", target_bir_lowering=False, num_devices=1)
    io = {n: nc.dram_tensor(n, a.shape, mybir.dt.from_np(a.dtype), kind="ExternalInput").ap() for n, a in arrays.items()}
    x4 = nc.dram_tensor("x4", (B * L, C), F32, kind="ExternalOutput").ap()
    two_layers(nc, io, x4)
    r = run_bass_kernel_spmd(nc, [arrays], core_ids=[0])
    return r.results[0]["x4"].reshape(B, L, C)
```
